# Optimizing a Trainium2 kernel written in Bass

```python
import numpy as np
import jax
import jax.numpy as jnp

def _softmax(x, axis=-1):
    return jax.nn.softmax(x, axis=axis)

def _gelu(x):
    return jax.nn.gelu(x, approximate=True)

def _silu(x):
    return jax.nn.silu(x)

def _sigmoid(x):
    return jax.nn.sigmoid(x)

def _layernorm(x, axis=-1, eps=1e-05):
    m = jnp.mean(x, axis=axis, keepdims=True)
    v = jnp.var(x, axis=axis, keepdims=True)
    return (x - m) / jnp.sqrt(v + eps)

def _scatter_add(tgt, idx, src, axis=0):
    return tgt.at[idx].add(src)

def _segment_sum(src, seg, n):
    return jax.ops.segment_sum(src, seg, n)
kernel_name = 'mk_gnn_ffn_d2_gnn_r8_d16b89'

def setup_inputs(seed: int=0):
    np.random.seed(seed)
    _w = jnp.asarray

    def _rec_inputs():
        import jax
        import jax.numpy as jnp
        _gk = jax.random.key(seed)
        x = -0.0002928 + 1 * jax.random.normal(jax.random.fold_in(_gk, 1), (6250, 256), jnp.float32)
        src = jax.random.randint(jax.random.fold_in(_gk, 2), (100000,), 0, 6250, jnp.int32)
        dst = jax.random.randint(jax.random.fold_in(_gk, 3), (100000,), 0, 6250, jnp.int32)
        _o = jnp.argsort(dst, stable=True)
        src = src[_o]
        dst = dst[_o]
        edge_attr_256 = 0.000150688 + 1.00006 * jax.random.normal(jax.random.fold_in(_gk, 12), (100000, 256), jnp.float32)
        edge_attr_64 = jax.random.uniform(jax.random.fold_in(_gk, 13), (100000, 64), jnp.float32, 0.0, 1)
        return (x, src, dst, edge_attr_256, edge_attr_64)
    x, src, dst, edge_attr_256, edge_attr_64 = _rec_inputs()

    def _L0_gnn_setup():
        import jax, jax.numpy as jnp
        import numpy as np
        N_NODES = 2048
        N_EDGES = 32768
        D = 256
        key = jax.random.key(seed)
        ks = jax.random.split(key, 7)
        h = jax.random.normal(ks[0], (N_NODES, D), dtype=jnp.float32)
        edge_src = jax.random.randint(ks[1], (N_EDGES,), 0, N_NODES, dtype=jnp.int32)
        edge_dst = jax.random.randint(ks[2], (N_EDGES,), 0, N_NODES, dtype=jnp.int32)
        edge_w = jax.random.normal(ks[3], (N_EDGES, D), dtype=jnp.float32)
        W_self = jax.random.normal(ks[4], (D, D), dtype=jnp.float32) * (2.0 / D) ** 0.5
        W_func = jax.random.normal(ks[5], (D, D), dtype=jnp.float32) * (2.0 / D) ** 0.5
        W_att = jax.random.normal(ks[6], (2 * D + D, 1), dtype=jnp.float32) * 0.05
        return {'h': h, 'edge_src': edge_src, 'edge_dst': edge_dst, 'edge_w': edge_w, 'W_self': W_self, 'W_func': W_func, 'W_att': W_att}
    _L0_gnn_all = _L0_gnn_setup()
    _L0_gnn_in = {k: v for k, v in _L0_gnn_all.items() if k in ('W_self', 'W_func', 'W_att')}
    del _L0_gnn_all

    def _L0_ffn_setup():
        import jax, jax.numpy as jnp
        import numpy as np
        B, S, D = (8, 512, 256)
        H = 4 * D
        CAPACITY = 0.5
        key = jax.random.key(seed)
        ks = jax.random.split(key, 6)
        x = jax.random.normal(ks[0], (B, S, D), dtype=jnp.float32)
        attention_mask = jnp.zeros((B, 1, 1, S), dtype=jnp.float32)
        wr = jax.random.normal(ks[1], (D, 1), dtype=jnp.float32) * 0.02
        br = jnp.zeros((1,), dtype=jnp.float32)
        w1 = jax.random.normal(ks[2], (D, H), dtype=jnp.float32) * 0.02
        b1 = jnp.zeros((H,), dtype=jnp.float32)
        w2 = jax.random.normal(ks[3], (H, D), dtype=jnp.float32) * 0.02
        b2 = jnp.zeros((D,), dtype=jnp.float32)
        return {'x': x, 'attention_mask': attention_mask, 'wr': wr, 'br': br, 'w1': w1, 'b1': b1, 'w2': w2, 'b2': b2}
    _L0_ffn_all = _L0_ffn_setup()
    _L0_ffn_in = {k: v for k, v in _L0_ffn_all.items() if k in ('attention_mask', 'wr', 'br', 'w1', 'b1', 'w2', 'b2')}
    del _L0_ffn_all

    def _L1_gnn_setup():
        import jax, jax.numpy as jnp
        import numpy as np
        N = 12500
        E = 200000
        D_NODE = 256
        D_MSG = 128
        D_RAD = 64
        HEADS = 4
        OUTC = D_MSG // HEADS

        def _w(key, shape):
            fan_in = shape[-1]
            return jax.random.normal(key, shape, dtype=jnp.float32) / jnp.sqrt(jnp.float32(fan_in))
        key = jax.random.key(seed)
        ks = jax.random.split(key, 16)
        x = jax.random.normal(ks[0], (N, D_NODE), dtype=jnp.float32)
        edge_attr = jax.random.uniform(ks[1], (E, D_RAD), dtype=jnp.float32)
        edge_index = jax.random.randint(ks[2], (2, E), 0, N, dtype=jnp.int64)
        return {'x': x, 'edge_attr': edge_attr, 'edge_index': edge_index, 'W_edge': _w(ks[3], (D_RAD, D_RAD)), 'W_n2m': _w(ks[4], (D_MSG, D_NODE)), 'Wq': _w(ks[5], (D_MSG, D_MSG)), 'bq': jnp.zeros((D_MSG,), jnp.float32), 'Wk': _w(ks[6], (D_MSG, D_MSG)), 'bk': jnp.zeros((D_MSG,), jnp.float32), 'Wv': _w(ks[7], (D_MSG, D_MSG)), 'bv': jnp.zeros((D_MSG,), jnp.float32), 'We': _w(ks[8], (D_MSG, D_RAD)), 'Wskip': _w(ks[9], (D_MSG, D_MSG)), 'bskip': jnp.zeros((D_MSG,), jnp.float32), 'Wbeta': _w(ks[10], (1, 3 * D_MSG)), 'W_m2n': _w(ks[11], (D_NODE, D_MSG))}
    _L1_gnn_all = _L1_gnn_setup()
    _L1_gnn_in = {k: v for k, v in _L1_gnn_all.items() if k in ('W_edge', 'W_n2m', 'Wq', 'bq', 'Wk', 'bk', 'Wv', 'bv', 'We', 'Wskip', 'bskip', 'Wbeta', 'W_m2n')}
    del _L1_gnn_all

    def _L1_ffn_setup():
        import jax, jax.numpy as jnp
        import numpy as np
        B, N, D = (16, 512, 256)
        NUM_EXPERTS, TOP_K, HEADS = (4, 2, 4)
        N_EDGES = 131072
        LN_EPS = 1e-05

        def _layernorm(x, g, b):
            mu = x.mean(-1, keepdims=True)
            var = ((x - mu) ** 2).mean(-1, keepdims=True)
            return (x - mu) * jax.lax.rsqrt(var + LN_EPS) * g + b

        def _forward(x, edge_index, W_gat, att_src, att_dst, b_gat, ln_gamma, ln_beta, W1, b1, W2, b2):
            Bc, Nc, Dc = x.shape
            M = Bc * Nc
            x_flat = x.reshape(M, Dc)
            h = (x_flat @ W_gat).reshape(M, HEADS, NUM_EXPERTS)
            loops = jnp.arange(M, dtype=edge_index.dtype)
            src = jnp.concatenate([edge_index[0], loops])
            dst = jnp.concatenate([edge_index[1], loops])
            a_src = (h * att_src).sum(-1)
            a_dst = (h * att_dst).sum(-1)
            e = jax.nn.leaky_relu(a_src[src] + a_dst[dst], negative_slope=0.2)
            e_max = jax.ops.segment_max(e, dst, num_segments=M)
            ee = jnp.exp(e - e_max[dst])
            denom = jax.ops.segment_sum(ee, dst, num_segments=M)
            alpha = ee / (denom[dst] + 1e-16)
            msg = h[src] * alpha[:, :, None]
            agg = jax.ops.segment_sum(msg, dst, num_segments=M).reshape(M, HEADS * NUM_EXPERTS) + b_gat
            scores = _layernorm(agg, ln_gamma, ln_beta).reshape(M, HEADS, NUM_EXPERTS).mean(1)
            scores = scores.reshape(Bc, Nc, NUM_EXPERTS)
            topk_s, topk_i = jax.lax.top_k(scores, TOP_K)
            w = jax.nn.softmax(topk_s, axis=-1)
            out = jnp.zeros_like(x)
            for ei in range(NUM_EXPERTS):
                g = jnp.where(topk_i == ei, w, 0.0).sum(-1)
                hh = jax.nn.gelu(x @ W1[ei] + b1[ei], approximate=False)
                out = out + g[..., None] * (hh @ W2[ei] + b2[ei])
            return out
        key = jax.random.key(seed)
        ks = jax.random.split(key, 8)
        s = 0.05
        return {'x': jax.random.normal(ks[0], (B, N, D), jnp.float32), 'W_gat': jax.random.normal(ks[1], (D, HEADS * NUM_EXPERTS), jnp.float32) * s, 'att_src': jax.random.normal(ks[2], (HEADS, NUM_EXPERTS), jnp.float32) * s, 'att_dst': jax.random.normal(ks[3], (HEADS, NUM_EXPERTS), jnp.float32) * s, 'b_gat': jnp.zeros((HEADS * NUM_EXPERTS,), jnp.float32), 'ln_gamma': jnp.ones((HEADS * NUM_EXPERTS,), jnp.float32), 'ln_beta': jnp.zeros((HEADS * NUM_EXPERTS,), jnp.float32), 'W1': jax.random.normal(ks[4], (NUM_EXPERTS, D, 2 * D), jnp.float32) * s, 'b1': jnp.zeros((NUM_EXPERTS, 2 * D), jnp.float32), 'W2': jax.random.normal(ks[5], (NUM_EXPERTS, 2 * D, D), jnp.float32) * s, 'b2': jnp.zeros((NUM_EXPERTS, D), jnp.float32), 'edge_index': jax.random.randint(ks[6], (2, N_EDGES), 0, B * N, jnp.int32)}
    _L1_ffn_all = _L1_ffn_setup()
    _L1_ffn_in = {k: v for k, v in _L1_ffn_all.items() if k in ('W_gat', 'att_src', 'att_dst', 'b_gat', 'ln_gamma', 'ln_beta', 'W1', 'b1', 'W2', 'b2', 'edge_index')}
    del _L1_ffn_all
    return {'x': x, 'src': src, 'dst': dst, 'edge_attr_256': edge_attr_256, 'edge_attr_64': edge_attr_64, 'L0_gnn_W_self': _L0_gnn_in['W_self'], 'L0_gnn_W_func': _L0_gnn_in['W_func'], 'L0_gnn_W_att': _L0_gnn_in['W_att'], 'L0_ffn_attention_mask': _L0_ffn_in['attention_mask'], 'L0_ffn_wr': _L0_ffn_in['wr'], 'L0_ffn_br': _L0_ffn_in['br'], 'L0_ffn_w1': _L0_ffn_in['w1'], 'L0_ffn_b1': _L0_ffn_in['b1'], 'L0_ffn_w2': _L0_ffn_in['w2'], 'L0_ffn_b2': _L0_ffn_in['b2'], 'L1_gnn_W_edge': _L1_gnn_in['W_edge'], 'L1_gnn_W_n2m': _L1_gnn_in['W_n2m'], 'L1_gnn_Wq': _L1_gnn_in['Wq'], 'L1_gnn_bq': _L1_gnn_in['bq'], 'L1_gnn_Wk': _L1_gnn_in['Wk'], 'L1_gnn_bk': _L1_gnn_in['bk'], 'L1_gnn_Wv': _L1_gnn_in['Wv'], 'L1_gnn_bv': _L1_gnn_in['bv'], 'L1_gnn_We': _L1_gnn_in['We'], 'L1_gnn_Wskip': _L1_gnn_in['Wskip'], 'L1_gnn_bskip': _L1_gnn_in['bskip'], 'L1_gnn_Wbeta': _L1_gnn_in['Wbeta'], 'L1_gnn_W_m2n': _L1_gnn_in['W_m2n'], 'L1_ffn_W_gat': _L1_ffn_in['W_gat'], 'L1_ffn_att_src': _L1_ffn_in['att_src'], 'L1_ffn_att_dst': _L1_ffn_in['att_dst'], 'L1_ffn_b_gat': _L1_ffn_in['b_gat'], 'L1_ffn_ln_gamma': _L1_ffn_in['ln_gamma'], 'L1_ffn_ln_beta': _L1_ffn_in['ln_beta'], 'L1_ffn_W1': _L1_ffn_in['W1'], 'L1_ffn_b1': _L1_ffn_in['b1'], 'L1_ffn_W2': _L1_ffn_in['W2'], 'L1_ffn_b2': _L1_ffn_in['b2'], 'L1_ffn_edge_index': _L1_ffn_in['edge_index']}

def reference(x, src, dst, edge_attr_256, edge_attr_64, L0_gnn_W_self, L0_gnn_W_func, L0_gnn_W_att, L0_ffn_attention_mask, L0_ffn_wr, L0_ffn_br, L0_ffn_w1, L0_ffn_b1, L0_ffn_w2, L0_ffn_b2, L1_gnn_W_edge, L1_gnn_W_n2m, L1_gnn_Wq, L1_gnn_bq, L1_gnn_Wk, L1_gnn_bk, L1_gnn_Wv, L1_gnn_bv, L1_gnn_We, L1_gnn_Wskip, L1_gnn_bskip, L1_gnn_Wbeta, L1_gnn_W_m2n, L1_ffn_W_gat, L1_ffn_att_src, L1_ffn_att_dst, L1_ffn_b_gat, L1_ffn_ln_gamma, L1_ffn_ln_beta, L1_ffn_W1, L1_ffn_b1, L1_ffn_W2, L1_ffn_b2, L1_ffn_edge_index):
    import jax
    import jax.numpy as jnp

    def _L0_gnn_ref(h, edge_src, edge_dst, edge_w, W_self, W_func, W_att):
        import jax, jax.numpy as jnp
        import numpy as np
        N_NODES = 2048
        N_EDGES = 32768
        D = 256
        'My_GATLayer forward (att_ew=True, relu=True, res_connection=True, no dropout).'
        N, d = h.shape
        h_s = h @ W_self
        z = h @ W_func
        w_src, w_dst, w_ew = (W_att[:d], W_att[d:2 * d], W_att[2 * d:])
        e = (z @ w_src)[edge_src] + (z @ w_dst)[edge_dst] + edge_w @ w_ew
        e = jax.nn.leaky_relu(e, negative_slope=0.01)
        m = jax.ops.segment_max(e, edge_dst, num_segments=N)
        m = jnp.where(jnp.isfinite(m), m, 0.0)
        ex = jnp.exp(e - m[edge_dst])
        den = jax.ops.segment_sum(ex, edge_dst, num_segments=N)
        alpha = ex / den[edge_dst]
        agg = jax.ops.segment_sum(alpha * z[edge_src], edge_dst, num_segments=N)
        deg = jax.ops.segment_sum(jnp.ones((e.shape[0], 1), e.dtype), edge_dst, num_segments=N)
        h_new = jnp.where(deg > 0, h_s + agg, h)
        h_new = jax.nn.relu(h_new)
        return h + h_new

    def _L0_ffn_ref(x, attention_mask, wr, br, w1, b1, w2, b2):
        import jax, jax.numpy as jnp
        import numpy as np
        B, S, D = (8, 512, 256)
        H = 4 * D
        CAPACITY = 0.5
        b, s, d = x.shape
        weights = (jnp.einsum('bsd,do->bso', x, wr) + br)[..., 0]
        k = max(1, int(CAPACITY * s))
        kk = k - 1 if k > 1 else 1
        _, idx = jax.lax.top_k(weights, k)
        sel_idx = idx[:, :kk]
        sel = jnp.take_along_axis(x, sel_idx[:, :, None], axis=1)
        h = jax.nn.gelu(jnp.einsum('bkd,dh->bkh', sel, w1) + b1)
        y = jnp.einsum('bkh,hd->bkd', h, w2) + b2
        w_sel = jnp.take_along_axis(weights, sel_idx, axis=1)
        y = y * w_sel[..., None]
        batch_idx = jnp.arange(b)[:, None]
        processed = jnp.zeros_like(x).at[batch_idx, sel_idx].set(y)
        return processed + x

    def _L1_gnn_ref(x, edge_attr, edge_index, W_edge, W_n2m, Wq, bq, Wk, bk, Wv, bv, We, Wskip, bskip, Wbeta, W_m2n):
        import jax, jax.numpy as jnp
        import numpy as np
        N = 12500
        E = 200000
        D_NODE = 256
        D_MSG = 128
        D_RAD = 64
        HEADS = 4
        OUTC = D_MSG // HEADS

        def _w(key, shape):
            fan_in = shape[-1]
            return jax.random.normal(key, shape, dtype=jnp.float32) / jnp.sqrt(jnp.float32(fan_in))
        src = edge_index[0]
        dst = edge_index[1]
        n = x.shape[0]
        scale = 1.0 / jnp.sqrt(jnp.float32(OUTC))
        ee = edge_attr @ W_edge.T
        m = x @ W_n2m.T
        q = (m @ Wq.T + bq).reshape(n, HEADS, OUTC)
        k = (m @ Wk.T + bk).reshape(n, HEADS, OUTC)
        v = (m @ Wv.T + bv).reshape(n, HEADS, OUTC)
        e = (ee @ We.T).reshape(-1, HEADS, OUTC)
        kj = k[src] + e
        alpha = jnp.einsum('ehc,ehc->eh', q[dst], kj) * scale
        amax = jax.ops.segment_max(alpha, dst, num_segments=n)
        expa = jnp.exp(alpha - amax[dst])
        asum = jax.ops.segment_sum(expa, dst, num_segments=n)
        alpha = expa / (asum[dst] + 1e-16)
        msg = (v[src] + e) * alpha[..., None]
        out = jax.ops.segment_sum(msg, dst, num_segments=n)
        out = out.reshape(n, D_MSG)
        x_r = m @ Wskip.T + bskip
        beta = jax.nn.sigmoid(jnp.concatenate([out, x_r, out - x_r], axis=-1) @ Wbeta.T)
        out = beta * x_r + (1.0 - beta) * out
        return out @ W_m2n.T

    def _L1_ffn_ref(x, W_gat, att_src, att_dst, b_gat, ln_gamma, ln_beta, W1, b1, W2, b2, edge_index):
        import jax, jax.numpy as jnp
        import numpy as np
        B, N, D = (16, 512, 256)
        NUM_EXPERTS, TOP_K, HEADS = (4, 2, 4)
        N_EDGES = 131072
        LN_EPS = 1e-05

        def _layernorm(x, g, b):
            mu = x.mean(-1, keepdims=True)
            var = ((x - mu) ** 2).mean(-1, keepdims=True)
            return (x - mu) * jax.lax.rsqrt(var + LN_EPS) * g + b

        def _forward(x, edge_index, W_gat, att_src, att_dst, b_gat, ln_gamma, ln_beta, W1, b1, W2, b2):
            Bc, Nc, Dc = x.shape
            M = Bc * Nc
            x_flat = x.reshape(M, Dc)
            h = (x_flat @ W_gat).reshape(M, HEADS, NUM_EXPERTS)
            loops = jnp.arange(M, dtype=edge_index.dtype)
            src = jnp.concatenate([edge_index[0], loops])
            dst = jnp.concatenate([edge_index[1], loops])
            a_src = (h * att_src).sum(-1)
            a_dst = (h * att_dst).sum(-1)
            e = jax.nn.leaky_relu(a_src[src] + a_dst[dst], negative_slope=0.2)
            e_max = jax.ops.segment_max(e, dst, num_segments=M)
            ee = jnp.exp(e - e_max[dst])
            denom = jax.ops.segment_sum(ee, dst, num_segments=M)
            alpha = ee / (denom[dst] + 1e-16)
            msg = h[src] * alpha[:, :, None]
            agg = jax.ops.segment_sum(msg, dst, num_segments=M).reshape(M, HEADS * NUM_EXPERTS) + b_gat
            scores = _layernorm(agg, ln_gamma, ln_beta).reshape(M, HEADS, NUM_EXPERTS).mean(1)
            scores = scores.reshape(Bc, Nc, NUM_EXPERTS)
            topk_s, topk_i = jax.lax.top_k(scores, TOP_K)
            w = jax.nn.softmax(topk_s, axis=-1)
            out = jnp.zeros_like(x)
            for ei in range(NUM_EXPERTS):
                g = jnp.where(topk_i == ei, w, 0.0).sum(-1)
                hh = jax.nn.gelu(x @ W1[ei] + b1[ei], approximate=False)
                out = out + g[..., None] * (hh @ W2[ei] + b2[ei])
            return out
        return _forward(x, edge_index, W_gat, att_src, att_dst, b_gat, ln_gamma, ln_beta, W1, b1, W2, b2)
    edge_index = jnp.stack([src, dst])
    x = x + _L0_gnn_ref(_layernorm(x, axis=-1), src, dst, edge_attr_256, L0_gnn_W_self, L0_gnn_W_func, L0_gnn_W_att)
    x = x + _L0_ffn_ref(_layernorm(x, axis=-1)[None], L0_ffn_attention_mask, L0_ffn_wr, L0_ffn_br, L0_ffn_w1, L0_ffn_b1, L0_ffn_w2, L0_ffn_b2)[0]
    x = x + _L1_gnn_ref(_layernorm(x, axis=-1), edge_attr_64, edge_index, L1_gnn_W_edge, L1_gnn_W_n2m, L1_gnn_Wq, L1_gnn_bq, L1_gnn_Wk, L1_gnn_bk, L1_gnn_Wv, L1_gnn_bv, L1_gnn_We, L1_gnn_Wskip, L1_gnn_bskip, L1_gnn_Wbeta, L1_gnn_W_m2n)
    x = x + _L1_ffn_ref(_layernorm(x, axis=-1)[None], L1_ffn_W_gat, L1_ffn_att_src, L1_ffn_att_dst, L1_ffn_b_gat, L1_ffn_ln_gamma, L1_ffn_ln_beta, L1_ffn_W1, L1_ffn_b1, L1_ffn_W2, L1_ffn_b2, L1_ffn_edge_index)[0]
    return x

_drawn_inputs = setup_inputs


def setup_inputs(seed=0):
    import zlib

    import numpy as np

    out = dict(_drawn_inputs(seed))
    spreads = {'L0_ffn_b1': (0.0, 0.8),
     'L0_ffn_b2': (0.0, 0.8),
     'L1_gnn_bq': (0.0, 2.0),
     'L1_gnn_bk': (0.0, 2.0),
     'L1_gnn_bv': (0.0, 2.0),
     'L1_gnn_bskip': (0.0, 1.111),
     'L1_ffn_b_gat': (0.0, 0.437),
     'L1_ffn_ln_gamma': (1.0, 0.6),
     'L1_ffn_ln_beta': (0.0, 2.0),
     'L1_ffn_b1': (0.0, 1.186),
     'L1_ffn_b2': (0.0, 0.929)}
    factors = {'L0_ffn_wr': 5.74,
     'L0_ffn_w1': 6.714,
     'L0_ffn_w2': 6.127,
     'L1_ffn_att_src': 12.293,
     'L1_ffn_att_dst': 200.0,
     'edge_attr_64': 5.994,
     'L1_gnn_Wq': 3.016}
    for name, (base, spread) in spreads.items():
        noise = np.random.default_rng([zlib.crc32(name.encode()), seed]).standard_normal(out[name].shape)
        drawn = base * np.exp(spread * noise) if base else spread * noise
        out[name] = jnp.asarray(drawn.astype(out[name].dtype))
    for name, factor in factors.items():
        out[name] = (out[name] * factor).astype(out[name].dtype)
    return out
```

```python
from contextlib import ExitStack

import numpy as np

import concourse.bass as bass
from concourse import mybir

ALU = mybir.AluOpType
ACT = mybir.ActivationFunctionType
AX = mybir.AxisListType
F32 = mybir.dt.float32
I32 = mybir.dt.int32
U32 = mybir.dt.uint32

P = 128
N = 6250
D = 256
NB = 50
NP = NB * P
E = 100000
C = 782
BC = 17
E2 = 131072
C2 = E2 // P
BIG = 1e30
EPS = 1e-5


class Links:

    def __init__(self, eng, sem):
        self.eng, self.sem, self.n, self.turns = eng, sem, 0, 0

    def mark(self, ins):
        ins.then_inc(self.sem, 1)
        self.n += 1

    def settle(self):
        self.eng.wait_ge(self.sem, self.turns + self.n)

    def link(self, ins):
        self.mark(ins)
        self.settle()

    def enter(self, i, per):
        self.start, self.per, self.turns = self.n, per, i * per

    def leave(self, count):
        assert self.n - self.start == self.per, f"{self.n - self.start} links in the body"
        self.n, self.turns = self.start + self.per * count, 0


class Stage:

    used = []

    def __init__(self, nc, name):
        self.nc, self.name, self.stack = nc, name, ExitStack()

    def __enter__(self):
        return self

    def __exit__(self, *a):
        return self.stack.__exit__(*a)

    def sb(self, name, shape, dt=F32):
        return self.stack.enter_context(self.nc.sbuf_tensor(f"{self.name}_{name}", shape, dt))

    def ps(self, name, shape=(P, 512), dt=F32):
        return self.stack.enter_context(self.nc.psum_tensor(f"{self.name}_{name}", list(shape), dt))

    def sem(self, name):
        sem = self.nc.alloc_semaphore(f"{self.name}_{name}")
        Stage.used.append(sem)
        return sem

    def gather_sem(self, name):
        return self.nc.alloc_semaphore(f"{self.name}_{name}")

    def sems(self, name, n=2):
        return [self.sem(f"{name}{i}") for i in range(n)]

    def block(self):
        return self.nc.Block()


def recycle(nc):
    numbers = sorted(s.num for s in Stage.used)
    with nc.Block() as block:
        @block.gpsimd
        def _(pool):
            while numbers:
                n = 1
                while n < len(numbers) and numbers[n] == numbers[0] + n:
                    n += 1
                pool.sem_clear(range(numbers[0], numbers[0] + n))
                del numbers[:n]
    for s in Stage.used:
        nc.release_semaphore(s)
    Stage.used.clear()


def gate(eng, sem, value, passed):
    eng.wait_ge(sem, value)
    eng.sem_inc(passed, 1)


def flat(t, w):
    return t[:].rearrange("p a b -> p (a b)")


class G:
    pass


def load_nodes(nc, g):
    with Stage(nc, "ld") as s:
        dma, made, dve = s.sem("dma"), s.sem("made"), s.sem("dve")
        itmp = s.sb("itmp", [P, NB], I32)
        ktmp = s.sb("ktmp", [P, P], I32)
        dtmp = s.sb("dtmp", [P, C], I32)
        with s.block() as block:
            @block.sync
            def _(sp):
                sp.dma_start(g.x[:], g.in_x.rearrange("(b p) d -> p b d", p=P)).then_inc(dma, 16)
                sp.dma_start(g.src[:], g.in_src.bitcast(U32)).then_inc(dma, 16)
                sp.dma_start(dtmp[:], g.in_dst).then_inc(dma, 16)
                sp.wait_ge(dma, 48)

            @block.gpsimd
            def _(pool):
                pool.memset(g.ident[:], 0.0).then_inc(made, 1)
                pool.memset(g.ones[:], 1.0).then_inc(made, 1)
                pool.memset(g.below[:], 1.0).then_inc(made, 1)
                pool.iota(itmp[:], [[P, NB]], base=0, channel_multiplier=1).then_inc(made, 1)
                pool.iota(ktmp[:], [[1, P]], base=1, channel_multiplier=0).then_inc(made, 1)
                pool.wait_ge(made, 5)
                pool.affine_select(out=g.ident[:], in_=g.ident[:], compare_op=ALU.not_equal, fill=1.0,
                                   base=0, pattern=[[-1, P]], channel_multiplier=1).then_inc(made, 1)
                pool.affine_select(out=g.below[:], in_=g.below[:], compare_op=ALU.is_gt, fill=0.0,
                                   base=0, pattern=[[-1, P]], channel_multiplier=1).then_inc(made, 1)

            @block.vector
            def _(v):
                v.wait_ge(made, 7)
                v.tensor_copy(g.nodeid[:], itmp[:]).then_inc(dve, 1)
                v.tensor_copy(g.chunkno[:], ktmp[:]).then_inc(dve, 1)
                v.wait_ge(dma, 48)
                v.tensor_copy(g.dstf[:], dtmp[:]).then_inc(dve, 1)
                v.wait_ge(dve, 3)


def node_stats(nc, g, name):
    with Stage(nc, name) as s:
        six = s.sb("six", [P, NB * 6])
        t = s.sb("t", [P, 3, NB])
        dve, var_ready, std_ready = s.sem("dve"), s.sem("var_ready"), s.sem("std_ready")
        v6 = six[:].rearrange("p (b k) -> p k b", k=6)
        with s.block() as block:
            @block.vector
            def _(v):
                ln = Links(v, dve)
                with v.Fori(0, NB) as b:
                    ln.enter(b, 1)
                    ln.mark(v.bn_stats(six[:, bass.ds(b * 6, 6)], flat(g.x, D)[:, bass.ds(b * D, D)]))
                    ln.leave(NB)
                ln.settle()
                ln.mark(v.tensor_tensor(g.mean[:], v6[:, 1, :], v6[:, 4, :], ALU.add))
                ln.mark(v.tensor_tensor(t[:, 0, :], v6[:, 1, :], v6[:, 4, :], ALU.subtract))
                ln.link(v.tensor_tensor(t[:, 1, :], v6[:, 2, :], v6[:, 5, :], ALU.add))
                ln.mark(v.tensor_scalar(g.mean[:], g.mean[:], 0.5, None, ALU.mult))
                ln.mark(v.tensor_scalar(t[:, 1, :], t[:, 1, :], 1.0 / D, EPS, ALU.mult, ALU.add))
                ln.link(v.tensor_tensor(t[:, 0, :], t[:, 0, :], t[:, 0, :], ALU.mult))
                v.scalar_tensor_tensor(out=t[:, 2, :], in0=t[:, 0, :], scalar=0.25, in1=t[:, 1, :],
                                       op0=ALU.mult, op1=ALU.add).then_inc(var_ready, 1)
                v.wait_ge(std_ready, 1)
                ln.link(v.reciprocal(g.rstd[:], t[:, 2, :]))

            @block.scalar
            def _(act):
                act.wait_ge(var_ready, 1)
                act.activation(t[:, 2, :], t[:, 2, :], ACT.Sqrt).then_inc(std_ready, 1)


def project(nc, g, name, w, width, out_width, finish, per, tables=(), prepare=None, depth=2):
    table = tables or None
    half = NB // 2
    with Stage(nc, name) as s:
        xn = [s.sb(f"xn{h}", [P, D]) for h in range(2)]
        xt = [s.sb(f"xt{h}", [P, 2, P]) for h in range(2)]
        out = [s.sb(f"out{h}", [P, max(out_width, 1)]) for h in range(2)]
        pt = [s.ps(f"pt{h}") for h in range(2)]
        po = [s.ps(f"po{h}") for h in range(2)]
        normed, turned, copied, product, finished = (s.sems(x) for x in (
            "normed", "turned", "copied", "product", "finished"))
        stored = s.sems("stored")
        dve = s.sem("dve")
        with s.block() as block:
            @block.vector
            def _(v):
                ln = Links(v, dve)
                for h in range(2):
                    v.sem_inc(normed[h], 1)
                    v.sem_inc(finished[h], 1)
                with v.Fori(0, half) as i:
                    ln.enter(i, 2 * per)
                    for h in range(2):
                        b = i * 2 + h
                        rows = flat(g.x, D)[:, bass.ds(b * D, D)]
                        v.wait_ge(turned[h], i + 1)
                        if prepare is not None:
                            prepare(v, b, xn[h]).then_inc(normed[h], 1)
                            continue
                        v.tensor_scalar(xn[h][:], rows, g.mean[:, bass.ds(b, 1)], g.rstd[:, bass.ds(b, 1)],
                                        ALU.subtract, ALU.mult).then_inc(normed[h], 1)
                    for h in range(2):
                        b = i * 2 + h
                        rows = flat(g.x, D)[:, bass.ds(b * D, D)]
                        v.wait_ge(normed[h], i + 2)
                        v.wait_ge(product[h], i + 2)
                        if table is not None:
                            v.wait_ge(stored[h], (i + 1) * (16 * len(tables)))
                        finish(v, ln, h, b, rows, xn[h], po[h], out[h]).then_inc(finished[h], 1)
                    ln.leave(half)
                for h in range(2):
                    v.wait_ge(finished[h], half + 1)

            @block.tensor
            def _(pe):
                for h in range(2):
                    pe.sem_inc(turned[h], 1)
                    pe.sem_inc(product[h], 1)
                with pe.Fori(0, half) as i:
                    for h in range(2):
                        pe.wait_ge(normed[h], i + 2)
                        pe.wait_ge(copied[h], i + 1)
                        for k in range(depth):
                            ins = pe.transpose(pt[h][:, k * P:(k + 1) * P], xn[h][:, k * P:(k + 1) * P], g.ident[:])
                        ins.then_inc(turned[h], 1)
                    for h in range(2):
                        pe.wait_ge(copied[h], i + 2)
                        pe.wait_ge(finished[h], i + 1)
                        for k in range(depth):
                            ins = pe.matmul(po[h][:, 0:width], xt[h][:, k, :], w[:, k, :], start=(k == 0),
                                            stop=(k == depth - 1))
                        ins.then_inc(product[h], 1)

            @block.scalar
            def _(act):
                for h in range(2):
                    act.sem_inc(copied[h], 1)
                with act.Fori(0, half) as i:
                    for h in range(2):
                        act.wait_ge(turned[h], i + 2)
                        act.wait_ge(product[h], i + 1)
                        act.activation(flat(xt[h], P)[:, 0:depth * P], pt[h][:, 0:depth * P], ACT.Copy).then_inc(copied[h], 1)

            if table is not None:
                @block.sync
                def _(sp):
                    for h in range(2):
                        sp.sem_inc(stored[h], 16 * len(tables))
                    with sp.Fori(0, half) as i:
                        for h in range(2):
                            sp.wait_ge(finished[h], i + 2)
                            for to, c0, c1 in tables:
                                sp.dma_start(to[bass.ds((i * 2 + h) * P, P), :],
                                             out[h][:, c0:c1]).then_inc(stored[h], 16)
                    for h in range(2):
                        sp.wait_ge(stored[h], 16 * len(tables) * (half + 1))


def segments(nc, g, name, dstf, cols, edges, start, end, keys):
    groups = cols * P // P
    with Stage(nc, name) as s:
        firsts = s.sb("firsts", [1, groups])
        firstb = s.sb("firstb", [P, groups])
        c1 = s.sb("c1", [P, NB])
        gi = s.sb("gi", [P, NB], U32)
        rows = s.sb("rows", [P, NB, P])
        one = s.sb("one", [1, 1])
        pb = [s.ps(f"pb{h}") for h in range(2)]
        half = groups // 2
        put, got, made, bc, counted, wrote, dve = (s.sem(x) for x in (
            "put", "got", "made", "bc", "counted", "wrote", "dve"))
        gath = s.gather_sem("gath")
        counts = nc.dram_tensor(f"{name}_counts", (NP + 1, 1), F32, kind="Internal").ap()
        with s.block() as block:
            @block.sync
            def _(sp):
                sp.dma_start(keys.rearrange("(p c) -> p c", p=P), dstf[:]).then_inc(put, 16)
                sp.wait_ge(put, 16)
                with nc.allow_non_contiguous_dma("one key of every 128"):
                    sp.dma_start(firsts[:], keys.rearrange("(a g k) -> a g k", a=1, k=P)[:, :, 0]).then_inc(got, 16)
                    sp.wait_ge(counted, 1)
                    sp.dma_start(counts[0:NP, :].rearrange("(b p) o -> p (b o)", p=P), start[:]).then_inc(wrote, 16)
                    sp.dma_start(counts[NP:NP + 1, :], one[:]).then_inc(wrote, 16)
                    sp.wait_ge(wrote, 32)
                    sp.dma_start(end[:], counts[1:NP + 1, :].rearrange("(b p) o -> p (b o)", p=P)).then_inc(wrote, 16)
                    sp.wait_ge(wrote, 48)

            @block.tensor
            def _(pe):
                pe.wait_ge(got, 16)
                for h in range(2):
                    pe.matmul(pb[h][:, 0:half], g.ones[0:1, :], firsts[:, h * half:(h + 1) * half],
                              start=True, stop=True).then_inc(bc, 1)

            @block.vector
            def _(v):
                ln = Links(v, dve)
                ln.mark(v.memset(one[:], float(edges)))
                v.wait_ge(bc, 2)
                for h in range(2):
                    ln.mark(v.tensor_copy(firstb[:, h * half:(h + 1) * half], pb[h][:, 0:half]))
                ln.settle()
                for b in range(NB):
                    if b % 6 == 0:
                        ln.settle()
                    junk = flat(rows, P)[:, (b % 6) * groups:(b % 6 + 1) * groups]
                    ln.mark(v.tensor_scalar(junk, firstb[:], g.nodeid[:, b:b + 1], 0.0, ALU.is_lt, ALU.add,
                                            accum_out=c1[:, b:b + 1]))
                ln.settle()
                ln.link(v.tensor_scalar(c1[:], c1[:], -1.0, 0.0, ALU.add, ALU.max))
                v.tensor_copy(gi[:], c1[:]).then_inc(made, 1)
                v.wait_ge(gath, 16 * NB)
                ln.link(v.tensor_tensor(rows[:], rows[:], g.nodeid[:].rearrange("p (b o) -> p b o", o=1).to_broadcast([P, NB, P]),
                                        ALU.is_lt))
                ln.link(v.tensor_reduce(start[:], rows[:], AX.X, ALU.add))
                v.scalar_tensor_tensor(out=start[:], in0=c1[:], scalar=float(P), in1=start[:],
                                       op0=ALU.mult, op1=ALU.add).then_inc(counted, 1)

            @block.gpsimd
            def _(pool):
                pool.wait_ge(made, 1)
                for b in range(NB):
                    pool.indirect_dma_start(rows[:, b, :], None, keys.rearrange("(g k) -> g k", k=P),
                                            bass.IndirectOffsetOnAxis(ap=gi[:, b:b + 1], axis=0)).then_inc(gath, 16)
                pool.wait_ge(gath, 16 * NB)


def boundaries(nc, g, name, dstf, cols, reset, keep):
    with Stage(nc, name) as s:
        dve = s.sem("dve")
        with s.block() as block:
            @block.vector
            def _(v):
                ln = Links(v, dve)
                ln.mark(v.memset(keep[:, 0:1], 0.0))
                ln.mark(v.tensor_tensor(keep[:, 1:cols], dstf[:, 1:cols], dstf[:, 0:cols - 1], ALU.is_equal))
                ln.settle()
                ln.link(v.tensor_scalar(reset[:], keep[:], -1.0, BIG, ALU.add, ALU.mult))


def spread(nc, g, name, nodes, heads, dstf, cols, edges, start, end, keep, per_edge):
    with Stage(nc, name) as s:
        table = nc.dram_tensor(f"{name}_table", (NP, heads), F32, kind="Internal").ap()
        firsts = nc.dram_tensor(f"{name}_firsts", (P * cols, heads), F32, kind="Internal").ap()
        zero = s.sb("zero", [P, cols * heads])
        at = s.sb("at", [P, NB], F32)
        empty = s.sb("empty", [P, NB], F32)
        ai = s.sb("ai", [P, NB], U32)
        lane = s.sb("lane", [P, heads])
        li = s.sb("li", [P, 1], U32)
        lf = s.sb("lf", [P, 1], F32)
        zeroed, made, put, loaded, dve = (s.sem(x) for x in ("zeroed", "made", "put", "loaded", "dve"))
        scattered, lane_got = s.gather_sem("scattered"), s.gather_sem("lane_got")
        with s.block() as block:
            @block.vector
            def _(v):
                ln = Links(v, dve)
                v.memset(zero[:], 0.0).then_inc(zeroed, 1)
                ln.mark(v.tensor_tensor(empty[:], start[:], end[:], ALU.is_ge))
                ln.link(v.tensor_scalar(lf[:], dstf[:, 0:1], float(NP - 1), None, ALU.min))
                ln.link(v.scalar_tensor_tensor(out=at[:], in0=empty[:], scalar=float(1 << 20), in1=start[:],
                                               op0=ALU.mult, op1=ALU.add))
                v.tensor_copy(ai[:], at[:]).then_inc(made, 1)
                v.tensor_copy(li[:], lf[:]).then_inc(made, 1)
                v.wait_ge(loaded, 16)
                v.wait_ge(lane_got, 16)
                ln.link(v.tensor_copy(per_edge[:, 0, :], lane[:]))
                for h in range(heads):
                    ln.mark(v.tensor_tensor_scan(per_edge[:, :, h], keep[:], per_edge[:, :, h], 0.0,
                                                 ALU.mult, ALU.add))
                ln.settle()

            @block.sync
            def _(sp):
                sp.wait_ge(zeroed, 1)
                sp.dma_start(firsts.rearrange("(p c) h -> p (c h)", p=P), zero[:]).then_inc(put, 16)
                with nc.allow_non_contiguous_dma("a table of a few columns"):
                    sp.dma_start(table.rearrange("(b p) h -> p b h", p=P), nodes).then_inc(put, 16)
                sp.wait_ge(scattered, 16 * NB)
                sp.dma_start(per_edge[:], firsts.rearrange("(p c) h -> p c h", p=P)).then_inc(loaded, 16)
                sp.wait_ge(loaded, 16)

            @block.gpsimd
            def _(pool):
                pool.wait_ge(made, 2)
                pool.wait_ge(put, 32)
                pool.indirect_dma_start(lane[:], None, table,
                                        bass.IndirectOffsetOnAxis(ap=li[:, 0:1], axis=0)).then_inc(lane_got, 16)
                for b in range(NB):
                    pool.indirect_dma_start(firsts, bass.IndirectOffsetOnAxis(ap=ai[:, b:b + 1], axis=0),
                                            nodes[:, b, :], None, bounds_check=P * cols - 1,
                                            oob_is_err=False).then_inc(scattered, 16)
                pool.wait_ge(scattered, 16 * NB)


def carry_in(nc, g, name, dstf, cols, last, feats, heads, carries):
    width = feats + 2 * heads
    fh = feats // heads
    with Stage(nc, name) as s:
        diag = s.sb("diag", [P, P])
        same = s.sb("same", [P, P])
        off = s.sb("off", [P, P])
        mm = s.sb("mm", [P, heads, P])
        em = s.sb("em", [P, heads, P])
        et = s.sb("et", [P, heads, P])
        nmax = s.sb("nmax", [P, heads])
        out = s.sb("out", [P, width])
        pr = s.ps("pr")
        pt = s.ps("pt")
        pc = s.ps("pc")
        dd, rowed, maxed, exped, turned, copied, summed, done, put, dve, act_s = (s.sem(x) for x in (
            "dd", "rowed", "maxed", "exped", "turned", "copied", "summed", "done", "put", "dve", "act"))
        with s.block() as block:
            @block.vector
            def _(v):
                ln = Links(v, dve)
                for h in range(-1, heads):
                    column = dstf[:, cols - 1:cols] if h < 0 else last[:, feats + heads + h:feats + heads + h + 1]
                    if h >= 0:
                        v.wait_ge(rowed, h + 1)
                    v.tensor_scalar(diag[:], g.ident[:], column, None, ALU.mult).then_inc(dd, 1)
                    v.wait_ge(rowed, h + 2)
                    if h < 0:
                        ln.link(v.tensor_scalar(same[:], pr[:, 0:P], dstf[:, 0:1], None, ALU.is_equal))
                        ln.link(v.tensor_tensor(same[:], same[:], g.below[:], ALU.mult))
                        ln.link(v.tensor_scalar(off[:], same[:], -1.0, BIG, ALU.add, ALU.mult))
                    else:
                        ln.link(v.tensor_tensor(mm[:, h, :], pr[:, 0:P], off[:], ALU.add))
                ln.link(v.tensor_reduce(out[:, feats + heads:], mm[:], AX.X, ALU.max))
                v.tensor_scalar(nmax[:], out[:, feats + heads:], -1.0, None, ALU.mult).then_inc(maxed, 1)
                v.wait_ge(exped, 1)
                for h in range(heads):
                    ln.mark(v.tensor_tensor(em[:, h, :], em[:, h, :], same[:], ALU.mult))
                ln.settle()
                v.sem_inc(exped, 1)
                v.wait_ge(turned, 1)
                v.tensor_copy(flat(et, P), pt[:, 0:heads * P]).then_inc(copied, 1)
                v.wait_ge(summed, 1)
                v.tensor_copy(out[:, 0:feats + heads], pc[:, 0:feats + heads]).then_inc(done, 1)

            @block.tensor
            def _(pe):
                for h in range(heads + 1):
                    pe.wait_ge(dd, h + 1)
                    if h:
                        pe.wait_ge(dve, 3 + h - 1)
                    pe.matmul(pr[:, 0:P], g.ones[:], diag[:], start=True, stop=True).then_inc(rowed, 1)
                pe.wait_ge(exped, 2)
                for h in range(heads):
                    ins = pe.transpose(pt[:, h * P:(h + 1) * P], em[:, h, :], g.ident[:])
                ins.then_inc(turned, 1)
                pe.wait_ge(copied, 1)
                for h in range(heads):
                    pe.matmul(pc[:, h * fh:(h + 1) * fh], et[:, h, :], last[:, h * fh:(h + 1) * fh], start=True, stop=True)
                    ins = pe.matmul(pc[:, feats + h:feats + h + 1], et[:, h, :], last[:, feats + h:feats + h + 1],
                                    start=True, stop=True)
                ins.then_inc(summed, 1)

            @block.scalar
            def _(act):
                act.wait_ge(maxed, 1)
                for h in range(heads):
                    ins = act.activation(em[:, h, :], mm[:, h, :], ACT.Exp, bias=nmax[:, h:h + 1])
                ins.then_inc(exped, 1)

            @block.sync
            def _(sp):
                sp.wait_ge(done, 1)
                sp.dma_start(carries, out[:]).then_inc(put, 16)
                sp.wait_ge(put, 16)


def gather_ends(nc, g, name, s, cols, feats, heads, start, end, table, carries, rows, carried):
    width = feats + 2 * heads
    work = carried
    e1 = s.sb("e1", [P, NB])
    q = s.sb("q", [P, NB])
    ei = s.sb("ei", [P, NB], U32)
    qi = s.sb("qi", [P, NB], U32)
    step = s.sb("step", [P, P])
    big = s.sb("big", [P, NB, P])
    made, dve, got = s.sem("made"), s.sem("gdve"), s.gather_sem("got")
    with s.block() as block:
        @block.vector
        def _(v):
            ln = Links(v, dve)
            ln.mark(v.tensor_scalar(e1[:], end[:], -1.0, 0.0, ALU.add, ALU.max))
            ln.link(v.tensor_scalar(step[:], g.chunkno[:], float(cols), None, ALU.mult))
            ln.link(v.tensor_tensor(big[:], step[:].rearrange("p (o k) -> p o k", o=1).to_broadcast([P, NB, P]),
                                    e1[:].rearrange("p (b o) -> p b o", o=1).to_broadcast([P, NB, P]), ALU.is_le))
            ln.link(v.tensor_reduce(q[:], big[:], AX.X, ALU.add))
            v.tensor_copy(ei[:], e1[:]).then_inc(made, 1)
            v.tensor_copy(qi[:], q[:]).then_inc(made, 1)
            ln.link(v.tensor_scalar(q[:], q[:], float(cols), None, ALU.mult))
            ln.link(v.tensor_tensor(q[:], start[:], q[:], ALU.is_lt))
            ln.link(v.tensor_scalar(q[:], q[:], -1.0, BIG, ALU.add, ALU.mult))
            v.wait_ge(got, 32 * NB)
            for h in range(heads):
                m = carried[:, :, feats + heads + h]
                ln.mark(v.tensor_tensor(m, m, q[:], ALU.add))
            ln.settle()

        @block.gpsimd
        def _(pool):
            pool.wait_ge(made, 2)
            for b in range(NB):
                pool.indirect_dma_start(rows[:, b, :], None, table,
                                        bass.IndirectOffsetOnAxis(ap=ei[:, b:b + 1], axis=0)).then_inc(got, 16)
                pool.indirect_dma_start(carried[:, b, :], None, carries,
                                        bass.IndirectOffsetOnAxis(ap=qi[:, b:b + 1], axis=0)).then_inc(got, 16)
            pool.wait_ge(got, 32 * NB)


def merge(nc, g, s, feats, heads, rows, carried, extra=None, eps=0.0):
    fh = feats // heads
    parts = [rows, carried] + ([extra] if extra is not None else [])
    mt = s.sb("mt", [P, NB, heads])
    dve, act_s, ready = s.sem("mdve"), s.sem("mact"), s.sem("mready")
    mx = [x[:, :, feats + heads:feats + 2 * heads] for x in parts]
    with s.block() as block:
        @block.vector
        def _(v):
            ln = Links(v, dve)
            ln.link(v.tensor_tensor(mt[:], mx[0], mx[1], ALU.max))
            if extra is not None:
                ln.link(v.tensor_tensor(mt[:], mt[:], mx[2], ALU.max))
            for m in mx:
                ln.mark(v.tensor_tensor(m, m, mt[:], ALU.subtract))
            ln.settle()
            v.sem_inc(ready, 1)
            v.wait_ge(act_s, len(parts))
            for h in range(heads):
                for x in parts:
                    f = x[:, :, feats + heads + h:feats + heads + h + 1]
                    ln.mark(v.tensor_tensor(x[:, :, h * fh:(h + 1) * fh], x[:, :, h * fh:(h + 1) * fh],
                                            f.to_broadcast([P, NB, fh]), ALU.mult))
                    ln.mark(v.tensor_tensor(x[:, :, feats + h:feats + h + 1], x[:, :, feats + h:feats + h + 1], f, ALU.mult))
            ln.settle()
            for x in parts[1:]:
                ln.link(v.tensor_tensor(rows[:, :, 0:feats + heads], rows[:, :, 0:feats + heads],
                                        x[:, :, 0:feats + heads], ALU.add))
            ln.link(v.tensor_scalar(mt[:], rows[:, :, feats:feats + heads], eps, None, ALU.add))
            ln.link(v.reciprocal(mt[:], mt[:]))
            for h in range(heads):
                ln.mark(v.tensor_tensor(rows[:, :, h * fh:(h + 1) * fh], rows[:, :, h * fh:(h + 1) * fh],
                                        mt[:, :, h:h + 1].to_broadcast([P, NB, fh]), ALU.mult))
            ln.settle()

        @block.scalar
        def _(act):
            act.wait_ge(ready, 1)
            for m in mx:
                act.activation(m, m, ACT.Exp).then_inc(act_s, 1)


def gat_weights(nc, g, s, w, wew):
    att = s.sb("att", [P, 3 * D])
    junk = s.sb("junk", [P, D])
    got, dve = s.sem("wgot"), s.sem("wdve")
    with s.block() as block:
        @block.sync
        def _(sp):
            sp.dma_start(w[:, :, 0:D], g.W_func.rearrange("(k p) n -> p k n", p=P)).then_inc(got, 16)
            sp.dma_start(att[:], g.W_att.rearrange("n o -> (n o)").partition_broadcast(P)).then_inc(got, 16)
            sp.wait_ge(got, 32)

        @block.vector
        def _(v):
            ln = Links(v, dve)
            v.wait_ge(got, 32)
            ln.mark(v.tensor_copy(wew[:], att[:, 2 * D:]))
            for k in range(2):
                for j in range(2):
                    ln.link(v.tensor_tensor_reduce(junk[:], w[:, k, 0:D], att[:, j * D:(j + 1) * D], 1.0, 0.0,
                                                   ALU.mult, ALU.add, w[:, k, D + j:D + j + 1]))


def gat_edges(nc, g, s, wew, sdst, keep, reset, ztable, sums, last):
    W = D + 2
    turns = C // BC // 2
    ea = [s.sb(f"ea{h}", [P, BC, D]) for h in range(2)]
    zg = [s.sb(f"zg{h}", [P, BC, W]) for h in range(2)]
    ob = [s.sb(f"ob{h}", [P, BC, W]) for h in range(2)]
    ix = [s.sb(f"ix{h}", [P, BC], U32) for h in range(2)]
    ew = s.sb("ew", [P, BC])
    sc = s.sb("sc", [P, BC])
    lk = s.sb("lk", [P, BC])
    mb = [s.sb(f"mb{h}", [P, BC + 1]) for h in range(2)]
    wd = [s.sb(f"wd{h}", [P, 2, BC]) for h in range(2)]
    scored, weighed, done, ea_used = (s.sems(x) for x in ("scored", "weighed", "done", "ea_used"))
    ea_got, stored, scaled = (s.sems(x) for x in ("ea_got", "stored", "scaled"))
    z_got = [s.gather_sem(f"z_got{h}") for h in range(2)]
    dve, ixd, passed, lastd = s.sem("dve"), s.sem("ixd"), s.sem("passed"), s.sem("lastd")
    rows = g.edge256.rearrange("(p c) d -> p c d", p=P)
    out = sums.rearrange("(p c) w -> p c w", p=P)
    with s.block() as block:
        @block.sync
        def _(sp):
            def load(h, turn, c0):
                sp.wait_ge(ea_used[h], turn + 1)
                sp.dma_start(ea[h][:], rows[:, bass.ds(c0, BC), :]).then_inc(ea_got[h], 16)

            def store(h, turn, c0):
                sp.wait_ge(done[h], turn + 2)
                sp.dma_start(out[:, bass.ds(c0, BC), :], ob[h][:]).then_inc(stored[h], 16)

            for h in range(2):
                sp.sem_inc(stored[h], 16)
            load(0, 0, 0)
            with sp.Fori(0, turns - 1) as i:
                load(1, i, (i * 2 + 1) * BC)
                store(0, i, i * 2 * BC)
                load(0, i + 1, (i * 2 + 2) * BC)
                store(1, i, (i * 2 + 1) * BC)
            load(1, turns - 1, (turns * 2 - 1) * BC)
            for h in range(2):
                store(h, turns - 1, (turns * 2 - 2 + h) * BC)
            for h in range(2):
                sp.wait_ge(stored[h], 16 * (turns + 1))

        @block.gpsimd
        def _(pool):
            with pool.Fori(0, turns) as i:
                for h in range(2):
                    gate(pool, done[h], i + 1, passed)
                    pool.tensor_copy(ix[h][:], g.src[:, bass.ds((i * 2 + h) * BC, BC)]).then_inc(ixd, 1)
                    gate(pool, ixd, i * 2 + h + 1, passed)
                    for k in range(BC):
                        pool.indirect_dma_start(zg[h][:, k, :], None, ztable,
                                                bass.IndirectOffsetOnAxis(ap=ix[h][:, k:k + 1], axis=0)).then_inc(z_got[h], 16)
            for h in range(2):
                pool.wait_ge(z_got[h], 16 * BC * turns)

        @block.vector
        def _(v):
            ln = Links(v, dve)
            for h in range(2):
                v.sem_inc(scored[h], 1)
                v.sem_inc(done[h], 1)
                v.sem_inc(ea_used[h], 1)
            ln.mark(v.memset(mb[1][:], 0.0))
            ln.link(v.memset(ob[1][:, BC - 1, :], 0.0))
            with v.Fori(0, turns) as i:
                ln.enter(i, 2 * (8 + BC))
                for h in range(2):
                    cols = bass.ds((i * 2 + h) * BC, BC)
                    v.wait_ge(ea_got[h], (i + 1) * 16)
                    for k in range(BC):
                        ins = v.tensor_tensor_reduce(ea[h][:, k, :], ea[h][:, k, :], wew[:], 1.0, 0.0,
                                                     ALU.mult, ALU.add, ew[:, k:k + 1])
                    ins.then_inc(ea_used[h], 1)
                    v.wait_ge(ea_used[h], i + 2)
                    ln.link(v.tensor_tensor(sc[:], ew[:], sdst[:, cols], ALU.add))
                    v.wait_ge(z_got[h], (i + 1) * (16 * BC))
                    ln.link(v.tensor_tensor(sc[:], sc[:], zg[h][:, :, D], ALU.add))
                    ln.mark(v.tensor_copy(mb[h][:, 0:1], mb[1 - h][:, BC:BC + 1]))
                    ln.link(v.scalar_tensor_tensor(out=lk[:], in0=sc[:], scalar=0.01, in1=sc[:],
                                                   op0=ALU.mult, op1=ALU.max))
                    ln.link(v.tensor_tensor_scan(mb[h][:, 1:BC + 1], reset[:, cols], lk[:], mb[h][:, 0:1],
                                                 ALU.add, ALU.max))
                    v.wait_ge(weighed[h], i + 1)
                    ln.link(v.tensor_tensor(wd[h][:, 0, :], mb[h][:, 0:BC], mb[h][:, 1:BC + 1], ALU.subtract))
                    ln.link(v.tensor_tensor(wd[h][:, 0, :], wd[h][:, 0, :], reset[:, cols], ALU.add))
                    v.tensor_tensor(wd[h][:, 1, :], lk[:], mb[h][:, 1:BC + 1], ALU.subtract).then_inc(scored[h], 1)
                    v.wait_ge(stored[h], (i + 1) * 16)
                    ln.mark(v.tensor_copy(ob[h][:, :, D + 1], mb[h][:, 1:BC + 1]))
                    v.wait_ge(weighed[h], i + 2)
                    v.wait_ge(done[1 - h], i + 1 + h)
                    ln.settle()
                    before = ob[1 - h][:, BC - 1, :]
                    ln.link(v.tensor_tensor_scan(ob[h][:, :, D], wd[h][:, 0, :], wd[h][:, 1, :],
                                                 before[:, D:D + 1], ALU.mult, ALU.add))
                    for k in range(BC):
                        v.wait_ge(scaled[h], i * BC + (k + 1))
                        ins = v.scalar_tensor_tensor(out=ob[h][:, k, 0:D], in0=before[:, 0:D], scalar=wd[h][:, 0, k:k + 1],
                                                     in1=zg[h][:, k, 0:D], op0=ALU.mult, op1=ALU.add)
                        before = ob[h][:, k, :]
                        if k < BC - 1:
                            ln.link(ins)
                        else:
                            ins.then_inc(done[h], 1)
                ln.leave(turns)
            v.wait_ge(done[1], turns + 1)
            v.tensor_copy(last[:], ob[1][:, BC - 1, :]).then_inc(lastd, 1)
            v.wait_ge(lastd, 1)

        @block.scalar
        def _(act):
            for h in range(2):
                act.sem_inc(weighed[h], 1)
            with act.Fori(0, turns) as i:
                for h in range(2):
                    act.wait_ge(scored[h], i + 2)
                    act.activation(flat(wd[h], BC), flat(wd[h], BC), ACT.Exp).then_inc(weighed[h], 1)
                    act.wait_ge(weighed[h], i + 2)
                    act.wait_ge(z_got[h], (i + 1) * (16 * BC))
                    for k in range(BC):
                        act.activation(zg[h][:, k, 0:D], zg[h][:, k, 0:D], ACT.Copy,
                                       scale=wd[h][:, 1, k:k + 1]).then_inc(scaled[h], 1)


def l0_gnn(nc, g):
    W = D + 2
    ztable = nc.dram_tensor("ztable", (NP, W), F32, kind="Internal").ap()
    sums = nc.dram_tensor("gat_sums", (P * C, W), F32, kind="Internal").ap()
    carries = nc.dram_tensor("gat_carries", (P, W), F32, kind="Internal").ap()
    node_stats(nc, g, "st0")
    with Stage(nc, "g0") as s:
        last = s.sb("last", [P, W])
        with Stage(nc, "g0e") as s1:
            wew = s1.sb("wew", [P, D])
            sdst = s1.sb("sdst", [P, C])
            sdn = s1.sb("sdn", [P, NB, 1])
            keep = s1.sb("keep", [P, C])
            reset = s1.sb("reset", [P, C])
            with Stage(nc, "g0w") as s2:
                w = s2.sb("w", [P, 2, W])
                gat_weights(nc, g, s2, w, wew)

                def z_rows(v, ln, h, b, rows, xn, po, out):
                    ln.mark(v.tensor_scalar(flat(sdn, 1)[:, bass.ds(b, 1)], po[:, D + 1:W], 0.0, None, ALU.add))
                    return v.tensor_copy(out[:], po[:, 0:W])

                project(nc, g, "z", w, W, W, z_rows, 1, [(ztable, 0, W)])
            segments(nc, g, "seg", g.dstf, C, E, g.start, g.end, g.keys)
            boundaries(nc, g, "bnd", g.dstf, C, reset, keep)
            spread(nc, g, "sd", sdn[:], 1, g.dstf, C, E, g.start, g.end, keep,
                   sdst[:].rearrange("p (c o) -> p c o", o=1))
            gat_edges(nc, g, s1, wew, sdst, keep, reset, ztable, sums, last)
        carry_in(nc, g, "car0", g.dstf, C, last, D, 1, carries)
        rows = s.sb("rows", [P, NB, W])
        with Stage(nc, "g0f") as s1:
            carried = s1.sb("carried", [P, NB, W])
            gather_ends(nc, g, "end0", s1, C, D, 1, g.start, g.end, sums, carries, rows, carried)
            merge(nc, g, s1, D, 1, rows, carried)
        w = s.sb("wself", [P, 2, D])
        t = [s.sb(f"t{h}", [P, D]) for h in range(2)]
        some = s.sb("some", [P, NB])
        none = s.sb("none", [P, NB])
        got, dv = s.sem("sgot"), s.sem("sdv")
        with s.block() as block:
            @block.sync
            def _(sp):
                sp.dma_start(w[:], g.W_self.rearrange("(k p) n -> p k n", p=P)).then_inc(got, 16)
                sp.wait_ge(got, 16)

            @block.vector
            def _(v):
                ln = Links(v, dv)
                ln.mark(v.tensor_tensor(some[:], g.end[:], g.start[:], ALU.is_gt))
                ln.mark(v.tensor_tensor(none[:], g.end[:], g.start[:], ALU.is_le))
                ln.settle()

        def h_new(v, ln, h, b, rows_x, xn, po, out):
            u = t[h]
            agg = flat(rows, W)[:, bass.ds(b * W, D)]
            ln.link(v.tensor_tensor(u[:], po[:, 0:D], agg, ALU.add))
            ln.link(v.tensor_scalar(u[:], u[:], some[:, bass.ds(b, 1)], None, ALU.mult))
            ln.link(v.scalar_tensor_tensor(out=u[:], in0=xn[:], scalar=none[:, bass.ds(b, 1)], in1=u[:],
                                           op0=ALU.mult, op1=ALU.add))
            ln.link(v.scalar_tensor_tensor(out=u[:], in0=u[:], scalar=0.0, in1=xn[:], op0=ALU.max, op1=ALU.add))
            return v.tensor_tensor(rows_x, rows_x, u[:], ALU.add)

        project(nc, g, "hs", w, D, 0, h_new, 4)


SUPER = 5
HC = 4


def mlp(nc, g, s, name, w1, b1, w2, b2, biased, gates, groups, func, keep_normed):
    turns = NB // SUPER
    width = SUPER * P
    hw = width // 2
    uses = 2 * HC
    xn = s.sb("xn", [P, SUPER, D])
    xt = s.sb("xt", [P, 2, width])
    ht = [s.sb(f"ht{k}", [P, HC, width]) for k in range(2)]
    t = [s.sb(f"t{k}", [P, D]) for k in range(2)]
    pt = [s.ps(f"pt{k}") for k in range(2)]
    ph = [s.ps(f"ph{k}") for k in range(4)]
    py = [s.ps(f"py{k}") for k in range(2)]
    normed, turned, copied, hidden, acted, out_ready, out_read, dve = (s.sem(x) for x in (
        "normed", "turned", "copied", "hidden", "acted", "out_ready", "out_read", "mdve"))
    HU = uses * groups
    YU = SUPER * groups
    with s.block() as block:
        @block.vector
        def _(v):
            ln = Links(v, dve)
            v.sem_inc(out_read, 2)

            def norm(i):
                for j in range(SUPER):
                    b = i * SUPER + j
                    rows = flat(g.x, D)[:, bass.ds(b * D, D)]
                    ln.mark(v.tensor_scalar(xn[:, j, :], rows, g.mean[:, bass.ds(b, 1)], g.rstd[:, bass.ds(b, 1)],
                                            ALU.subtract, ALU.mult))
                ln.settle()
                v.sem_inc(normed, 1)
                if keep_normed:
                    for j in range(SUPER):
                        rows = flat(g.x, D)[:, bass.ds((i * SUPER + j) * D, D)]
                        ln.mark(v.tensor_tensor(rows, rows, xn[:, j, :], ALU.add))
                    ln.settle()

            def outputs(i):
                for q in range(groups):
                    for j in range(SUPER):
                        n = q * SUPER + j
                        b = i * SUPER + j
                        rows = flat(g.x, D)[:, bass.ds(b * D, D)]
                        gate_ = gates[:, bass.ds(b * groups + q, 1)]
                        v.wait_ge(out_ready, i * YU + (10 + n + 1))
                        src = py[n % 2][:, 0:D]
                        if biased[q]:
                            ln.link(v.tensor_tensor(t[n % 2][:], src, b2[:, q, :], ALU.add))
                            src = t[n % 2][:]
                        ln.mark(v.scalar_tensor_tensor(out=rows, in0=src, scalar=gate_, in1=rows,
                                                       op0=ALU.mult, op1=ALU.add))
                        ln.settle()
                        v.sem_inc(out_read, 1)

            per = SUPER * (2 if keep_normed else 1) + sum(SUPER * (2 if z else 1) for z in biased)
            norm(0)
            with v.Fori(0, turns - 1) as i:
                ln.enter(i, per)
                v.wait_ge(turned, i * SUPER + SUPER)
                norm(i + 1)
                outputs(i)
                ln.leave(turns - 1)
            outputs(turns - 1)

        @block.tensor
        def _(pe):
            pe.sem_inc(out_ready, 10)

            def turn(i, first=False):
                pe.wait_ge(normed, i + 1)
                for j in range(SUPER):
                    if j >= 2:
                        pe.wait_ge(copied, i * SUPER + (j - 1))
                    elif not first:
                        pe.wait_ge(copied, i * SUPER)
                    pe.transpose(pt[j % 2][:, 0:P], xn[:, j, 0:P], g.ident[:])
                    pe.transpose(pt[j % 2][:, P:D], xn[:, j, P:D], g.ident[:]).then_inc(turned, 1)

            def hide(i, q):
                if q == 0:
                    pe.wait_ge(copied, i * SUPER + SUPER)
                for c in range(HC):
                    for z in range(2):
                        u = q * uses + 2 * c + z
                        ch = q * HC + c
                        pe.wait_ge(acted, i * HU + (u + 1))
                        for k in range(2):
                            ins = pe.matmul(ph[u % 4][:, 0:hw], w1[:, k, ch * P:(ch + 1) * P],
                                            xt[:, k, z * hw:(z + 1) * hw], start=(k == 0), stop=(k == 1))
                        ins.then_inc(hidden, 1)

            def down(i, q):
                pe.wait_ge(acted, i * HU + ((q + 1) * uses + 4))
                for j in range(SUPER):
                    n = q * SUPER + j
                    pe.wait_ge(out_read, i * YU + (n + 1))
                    for c in range(HC):
                        ins = pe.matmul(py[n % 2][:, 0:D], ht[q % 2][:, c, j * P:(j + 1) * P], w2[:, q * HC + c, :],
                                        start=(c == 0), stop=(c == HC - 1))
                    ins.then_inc(out_ready, 1)

            def body(i, more):
                for q in range(groups):
                    hide(i, q)
                    if q:
                        down(i, q - 1)
                if more:
                    turn(i + 1)
                down(i, groups - 1)

            turn(0, True)
            with pe.Fori(0, turns - 1) as i:
                body(i, True)
            body(turns - 1, False)

        @block.scalar
        def _(act):
            act.sem_inc(acted, 4)

            def copy(i):
                for j in range(SUPER):
                    act.wait_ge(turned, i * SUPER + (j + 1))
                    act.activation(xt[:, :, j * P:(j + 1) * P], pt[j % 2][:, 0:D].rearrange("p (k n) -> p k n", k=2),
                                   ACT.Copy).then_inc(copied, 1)

            def act_groups(i):
                for q in range(groups):
                    act.wait_ge(out_ready, i * YU + (q * SUPER + 5))
                    for c in range(HC):
                        for z in range(2):
                            u = q * uses + 2 * c + z
                            act.wait_ge(hidden, i * HU + (u + 1))
                            act.activation(ht[q % 2][:, c, z * hw:(z + 1) * hw], ph[u % 4][:, 0:hw], func,
                                           bias=b1[:, q * HC + c:q * HC + c + 1]).then_inc(acted, 1)

            copy(0)
            with act.Fori(0, turns - 1) as i:
                act_groups(i)
                copy(i + 1)
            act_groups(turns - 1)


def router(nc, g, wgt):
    with Stage(nc, "rt") as s:
        wr = s.sb("wr", [P, D])
        br = s.sb("br", [P, 1])
        xn = [s.sb(f"xn{h}", [P, D]) for h in range(2)]
        acc = [s.sb(f"acc{h}", [P, 1]) for h in range(2)]
        got, dve = s.sem("got"), s.sem("dve")
        with s.block() as block:
            @block.sync
            def _(sp):
                sp.dma_start(wr[:], g.ins["L0_ffn_wr"].rearrange("n o -> (n o)").partition_broadcast(P)).then_inc(got, 16)
                sp.dma_start(br[:], g.ins["L0_ffn_br"].partition_broadcast(P)).then_inc(got, 16)
                sp.wait_ge(got, 32)

            @block.vector
            def _(v):
                ln = Links(v, dve)
                v.wait_ge(got, 32)
                with v.Fori(0, NB // 2) as i:
                    ln.enter(i, 6)
                    for h in range(2):
                        b = i * 2 + h
                        ln.mark(v.tensor_scalar(xn[h][:], flat(g.x, D)[:, bass.ds(b * D, D)], g.mean[:, bass.ds(b, 1)],
                                                g.rstd[:, bass.ds(b, 1)], ALU.subtract, ALU.mult))
                    ln.settle()
                    for h in range(2):
                        ln.mark(v.tensor_tensor_reduce(xn[h][:], xn[h][:], wr[:], 1.0, 0.0, ALU.mult, ALU.add, acc[h][:]))
                    ln.settle()
                    for h in range(2):
                        ln.mark(v.tensor_scalar(wgt[:, bass.ds(i * 2 + h, 1)], acc[h][:], br[:], None, ALU.add))
                    ln.leave(NB // 2)
                ln.settle()


def choose(nc, g, wgt, count, chosen):
    with Stage(nc, "ch") as s:
        u = s.sb("u", [P, NB], I32)
        half = s.sb("half", [P, NB], I32)
        keys = s.sb("keys", [P, 3, NB])
        mask = s.sb("mask", [P, NB])
        key = s.sb("key", [P, NB])
        junk = s.sb("junk", [P, NB])
        sure = s.sb("sure", [P, NB])
        missing, low, step, cand, cnt, take = (s.sb(n, [P, 1]) for n in ("missing", "low", "step", "cand", "cnt", "take"))
        pc = s.ps("pc")
        counted, summed, dve = s.sem("counted"), s.sem("summed"), s.sem("dve")
        bits = [16, 16, 13]
        with s.block() as block:
            @block.vector
            def _(v):
                ln = Links(v, dve)
                wi = wgt[:].bitcast(I32)
                ln.link(v.tensor_scalar(u[:], wi, 31, -2147483648, ALU.arith_shift_right, ALU.bitwise_or))
                ln.link(v.tensor_tensor(u[:], u[:], wi, ALU.bitwise_xor))
                ln.link(v.tensor_scalar(half[:], u[:], 16, None, ALU.logical_shift_right))
                ln.link(v.tensor_copy(keys[:, 0, :], half[:]))
                ln.link(v.tensor_scalar(half[:], u[:], 65535, None, ALU.bitwise_and))
                ln.mark(v.tensor_copy(keys[:, 1, :], half[:]))
                ln.mark(v.tensor_scalar(keys[:, 2, :], g.nodeid[:], -1.0, float(NP), ALU.mult, ALU.add))
                ln.mark(v.tensor_scalar(mask[:], g.nodeid[:], float(N), None, ALU.is_lt))
                ln.mark(v.memset(chosen[:], 0.0))
                ln.mark(v.memset(missing[:], float(count)))
                done = 0
                for level in range(3):
                    ln.settle()
                    ln.link(v.scalar_tensor_tensor(out=key[:], in0=keys[:, level, :], scalar=1.0, in1=mask[:],
                                                   op0=ALU.add, op1=ALU.mult))
                    ln.mark(v.tensor_scalar(key[:], key[:], -1.0, None, ALU.add))
                    ln.mark(v.memset(low[:], 0.0))
                    ln.mark(v.memset(step[:], float(2 ** (bits[level] - 1))))
                    ln.settle()
                    with v.Fori(0, bits[level]) as i:
                        ln.enter(i, 4)
                        ln.link(v.tensor_tensor(cand[:], low[:], step[:], ALU.add))
                        v.tensor_scalar(junk[:], key[:], cand[:], 0.0, ALU.is_ge, ALU.add,
                                        accum_out=cnt[:]).then_inc(counted, 1)
                        v.wait_ge(summed, i + (done + 1))
                        ln.link(v.tensor_scalar(take[:], pc[:, 0:1], missing[:], step[:], ALU.is_ge, ALU.mult))
                        ln.mark(v.tensor_tensor(low[:], low[:], take[:], ALU.add))
                        ln.mark(v.tensor_scalar(step[:], step[:], 0.5, None, ALU.mult))
                        ln.settle()
                        ln.leave(bits[level])
                    done += bits[level]
                    ln.link(v.tensor_scalar(sure[:], key[:], low[:], None, ALU.is_gt if level < 2 else ALU.is_ge))
                    ln.link(v.tensor_tensor(chosen[:], chosen[:], sure[:], ALU.add))
                    if level < 2:
                        ln.link(v.tensor_scalar(junk[:], key[:], low[:], 0.0, ALU.is_gt, ALU.add, accum_out=cnt[:]))
                        v.sem_inc(counted, 1)
                        v.wait_ge(summed, done + 1)
                        done += 1
                        ln.mark(v.tensor_tensor(missing[:], missing[:], pc[:, 0:1], ALU.subtract))
                        ln.mark(v.tensor_scalar(mask[:], key[:], low[:], None, ALU.is_equal))
                ln.settle()

            @block.tensor
            def _(pe):
                done = 0
                for level in range(3):
                    with pe.Fori(0, bits[level]) as i:
                        pe.wait_ge(counted, i + (done + 1))
                        pe.matmul(pc[:, 0:1], g.ones[:], cnt[:], start=True, stop=True).then_inc(summed, 1)
                    done += bits[level]
                    if level < 2:
                        pe.wait_ge(counted, done + 1)
                        pe.matmul(pc[:, 0:1], g.ones[:], cnt[:], start=True, stop=True).then_inc(summed, 1)
                        done += 1


def l0_ffn(nc, g):
    S, H = N, 4 * D
    kept = max(1, S // 2) - 1
    node_stats(nc, g, "st1")
    with Stage(nc, "f0") as s:
        wgt = s.sb("wgt", [P, NB])
        chosen = s.sb("chosen", [P, NB])
        gates = s.sb("gates", [P, NB, 2])
        w1 = s.sb("w1", [P, 2, H])
        w2 = s.sb("w2", [P, H // P, D])
        b1 = s.sb("b1", [P, H // P])
        b2 = s.sb("b2", [P, 2, D])
        got, dv = s.sem("got"), s.sem("dv")
        router(nc, g, wgt)
        choose(nc, g, wgt, kept, chosen)
        with s.block() as block:
            @block.sync
            def _(sp):
                sp.dma_start(w1[:], g.ins["L0_ffn_w1"].rearrange("(k p) n -> p k n", p=P)).then_inc(got, 16)
                sp.dma_start(w2[:], g.ins["L0_ffn_w2"].rearrange("(k p) n -> p k n", p=P)).then_inc(got, 16)
                with nc.allow_non_contiguous_dma("biases, one for a lane"):
                    sp.dma_start(b1[:], g.ins["L0_ffn_b1"].rearrange("(k p) -> p k", p=P)).then_inc(got, 16)
                sp.dma_start(b2[:, 0, :], g.ins["L0_ffn_b2"].partition_broadcast(P)).then_inc(got, 16)
                sp.wait_ge(got, 64)

            @block.vector
            def _(v):
                for q in range(2):
                    v.tensor_tensor(gates[:, :, q], wgt[:], chosen[:], ALU.mult).then_inc(dv, 1)
                v.wait_ge(dv, 2)

        mlp(nc, g, s, "mlp0", w1, b1, w2, b2, (True, False), flat(gates, 2), 2, ACT.Gelu_apprx_tanh, True)


MSG = 128
HEADS = 4
OUTC = MSG // HEADS
RAD = 64
GC = 4


def message_weights(nc, g, w, bias, wedge, wback, wout, wskip):
    with Stage(nc, "mw") as s:
        n2m = s.sb("n2m", [P, D])
        four = s.sb("four", [P, 4, P])
        fourt = s.sb("fourt", [P, 4 * P])
        we = s.sb("we", [P, RAD])
        wet = s.sb("wet", [RAD, P])
        ed = s.sb("ed", [RAD, RAD])
        m2n = s.sb("m2n", [P, 2, P])
        beta = s.sb("beta", [P, 3, P])
        pa, pb, pc, pd, pe_ = s.ps("pa"), s.ps("pb"), s.ps("pc"), s.ps("pd"), s.ps("pe")
        pf = s.ps("pf")
        got, turned, copied, made, dve = (s.sem(x) for x in ("got", "turned", "copied", "made", "dve"))
        I = g.ins
        with s.block() as block:
            @block.sync
            def _(sp):
                sp.dma_start(n2m[:], I["L1_gnn_W_n2m"]).then_inc(got, 16)
                for k, n in enumerate(("Wq", "Wk", "Wv", "Wskip")):
                    sp.dma_start(four[:, k, :], I["L1_gnn_" + n]).then_inc(got, 16)
                for k, n in enumerate(("bq", "bk", "bv", "bskip")):
                    sp.dma_start(bias[:, k * P:(k + 1) * P], I["L1_gnn_" + n].partition_broadcast(P)).then_inc(got, 16)
                sp.dma_start(we[:], I["L1_gnn_We"]).then_inc(got, 16)
                sp.dma_start(ed[:], I["L1_gnn_W_edge"]).then_inc(got, 16)
                sp.dma_start(m2n[:], I["L1_gnn_W_m2n"].rearrange("(k p) m -> p k m", p=P)).then_inc(got, 16)
                sp.dma_start(flat(beta, P), I["L1_gnn_Wbeta"].rearrange("o n -> (o n)").partition_broadcast(P)).then_inc(got, 16)
                sp.wait_ge(got, 16 * 13)

            @block.tensor
            def _(pe):
                pe.wait_ge(got, 16 * 13)
                for k in range(4):
                    pe.transpose(pa[:, k * P:(k + 1) * P], four[:, k, :], g.ident[:])
                pe.transpose(pb[0:RAD, 0:P], we[:], g.ident[:])
                for k in range(2):
                    ins = pe.transpose(pc[:, k * P:(k + 1) * P], m2n[:, k, :], g.ident[:])
                ins.then_inc(turned, 1)
                pe.wait_ge(copied, 2)
                pe.matmul(pd[:, :], n2m[:, 0:P], fourt[:], start=True, stop=True)
                pe.matmul(pe_[:, :], n2m[:, P:D], fourt[:], start=True, stop=True)
                pe.matmul(pf[0:RAD, 0:P], ed[:], wet[:], start=True, stop=True).then_inc(made, 1)

            @block.vector
            def _(v):
                ln = Links(v, dve)
                v.wait_ge(turned, 1)
                v.tensor_copy(fourt[:], pa[:]).then_inc(copied, 1)
                v.tensor_copy(wet[:], pb[0:RAD, 0:P]).then_inc(copied, 1)
                ln.mark(v.tensor_copy(wback[:, 0, :], pc[:, 0:D]))
                ln.mark(v.tensor_tensor(wout[:], beta[:, 0, :], beta[:, 2, :], ALU.add))
                ln.mark(v.tensor_tensor(wskip[:], beta[:, 1, :], beta[:, 2, :], ALU.subtract))
                v.wait_ge(made, 1)
                ln.mark(v.tensor_copy(w[:, 0, :], pd[:]))
                ln.mark(v.tensor_copy(w[:, 1, :], pe_[:]))
                ln.mark(v.tensor_copy(wedge[:], pf[0:RAD, 0:P]))
                ln.settle()


def attend_edges(nc, g, s, wedge, reset, qtable, kvtable, dsti, sums, last):
    W = MSG + 2 * HEADS
    turns = C // BC // 2
    groups = [range(k, min(k + GC, BC)) for k in range(0, BC, GC)]
    NG = len(groups)
    ea = [s.sb(f"ea{h}", [P, BC, RAD]) for h in range(2)]
    kv = [s.sb(f"kv{h}", [P, BC, 2, MSG]) for h in range(2)]
    qd = [s.sb(f"qd{h}", [P, BC, MSG]) for h in range(2)]
    ob = [s.sb(f"ob{h}", [P, BC, W]) for h in range(2)]
    ix = [s.sb(f"ix{h}", [P, 2, BC], U32) for h in range(2)]
    eat = [s.sb(f"eat{h}", [RAD, GC * P]) for h in range(2)]
    sc = s.sb("sc", [P, HEADS, BC])
    mb = [s.sb(f"mb{h}", [P, HEADS, BC + 1]) for h in range(2)]
    wd = [s.sb(f"wd{h}", [P, 2, HEADS, BC]) for h in range(2)]
    pt = [s.ps(f"pt{h}") for h in range(2)]
    pe_ = [s.ps(f"pe{h}") for h in range(2)]
    scored, weighed, done, ea_used = (s.sems(x) for x in ("scored", "weighed", "done", "ea_used"))
    ea_got, stored = (s.sems(x) for x in ("ea_got", "stored"))
    got = [s.gather_sem(f"got{h}") for h in range(2)]
    turned, copied, e_ready, e_read = (s.sem(x) for x in ("turned", "copied", "e_ready", "e_read"))
    dve, ixd, passed, lastd = s.sem("dve"), s.sem("ixd"), s.sem("passed"), s.sem("lastd")
    pe_passed = s.sem("pe_passed")
    rows = g.edge64.rearrange("(p c) d -> p c d", p=P)
    out = sums.rearrange("(p c) w -> p c w", p=P)
    with s.block() as block:
        @block.sync
        def _(sp):
            def load(h, turn, c0):
                sp.wait_ge(ea_used[h], turn + 1)
                sp.dma_start(ea[h][:], rows[:, bass.ds(c0, BC), :]).then_inc(ea_got[h], 16)

            def store(h, turn, c0):
                sp.wait_ge(done[h], turn + 2)
                sp.dma_start(out[:, bass.ds(c0, BC), :], ob[h][:]).then_inc(stored[h], 16)

            for h in range(2):
                sp.sem_inc(stored[h], 16)
            load(0, 0, 0)
            with sp.Fori(0, turns - 1) as i:
                load(1, i, (i * 2 + 1) * BC)
                store(0, i, i * 2 * BC)
                load(0, i + 1, (i * 2 + 2) * BC)
                store(1, i, (i * 2 + 1) * BC)
            load(1, turns - 1, (turns * 2 - 1) * BC)
            for h in range(2):
                store(h, turns - 1, (turns * 2 - 2 + h) * BC)
            for h in range(2):
                sp.wait_ge(stored[h], 16 * (turns + 1))

        @block.gpsimd
        def _(pool):
            with pool.Fori(0, turns) as i:
                for h in range(2):
                    cols = bass.ds((i * 2 + h) * BC, BC)
                    gate(pool, done[h], i + 1, passed)
                    pool.tensor_copy(ix[h][:, 0, :], g.src[:, cols]).then_inc(ixd, 1)
                    pool.tensor_copy(ix[h][:, 1, :], dsti[:, cols]).then_inc(ixd, 1)
                    gate(pool, ixd, i * 4 + 2 * h + 2, passed)
                    for k in range(BC):
                        pool.indirect_dma_start(kv[h][:, k, :, :].rearrange("p a b -> p (a b)"), None, kvtable,
                                                bass.IndirectOffsetOnAxis(ap=ix[h][:, 0, k:k + 1], axis=0)).then_inc(got[h], 16)
                        pool.indirect_dma_start(qd[h][:, k, :], None, qtable,
                                                bass.IndirectOffsetOnAxis(ap=ix[h][:, 1, k:k + 1], axis=0)).then_inc(got[h], 16)
            for h in range(2):
                pool.wait_ge(got[h], 32 * BC * turns)

        @block.tensor
        def _(pe):
            pe.sem_inc(e_ready, 2)
            for h in range(2):
                pe.sem_inc(ea_used[h], 1)
            with pe.Fori(0, turns) as i:
                for h in range(2):
                    pe.wait_ge(ea_got[h], (i + 1) * 16)
                    for gi, cols in enumerate(groups):
                        n = h * NG + gi
                        gate(pe, copied, i * (2 * NG) + (n + 1), pe_passed)
                        for z, k in enumerate(cols):
                            ins = pe.transpose(pt[n % 2][0:RAD, z * P:(z + 1) * P], ea[h][:, k, :], g.ident[:])
                        ins.then_inc(turned, 1)
                        pe.wait_ge(copied, i * (2 * NG) + (n + 3))
                        pe.wait_ge(e_read, i * (2 * NG) + (n + 1))
                        for z, k in enumerate(cols):
                            ins = pe.matmul(pe_[n % 2][:, z * P:(z + 1) * P], eat[n % 2][:, z * P:(z + 1) * P], wedge[:],
                                            start=True, stop=True)
                        ins.then_inc(e_ready, 1)
                    pe.sem_inc(ea_used[h], 1)

        @block.scalar
        def _(act):
            act.sem_inc(copied, 2)
            for h in range(2):
                act.sem_inc(weighed[h], 1)
            with act.Fori(0, turns) as i:
                for h in range(2):
                    for gi, cols in enumerate(groups):
                        n = h * NG + gi
                        wide = len(cols) * P
                        act.wait_ge(turned, i * (2 * NG) + (n + 1))
                        act.wait_ge(e_ready, i * (2 * NG) + (n + 1))
                        act.activation(eat[n % 2][:, 0:wide], pt[n % 2][0:RAD, 0:wide], ACT.Copy).then_inc(copied, 1)
                    act.wait_ge(scored[h], i + 2)
                    both = wd[h][:].rearrange("p a h c -> p (a h c)")
                    act.activation(both, both, ACT.Exp).then_inc(weighed[h], 1)

        @block.vector
        def _(v):
            ln = Links(v, dve)
            v.sem_inc(e_read, 2)
            for h in range(2):
                v.sem_inc(scored[h], 1)
                v.sem_inc(done[h], 1)
            ln.mark(v.memset(mb[1][:], 0.0))
            ln.link(v.memset(ob[1][:, BC - 1, :], 0.0))
            with v.Fori(0, turns) as i:
                ln.enter(i, 2 * (6 + 4 * HEADS + 2 * BC - 1))
                for h in range(2):
                    cs = bass.ds((i * 2 + h) * BC, BC)
                    v.wait_ge(got[h], (i + 1) * (32 * BC))
                    for gi, cols in enumerate(groups):
                        n = h * NG + gi
                        nc_ = len(cols)
                        part = kv[h][:, cols[0]:cols[0] + nc_, :, :]
                        e = pe_[n % 2][:, 0:nc_ * P].rearrange("p (c o m) -> p c o m", o=1, m=P).to_broadcast([P, nc_, 2, P])
                        v.wait_ge(e_ready, i * (2 * NG) + (n + 3))
                        v.tensor_tensor(part, part, e, ALU.add).then_inc(e_read, 1)
                    v.wait_ge(e_read, i * (2 * NG) + (2 + (h + 1) * NG))
                    ln.link(v.tensor_tensor(qd[h][:], qd[h][:], kv[h][:, :, 0, :], ALU.mult))
                    ln.mark(v.tensor_reduce(sc[:].rearrange("p h c -> p c h"), qd[h][:].rearrange("p c (h d) -> p c h d", h=HEADS),
                                            AX.X, ALU.add))
                    ln.link(v.tensor_copy(mb[h][:, :, 0:1], mb[1 - h][:, :, BC:BC + 1]))
                    for a in range(HEADS):
                        ln.mark(v.tensor_tensor_scan(mb[h][:, a, 1:BC + 1], reset[:, cs], sc[:, a, :], mb[h][:, a, 0:1],
                                                     ALU.add, ALU.max))
                    ln.settle()
                    v.wait_ge(weighed[h], i + 1)
                    ln.link(v.tensor_tensor(wd[h][:, 0, :, :], mb[h][:, :, 0:BC], mb[h][:, :, 1:BC + 1], ALU.subtract))
                    for a in range(HEADS):
                        ln.mark(v.tensor_tensor(wd[h][:, 0, a, :], wd[h][:, 0, a, :], reset[:, cs], ALU.add))
                    ln.link(v.tensor_tensor(wd[h][:, 1, :, :], sc[:], mb[h][:, :, 1:BC + 1], ALU.subtract))
                    v.sem_inc(scored[h], 1)
                    v.wait_ge(stored[h], (i + 1) * 16)
                    ln.mark(v.tensor_copy(ob[h][:, :, MSG + HEADS:].rearrange("p c h -> p h c"), mb[h][:, :, 1:BC + 1]))
                    v.wait_ge(weighed[h], i + 2)
                    v.wait_ge(done[1 - h], i + 1 + h)
                    ln.settle()
                    before = ob[1 - h][:, BC - 1, :]
                    for a in range(HEADS):
                        ln.mark(v.tensor_tensor_scan(ob[h][:, :, MSG + a], wd[h][:, 0, a, :], wd[h][:, 1, a, :],
                                                     before[:, MSG + a:MSG + a + 1], ALU.mult, ALU.add))
                    for a in range(HEADS):
                        vv = kv[h][:, :, 1, a * OUTC:(a + 1) * OUTC]
                        ln.mark(v.tensor_tensor(vv, vv, wd[h][:, 1, a, :].rearrange("p (c o) -> p c o", o=1)
                                                .to_broadcast([P, BC, OUTC]), ALU.mult))
                    ln.settle()
                    for k in range(BC):
                        decay = wd[h][:, 0, :, k:k + 1].to_broadcast([P, HEADS, OUTC])
                        to = ob[h][:, k, 0:MSG]
                        ln.link(v.tensor_tensor(to.rearrange("p (h d) -> p h d", h=HEADS),
                                                before[:, 0:MSG].rearrange("p (h d) -> p h d", h=HEADS), decay, ALU.mult))
                        ins = v.tensor_tensor(to, to, kv[h][:, k, 1, :], ALU.add)
                        before = ob[h][:, k, :]
                        if k < BC - 1:
                            ln.link(ins)
                        else:
                            ins.then_inc(done[h], 1)
                ln.leave(turns)
            v.wait_ge(done[1], turns + 1)
            v.tensor_copy(last[:], ob[1][:, BC - 1, :]).then_inc(lastd, 1)
            v.wait_ge(lastd, 1)


def l1_gnn(nc, g):
    W = MSG + 2 * HEADS
    scale = float(1.0 / np.sqrt(np.float32(OUTC)))
    qtable = nc.dram_tensor("qtable", (NP, MSG), F32, kind="Internal").ap()
    kvtable = nc.dram_tensor("kvtable", (NP, 2 * MSG), F32, kind="Internal").ap()
    sums = nc.dram_tensor("msg_sums", (P * C, W), F32, kind="Internal").ap()
    carries = nc.dram_tensor("msg_carries", (P, W), F32, kind="Internal").ap()
    if l0_gnn not in STAGES:
        segments(nc, g, "seg", g.dstf, C, E, g.start, g.end, g.keys)
    node_stats(nc, g, "st2")
    with Stage(nc, "g1") as s:
        last = s.sb("last", [P, W])
        wback = s.sb("wback", [P, 1, D])
        wedge = s.sb("wedge", [RAD, P])
        wout = s.sb("wout", [P, MSG])
        wskip = s.sb("wskip", [P, MSG])
        xr = s.sb("xr", [P, NB, MSG])
        with Stage(nc, "g1p") as s1:
            w = s1.sb("w", [P, 2, 4 * MSG])
            bias = s1.sb("bias", [P, 4 * MSG])
            message_weights(nc, g, w, bias, wedge, wback, wout, wskip)

            def rows4(v, ln, h, b, rows, xn, po, out):
                ln.mark(v.tensor_tensor(flat(xr, MSG)[:, bass.ds(b * MSG, MSG)], po[:, 3 * MSG:], bias[:, 3 * MSG:], ALU.add))
                ln.link(v.tensor_tensor(out[:], po[:, 0:3 * MSG], bias[:, 0:3 * MSG], ALU.add))
                return v.tensor_scalar(out[:, 0:MSG], out[:, 0:MSG], scale, None, ALU.mult)

            project(nc, g, "qkv", w, 4 * MSG, 3 * MSG, rows4, 2, [(qtable, 0, MSG), (kvtable, MSG, 3 * MSG)])
        with Stage(nc, "g1e") as s1:
            keep = s1.sb("keep", [P, C])
            reset = s1.sb("reset", [P, C])
            dsti = s1.sb("dsti", [P, C], U32)
            dv = s1.sem("dv")
            boundaries(nc, g, "bnd1", g.dstf, C, reset, keep)
            with s1.block() as block:
                @block.vector
                def _(v):
                    ln = Links(v, dv)
                    ln.link(v.tensor_scalar(keep[:], g.dstf[:], float(NP - 1), None, ALU.min))
                    ln.link(v.tensor_copy(dsti[:], keep[:]))
            attend_edges(nc, g, s1, wedge, reset, qtable, kvtable, dsti, sums, last)
        carry_in(nc, g, "car1", g.dstf, C, last, MSG, HEADS, carries)
        rows = s.sb("rows", [P, NB, W])
        with Stage(nc, "g1f") as s1:
            carried = s1.sb("carried", [P, NB, W])
            gather_ends(nc, g, "end1", s1, C, MSG, HEADS, g.start, g.end, sums, carries, rows, carried)
            merge(nc, g, s1, MSG, HEADS, rows, carried, eps=1e-16)
            some = s1.sb("some", [P, NB])
            beta = s1.sb("beta", [P, 2, NB])
            dv, logit, exped = s1.sem("bdv"), s1.sem("logit"), s1.sem("exped")
            tmp = carried[:, :, 0:MSG]
            o = rows[:, :, 0:MSG]

            def wide(t):
                return t.rearrange("p (b o) -> p b o", o=1).to_broadcast([P, NB, MSG])

            def tall(t):
                return t[:].rearrange("p (o m) -> p o m", o=1).to_broadcast([P, NB, MSG])

            with s1.block() as block:
                @block.vector
                def _(v):
                    ln = Links(v, dv)
                    ln.link(v.tensor_tensor(some[:], g.end[:], g.start[:], ALU.is_gt))
                    ln.link(v.tensor_tensor(o, o, wide(some[:]), ALU.mult))
                    ln.link(v.tensor_tensor(tmp, o, tall(wout), ALU.mult))
                    ln.link(v.tensor_reduce(beta[:, 0, :], tmp, AX.X, ALU.add))
                    ln.link(v.tensor_tensor(tmp, xr[:], tall(wskip), ALU.mult))
                    ln.link(v.tensor_reduce(beta[:, 1, :], tmp, AX.X, ALU.add))
                    v.tensor_tensor(beta[:, 0, :], beta[:, 0, :], beta[:, 1, :], ALU.add).then_inc(logit, 1)
                    v.wait_ge(exped, 1)
                    ln.link(v.tensor_scalar(beta[:, 0, :], beta[:, 0, :], 1.0, None, ALU.add))
                    ln.link(v.reciprocal(beta[:, 0, :], beta[:, 0, :]))
                    ln.link(v.tensor_scalar(beta[:, 1, :], beta[:, 0, :], -1.0, 1.0, ALU.mult, ALU.add))
                    ln.mark(v.tensor_tensor(xr[:], xr[:], wide(beta[:, 0, :]), ALU.mult))
                    ln.link(v.tensor_tensor(o, o, wide(beta[:, 1, :]), ALU.mult))
                    ln.link(v.tensor_tensor(xr[:], xr[:], o, ALU.add))

                @block.scalar
                def _(act):
                    act.wait_ge(logit, 1)
                    act.activation(beta[:, 0, :], beta[:, 0, :], ACT.Exp, scale=-1.0).then_inc(exped, 1)

        def mixed(v, b, to):
            return v.tensor_scalar(to[:, 0:MSG], flat(xr, MSG)[:, bass.ds(b * MSG, MSG)], 0.0, None, ALU.add)

        def add(v, ln, h, b, rows_x, xn, po, out):
            return v.tensor_tensor(rows_x, rows_x, po[:, 0:D], ALU.add)

        project(nc, g, "back", wback, D, 0, add, 0, prepare=mixed, depth=1)


EXPERTS = 4
GH = 4
ID_BITS = 13
BC2 = 32


def sort_edges(nc, g, dstf, src):
    bits_j, bits = C2.bit_length() - 1, E2.bit_length() - 1
    chunks = C2 // P
    with Stage(nc, "so") as s:
        ends = s.sb("ends", [P, 2, C2], I32)
        buf = [s.sb(f"buf{k}", [P, C2]) for k in range(2)]
        lane = s.sb("lane", [P, 1], I32)
        bit = s.sb("bit", [P, 1], I32)
        signs = s.sb("signs", [P, bits - bits_j])
        flips = s.sb("flips", [P, bits - bits_j])
        pt = s.ps("pt", [P, C2])
        got, made, ready, turned, dve = (s.sem(x) for x in ("got", "made", "ready", "turned", "dve"))
        trips = [b for k in range(bits_j + 1, bits + 1) for b in range(2)]
        source = []
        with s.block() as block:
            @block.sync
            def _(sp):
                sp.dma_start(ends[:], g.ins["L1_ffn_edge_index"].rearrange("z (p c) -> p z c", p=P)).then_inc(got, 16)
                sp.wait_ge(got, 16)

            @block.gpsimd
            def _(pool):
                pool.iota(lane[:], [[0, 1]], base=0, channel_multiplier=1).then_inc(made, 1)

            @block.vector
            def _(v):
                ln = Links(v, dve)
                v.wait_ge(made, 1)
                for k in range(bits - bits_j):
                    ln.link(v.tensor_scalar(bit[:], lane[:], k, 1, ALU.logical_shift_right, ALU.bitwise_and))
                    ln.link(v.tensor_copy(signs[:, k:k + 1], bit[:]))
                ln.link(v.tensor_scalar(signs[:], signs[:], -2.0, 1.0, ALU.mult, ALU.add))
                ln.mark(v.tensor_copy(flips[:, 0:1], signs[:, 0:1]))
                ln.mark(v.tensor_tensor(flips[:, 1:], signs[:, 1:], signs[:, 0:-1], ALU.mult))
                v.wait_ge(got, 16)
                ln.link(v.tensor_scalar(ends[:, 0, :], ends[:, 0, :], float(N - 1), None, ALU.min))
                ln.link(v.tensor_scalar(ends[:, 1, :], ends[:, 1, :], float(2 ** ID_BITS - 1), None, ALU.min))
                ln.link(v.tensor_scalar(ends[:, 1, :], ends[:, 1, :], ID_BITS, 1 << 28,
                                        ALU.logical_shift_left, ALU.bitwise_or))
                at = 0
                ln.link(v.tensor_tensor(buf[at][:].bitcast(I32), ends[:, 1, :], ends[:, 0, :], ALU.bitwise_or))
                trip = 0

                def compare(lo, hi, to_lo, to_hi, up):
                    ln.mark(v.tensor_tensor(to_lo, lo, hi, ALU.min if up else ALU.max))
                    ln.mark(v.tensor_tensor(to_hi, lo, hi, ALU.max if up else ALU.min))

                def stage(src_, dst_, stride):
                    a, b = (t.rearrange("p (m z i) -> p m z i", z=2, i=stride) for t in (src_, dst_))
                    compare(a[:, :, 0, :], a[:, :, 1, :], b[:, :, 0, :], b[:, :, 1, :], True)
                    ln.settle()

                for k in range(1, bits + 1):
                    if k >= bits_j:
                        j = k - bits_j
                        factor = flips[:, j:j + 1] if k < bits else signs[:, j - 1:j]
                        ln.link(v.tensor_scalar(buf[1 - at][:], buf[at][:], factor, None, ALU.mult))
                        at = 1 - at
                    if k > bits_j:
                        v.sem_inc(ready, 1)
                        source.append(at)
                        trip += 1
                        v.wait_ge(turned, trip)
                        ln.link(v.tensor_copy(buf[1 - at][:], pt[:]))
                        at = 1 - at
                        frm = buf[at][:]
                        for b in range(k - bits_j - 1, -1, -1):
                            stage(frm, buf[1 - at][:], 2 ** b)
                            at = 1 - at
                            frm = buf[at][:]
                        v.sem_inc(ready, 1)
                        source.append(at)
                        trip += 1
                        v.wait_ge(turned, trip)
                        ln.link(v.tensor_copy(buf[1 - at][:], pt[:]))
                        at = 1 - at
                        frm = buf[at][:]
                    else:
                        frm = buf[at][:]
                    for b in range(min(k, bits_j) - 1, -1, -1):
                        if k < bits_j:
                            w = [t.rearrange("p (o d m z i) -> p o d m z i", d=2, m=2 ** (k - 1 - b), z=2, i=2 ** b)
                                 for t in (frm, buf[1 - at][:])]
                            for d in range(2):
                                compare(w[0][:, :, d, :, 0, :], w[0][:, :, d, :, 1, :],
                                        w[1][:, :, d, :, 0, :], w[1][:, :, d, :, 1, :], d == 0)
                            ln.settle()
                        else:
                            stage(frm, buf[1 - at][:], 2 ** b)
                        at = 1 - at
                        frm = buf[at][:]
                keys = buf[at][:].bitcast(I32)
                ln.mark(v.tensor_scalar(ends[:, 0, :], keys, 2 ** ID_BITS - 1, None, ALU.bitwise_and))
                ln.mark(v.tensor_scalar(ends[:, 1, :], keys, ID_BITS, 2 ** ID_BITS - 1,
                                        ALU.logical_shift_right, ALU.bitwise_and))
                ln.settle()
                ln.mark(v.tensor_copy(src[:], ends[:, 0, :]))
                ln.mark(v.tensor_copy(dstf[:], ends[:, 1, :]))
                ln.settle()

            @block.tensor
            def _(pe):
                for trip, at in enumerate(source):
                    pe.wait_ge(ready, trip + 1)
                    for c in range(chunks):
                        ins = pe.transpose(pt[:, c * P:(c + 1) * P], buf[at][:, c * P:(c + 1) * P], g.ident[:])
                    ins.then_inc(turned, 1)


def route_edges(nc, g, s, table, adst, reset, src, sums, last):
    F = GH * EXPERTS
    W, T = F + 2 * GH, F + GH
    turns = C2 // BC2 // 2
    ge = [s.sb(f"ge{h}", [P, BC2, T]) for h in range(2)]
    ob = [s.sb(f"ob{h}", [P, BC2, W]) for h in range(2)]
    ix = [s.sb(f"ix{h}", [P, BC2], U32) for h in range(2)]
    sc = s.sb("sc", [P, GH, BC2])
    lk = s.sb("lk", [P, GH, BC2])
    mb = [s.sb(f"mb{h}", [P, GH, BC2 + 1]) for h in range(2)]
    wd = [s.sb(f"wd{h}", [P, 2, GH, BC2]) for h in range(2)]
    scored, weighed, done = (s.sems(x) for x in ("scored", "weighed", "done"))
    got, stored = [s.gather_sem(f"got{h}") for h in range(2)], s.sems("stored")
    dve, ixd, passed, lastd = s.sem("dve"), s.sem("ixd"), s.sem("passed"), s.sem("lastd")
    out = sums.rearrange("(p c) w -> p c w", p=P)
    with s.block() as block:
        @block.sync
        def _(sp):
            for h in range(2):
                sp.sem_inc(stored[h], 16)
            with sp.Fori(0, turns) as i:
                for h in range(2):
                    sp.wait_ge(done[h], i + 2)
                    sp.dma_start(out[:, bass.ds((i * 2 + h) * BC2, BC2), :], ob[h][:]).then_inc(stored[h], 16)
            for h in range(2):
                sp.wait_ge(stored[h], 16 * (turns + 1))

        @block.gpsimd
        def _(pool):
            with pool.Fori(0, turns) as i:
                for h in range(2):
                    gate(pool, done[h], i + 1, passed)
                    pool.tensor_copy(ix[h][:], src[:, bass.ds((i * 2 + h) * BC2, BC2)]).then_inc(ixd, 1)
                    gate(pool, ixd, i * 2 + h + 1, passed)
                    for k in range(BC2):
                        pool.indirect_dma_start(ge[h][:, k, :], None, table,
                                                bass.IndirectOffsetOnAxis(ap=ix[h][:, k:k + 1], axis=0)).then_inc(got[h], 16)
            for h in range(2):
                pool.wait_ge(got[h], 16 * BC2 * turns)

        @block.scalar
        def _(act):
            for h in range(2):
                act.sem_inc(weighed[h], 1)
            with act.Fori(0, turns) as i:
                for h in range(2):
                    act.wait_ge(scored[h], i + 2)
                    both = wd[h][:].rearrange("p a h c -> p (a h c)")
                    act.activation(both, both, ACT.Exp).then_inc(weighed[h], 1)

        @block.vector
        def _(v):
            ln = Links(v, dve)
            for h in range(2):
                v.sem_inc(scored[h], 1)
                v.sem_inc(done[h], 1)
            ln.mark(v.memset(mb[1][:], 0.0))
            ln.link(v.memset(ob[1][:, BC2 - 1, :], 0.0))
            with v.Fori(0, turns) as i:
                ln.enter(i, 2 * (6 + 4 * GH))
                for h in range(2):
                    cs = bass.ds((i * 2 + h) * BC2, BC2)
                    v.wait_ge(got[h], (i + 1) * (16 * BC2))
                    ln.link(v.tensor_tensor(sc[:].rearrange("p h c -> p c h"), ge[h][:, :, F:T], adst[:, cs, :], ALU.add))
                    ln.link(v.scalar_tensor_tensor(out=lk[:], in0=sc[:], scalar=0.2, in1=sc[:], op0=ALU.mult, op1=ALU.max))
                    ln.link(v.tensor_copy(mb[h][:, :, 0:1], mb[1 - h][:, :, BC2:BC2 + 1]))
                    for a in range(GH):
                        ln.mark(v.tensor_tensor_scan(mb[h][:, a, 1:BC2 + 1], reset[:, cs], lk[:, a, :], mb[h][:, a, 0:1],
                                                     ALU.add, ALU.max))
                    ln.settle()
                    v.wait_ge(weighed[h], i + 1)
                    ln.link(v.tensor_tensor(wd[h][:, 0, :, :], mb[h][:, :, 0:BC2], mb[h][:, :, 1:BC2 + 1], ALU.subtract))
                    for a in range(GH):
                        ln.mark(v.tensor_tensor(wd[h][:, 0, a, :], wd[h][:, 0, a, :], reset[:, cs], ALU.add))
                    ln.link(v.tensor_tensor(wd[h][:, 1, :, :], lk[:], mb[h][:, :, 1:BC2 + 1], ALU.subtract))
                    v.sem_inc(scored[h], 1)
                    v.wait_ge(stored[h], (i + 1) * 16)
                    ln.mark(v.tensor_copy(ob[h][:, :, F + GH:].rearrange("p c h -> p h c"), mb[h][:, :, 1:BC2 + 1]))
                    v.wait_ge(weighed[h], i + 2)
                    v.wait_ge(done[1 - h], i + 1 + h)
                    ln.settle()
                    before = ob[1 - h][:, BC2 - 1, :]
                    for a in range(GH):
                        ln.mark(v.tensor_tensor_scan(ob[h][:, :, F + a], wd[h][:, 0, a, :], wd[h][:, 1, a, :],
                                                     before[:, F + a:F + a + 1], ALU.mult, ALU.add))
                    for a in range(GH):
                        vv = ge[h][:, :, a * EXPERTS:(a + 1) * EXPERTS]
                        ln.mark(v.tensor_tensor(vv, vv, wd[h][:, 1, a, :].rearrange("p (c o) -> p c o", o=1)
                                                .to_broadcast([P, BC2, EXPERTS]), ALU.mult))
                    ln.settle()
                    for f in range(F):
                        ins = v.tensor_tensor_scan(ob[h][:, :, f], wd[h][:, 0, f // EXPERTS, :], ge[h][:, :, f],
                                                   before[:, f:f + 1], ALU.mult, ALU.add)
                    ins.then_inc(done[h], 1)
                ln.leave(turns)
            v.wait_ge(done[1], turns + 1)
            v.tensor_copy(last[:], ob[1][:, BC2 - 1, :]).then_inc(lastd, 1)
            v.wait_ge(lastd, 1)


def routing_weights(nc, g, w):
    F = GH * EXPERTS
    with Stage(nc, "rw") as s:
        att = s.sb("att", [P, 2, F])
        tmp = s.sb("tmp", [P, 2, 2, F])
        got, dve = s.sem("got"), s.sem("dve")
        with s.block() as block:
            @block.sync
            def _(sp):
                sp.dma_start(w[:, :, 0:F], g.ins["L1_ffn_W_gat"].rearrange("(k p) n -> p k n", p=P)).then_inc(got, 16)
                for z, n in enumerate(("att_src", "att_dst")):
                    sp.dma_start(att[:, z, :], g.ins["L1_ffn_" + n].rearrange("h e -> (h e)").partition_broadcast(P)).then_inc(got, 16)
                sp.wait_ge(got, 48)

            @block.vector
            def _(v):
                ln = Links(v, dve)
                v.wait_ge(got, 48)
                for k in range(2):
                    for z in range(2):
                        ln.mark(v.tensor_tensor(tmp[:, k, z, :], w[:, k, 0:F], att[:, z, :], ALU.mult))
                ln.settle()
                for k in range(2):
                    ln.mark(v.tensor_reduce(w[:, k, F:F + 2 * GH].rearrange("p (z h) -> p z h", z=2),
                                            tmp[:, k, :, :].rearrange("p z (h e) -> p z h e", h=GH), AX.X, ALU.add))
                ln.settle()


def expert_gates(nc, g, s, rows, gates):
    F = GH * EXPERTS
    W = F + 2 * GH
    par = s.sb("par", [P, 3, F])
    c = s.sb("c", [P, NB, F])
    sq = s.sb("sq", [P, NB, F])
    m = s.sb("m", [P, NB])
    r = s.sb("r", [P, NB])
    sc = s.sb("sc", [P, NB, EXPERTS])
    better = s.sb("better", [P, NB, EXPERTS])
    cmp_ = s.sb("cmp", [P, NB])
    got, rooted, exped, std, ex, dve = (s.sem(x) for x in ("egot", "rooted", "exped", "estd", "eex", "edve"))

    def wide(t, n):
        return t.rearrange("p (b o) -> p b o", o=1).to_broadcast([P, NB, n])

    def tall(t):
        return t.rearrange("p (o m) -> p o m", o=1).to_broadcast([P, NB, F])

    with s.block() as block:
        @block.sync
        def _(sp):
            for z, n in enumerate(("b_gat", "ln_gamma", "ln_beta")):
                sp.dma_start(par[:, z, :], g.ins["L1_ffn_" + n].partition_broadcast(P)).then_inc(got, 16)
            sp.wait_ge(got, 48)

        @block.vector
        def _(v):
            ln = Links(v, dve)
            v.wait_ge(got, 48)
            ln.link(v.tensor_tensor(c[:], rows[:, :, 0:F], tall(par[:, 0, :]), ALU.add))
            ln.link(v.tensor_reduce(m[:], c[:], AX.X, ALU.add))
            ln.link(v.tensor_scalar(m[:], m[:], 1.0 / F, None, ALU.mult))
            ln.link(v.tensor_tensor(c[:], c[:], wide(m[:], F), ALU.subtract))
            ln.link(v.tensor_tensor(sq[:], c[:], c[:], ALU.mult))
            ln.link(v.tensor_reduce(r[:], sq[:], AX.X, ALU.add))
            v.tensor_scalar(r[:], r[:], 1.0 / F, EPS, ALU.mult, ALU.add).then_inc(std, 1)
            v.wait_ge(rooted, 1)
            ln.link(v.reciprocal(r[:], r[:]))
            ln.link(v.tensor_tensor(c[:], c[:], wide(r[:], F), ALU.mult))
            ln.link(v.tensor_tensor(c[:], c[:], tall(par[:, 1, :]), ALU.mult))
            ln.link(v.tensor_tensor(c[:], c[:], tall(par[:, 2, :]), ALU.add))
            ln.link(v.tensor_reduce(sc[:], c[:].rearrange("p b (h e) -> p b e h", h=GH), AX.X, ALU.add))
            ln.mark(v.tensor_scalar(sc[:], sc[:], 1.0 / GH, None, ALU.mult))
            ln.mark(v.memset(better[:], 0.0))
            ln.settle()
            for e in range(EXPERTS):
                for f in range(EXPERTS):
                    if f != e:
                        ln.link(v.tensor_tensor(cmp_[:], sc[:, :, f], sc[:, :, e], ALU.is_ge if f < e else ALU.is_gt))
                        ln.link(v.tensor_tensor(better[:, :, e], better[:, :, e], cmp_[:], ALU.add))
            ln.mark(v.tensor_scalar(better[:], better[:], 1.5, None, ALU.is_lt))
            ln.link(v.tensor_reduce(m[:], sc[:], AX.X, ALU.max))
            v.tensor_tensor(sc[:], sc[:], wide(m[:], EXPERTS), ALU.subtract).then_inc(ex, 1)
            v.wait_ge(exped, 1)
            ln.link(v.tensor_tensor(sc[:], sc[:], better[:], ALU.mult))
            ln.link(v.tensor_reduce(m[:], sc[:], AX.X, ALU.add))
            ln.link(v.reciprocal(m[:], m[:]))
            ln.link(v.tensor_tensor(gates[:], sc[:], wide(m[:], EXPERTS), ALU.mult))

        @block.scalar
        def _(act):
            act.wait_ge(std, 1)
            act.activation(r[:], r[:], ACT.Sqrt).then_inc(rooted, 1)
            act.wait_ge(ex, 1)
            act.activation(sc[:], sc[:], ACT.Exp).then_inc(exped, 1)


def l1_ffn(nc, g):
    F = GH * EXPERTS
    W, T = F + 2 * GH, F + GH
    table = nc.dram_tensor("rtable", (NP, T), F32, kind="Internal").ap()
    sums = nc.dram_tensor("route_sums", (E2, W), F32, kind="Internal").ap()
    carries = nc.dram_tensor("route_carries", (P, W), F32, kind="Internal").ap()
    keys = nc.dram_tensor("keys2", (E2,), F32, kind="Internal").ap()
    node_stats(nc, g, "st3")
    with Stage(nc, "x1") as s:
        gates = s.sb("gates", [P, NB, EXPERTS])
        with Stage(nc, "x1r") as sr:
            start, end = sr.sb("start", [P, NB]), sr.sb("end", [P, NB])
            own = sr.sb("own", [P, NB, W])
            last = sr.sb("last", [P, W])
            with Stage(nc, "x1e") as s1:
                dstf = s1.sb("dstf", [P, C2])
                src = s1.sb("src", [P, C2], U32)
                keep = s1.sb("keep", [P, C2])
                reset = s1.sb("reset", [P, C2])
                adst = s1.sb("adst", [P, C2, GH])
                adn = s1.sb("adn", [P, NB, GH])
                w = s1.sb("w", [P, 2, W])
                dv = s1.sem("dv")
                sort_edges(nc, g, dstf, src)
                routing_weights(nc, g, w)

                def route_rows(v, ln, h, b, rows, xn, po, out):
                    ln.mark(v.tensor_scalar(flat(own, W)[:, bass.ds(b * W, W)], po[:, 0:W], 0.0, None, ALU.add))
                    ln.mark(v.tensor_scalar(flat(adn, GH)[:, bass.ds(b * GH, GH)], po[:, T:W], 0.0, None, ALU.add))
                    return v.tensor_copy(out[:], po[:, 0:T])

                project(nc, g, "rt1", w, W, T, route_rows, 2, [(table, 0, T)])
                segments(nc, g, "seg2", dstf, C2, E2, start, end, keys)
                boundaries(nc, g, "bnd2", dstf, C2, reset, keep)
                spread(nc, g, "ad", adn[:], GH, dstf, C2, E2, start, end, keep, adst[:])
                with Stage(nc, "x1l") as s2:
                    route_edges(nc, g, s2, table, adst, reset, src, sums, last)
                carry_in(nc, g, "car2", dstf, C2, last, F, GH, carries)
                with s1.block() as block:
                    @block.vector
                    def _(v):
                        ln = Links(v, dv)
                        m = own[:, :, F + GH:]
                        ln.link(v.tensor_tensor(m, m, own[:, :, F:F + GH], ALU.add))
                        ln.link(v.scalar_tensor_tensor(out=m, in0=m, scalar=0.2, in1=m, op0=ALU.mult, op1=ALU.max))
                        ln.link(v.memset(own[:, :, F:F + GH], 1.0))
            rows = sr.sb("rows", [P, NB, W])
            carried = sr.sb("carried", [P, NB, W])
            with Stage(nc, "x1g") as s1:
                gather_ends(nc, g, "end2", s1, C2, F, GH, start, end, sums, carries, rows, carried)
                none = s1.sb("none", [P, NB])
                dv2 = s1.sem("dv2")
                with s1.block() as block:
                    @block.vector
                    def _(v):
                        ln = Links(v, dv2)
                        ln.link(v.tensor_tensor(none[:], end[:], start[:], ALU.is_le))
                        ln.link(v.tensor_scalar(none[:], none[:], -BIG, None, ALU.mult))
                        ln.link(v.tensor_tensor(rows[:, :, F + GH:], rows[:, :, F + GH:],
                                                none[:].rearrange("p (b o) -> p b o", o=1).to_broadcast([P, NB, GH]), ALU.add))
                merge(nc, g, s1, F, GH, rows, carried, extra=own, eps=1e-16)
                expert_gates(nc, g, s1, rows, gates)
        H = 2 * D
        w1 = s.sb("w1", [P, 2, EXPERTS * H])
        w2 = s.sb("w2", [P, EXPERTS * H // P, D])
        b1 = s.sb("b1", [P, EXPERTS * H // P])
        b2 = s.sb("b2", [P, EXPERTS, D])
        got = s.sem("got")
        with s.block() as block:
            @block.sync
            def _(sp):
                for e in range(EXPERTS):
                    sp.dma_start(w1[:, :, e * H:(e + 1) * H], g.ins["L1_ffn_W1"][e].rearrange("(k p) n -> p k n", p=P)).then_inc(got, 16)
                    sp.dma_start(w2[:, e * HC:(e + 1) * HC, :], g.ins["L1_ffn_W2"][e].rearrange("(k p) n -> p k n", p=P)).then_inc(got, 16)
                    sp.dma_start(b2[:, e, :], g.ins["L1_ffn_b2"][e].partition_broadcast(P)).then_inc(got, 16)
                with nc.allow_non_contiguous_dma("biases, one for a lane"):
                    sp.dma_start(b1[:], g.ins["L1_ffn_b1"].rearrange("e (k p) -> p (e k)", p=P)).then_inc(got, 16)
                sp.wait_ge(got, 16 * (3 * EXPERTS + 1))
        mlp(nc, g, s, "mlp1", w1, b1, w2, b2, (True,) * EXPERTS, flat(gates, EXPERTS), EXPERTS, ACT.Gelu, False)


STAGES = [l0_gnn, l0_ffn, l1_gnn, l1_ffn]


def store_nodes(nc, g):
    with Stage(nc, "out") as s:
        put = s.sem("put")
        full = N // P
        with s.block() as block:
            @block.sync
            def _(sp):
                sp.dma_start(g.out[0:full * P, :].rearrange("(b p) d -> p b d", p=P),
                             g.x[:, 0:full, :]).then_inc(put, 16)
                sp.dma_start(g.out[full * P:N, :], g.x[0:N - full * P, full, :]).then_inc(put, 16)
                sp.wait_ge(put, 32)


def program(nc, ins, out):
    Stage.used.clear()
    g = G()
    g.out = out
    g.in_x, g.in_src, g.in_dst, g.edge256, g.edge64 = (ins[n] for n in ("x", "src", "dst", "edge_attr_256", "edge_attr_64"))
    g.ins = ins
    g.W_self, g.W_func, g.W_att = (ins["L0_gnn_" + n] for n in ("W_self", "W_func", "W_att"))
    with Stage(nc, "g") as s:
        g.x = s.sb("x", [P, NB, D])
        g.mean, g.rstd, g.start, g.end, g.nodeid = (s.sb(n, [P, NB]) for n in ("mean", "rstd", "start", "end", "nodeid"))
        g.src = s.sb("src", [P, C], U32)
        g.dstf = s.sb("dstf", [P, C])
        g.ident, g.ones, g.below, g.chunkno = (s.sb(n, [P, P]) for n in ("ident", "ones", "below", "chunkno"))
        g.keys = nc.dram_tensor("keys", (P * C,), F32, kind="Internal").ap()
        load_nodes(nc, g)
        for stage in STAGES:
            stage(nc, g)
            recycle(nc)
        store_nodes(nc, g)


def kernel(**inputs):
    import concourse.bacc as _bacc
    from concourse.bass_utils import run_bass_kernel_spmd as _run

    nc = _bacc.Bacc("TRN2", target_bir_lowering=False, num_devices=1)

    def lay_out(name, a):
        a = np.ascontiguousarray(a)
        if name == "x":
            a = np.concatenate([a, np.zeros((NP - N, D), a.dtype)])
        elif name in ("src", "dst"):
            a = np.concatenate([a, np.full(P * C - E, NP if name == "dst" else 0, a.dtype)]).reshape(P, C)
        elif name.startswith("edge_attr"):
            a = np.concatenate([a, np.zeros((P * C - E, a.shape[1]), a.dtype)])
        return a

    arrays, ins = {}, {}
    for name, a in inputs.items():
        a = lay_out(name, a)
        arrays[f"in_{name}"] = a
        ins[name] = nc.dram_tensor(f"in_{name}", a.shape, mybir.dt.from_np(a.dtype), kind="ExternalInput").ap()
    out = nc.dram_tensor("out_0", (N, D), F32, kind="ExternalOutput").ap()
    program(nc, ins, out)
    r = _run(nc, [arrays], core_ids=[0])
    return r.results[0]["out_0"]
```

```python
from contextlib import ExitStack

import numpy as np

import concourse.bass as bass
from concourse import mybir

ALU = mybir.AluOpType
ACT = mybir.ActivationFunctionType
AX = mybir.AxisListType
F32 = mybir.dt.float32
I32 = mybir.dt.int32
U32 = mybir.dt.uint32

P = 128
N = 6250
D = 256
NB = 50
NP = NB * P
E = 100000
C = 782
BC = 17
E2 = 131072
C2 = E2 // P
PU = 10
RING = 5
BIG = 1e30
EPS = 1e-5


class Links:

    def __init__(self, eng, sem):
        self.eng, self.sem, self.n, self.turns = eng, sem, 0, 0

    def mark(self, ins):
        ins.then_inc(self.sem, 1)
        self.n += 1

    def settle(self):
        self.eng.wait_ge(self.sem, self.turns + self.n)

    def link(self, ins):
        self.mark(ins)
        self.settle()

    def enter(self, i, per):
        self.start, self.per, self.turns = self.n, per, i * per

    def leave(self, count):
        assert self.n - self.start == self.per, f"{self.n - self.start} links in the body"
        self.n, self.turns = self.start + self.per * count, 0


class Stage:

    used = []

    def __init__(self, nc, name):
        self.nc, self.name, self.stack = nc, name, ExitStack()

    def __enter__(self):
        return self

    def __exit__(self, *a):
        return self.stack.__exit__(*a)

    def sb(self, name, shape, dt=F32):
        return self.stack.enter_context(self.nc.sbuf_tensor(f"{self.name}_{name}", shape, dt))

    def ps(self, name, shape=(P, 512), dt=F32):
        return self.stack.enter_context(self.nc.psum_tensor(f"{self.name}_{name}", list(shape), dt))

    def sem(self, name):
        sem = self.nc.alloc_semaphore(f"{self.name}_{name}")
        Stage.used.append(sem)
        return sem

    def gather_sem(self, name):
        return self.nc.alloc_semaphore(f"{self.name}_{name}")

    def sems(self, name, n=2):
        return [self.sem(f"{name}{i}") for i in range(n)]

    def block(self):
        return self.nc.Block()


def recycle(nc):
    numbers = sorted(s.num for s in Stage.used)
    with nc.Block() as block:
        @block.gpsimd
        def _(pool):
            while numbers:
                n = 1
                while n < len(numbers) and numbers[n] == numbers[0] + n:
                    n += 1
                pool.sem_clear(range(numbers[0], numbers[0] + n))
                del numbers[:n]
    for s in Stage.used:
        nc.release_semaphore(s)
    Stage.used.clear()


def gate(eng, sem, value, passed):
    eng.wait_ge(sem, value)
    eng.sem_inc(passed, 1)


def flat(t, w):
    return t[:].rearrange("p a b -> p (a b)")


class G:
    pass


def load_nodes(nc, g):
    with Stage(nc, "ld") as s:
        dma, made, dve = s.sem("dma"), s.sem("made"), s.sem("dve")
        itmp = s.sb("itmp", [P, NB], I32)
        ktmp = s.sb("ktmp", [P, P], I32)
        dtmp = s.sb("dtmp", [P, C], I32)
        with s.block() as block:
            @block.sync
            def _(sp):
                sp.dma_start(g.x[:], g.in_x.rearrange("(b p) d -> p b d", p=P)).then_inc(dma, 16)
                sp.dma_start(g.src[:], g.in_src.bitcast(U32)).then_inc(dma, 16)
                sp.dma_start(dtmp[:], g.in_dst).then_inc(dma, 16)
                sp.wait_ge(dma, 48)

            @block.gpsimd
            def _(pool):
                pool.memset(g.ident[:], 0.0).then_inc(made, 1)
                pool.memset(g.ones[:], 1.0).then_inc(made, 1)
                pool.memset(g.below[:], 1.0).then_inc(made, 1)
                pool.iota(itmp[:], [[P, NB]], base=0, channel_multiplier=1).then_inc(made, 1)
                pool.iota(ktmp[:], [[1, P]], base=1, channel_multiplier=0).then_inc(made, 1)
                pool.wait_ge(made, 5)
                pool.affine_select(out=g.ident[:], in_=g.ident[:], compare_op=ALU.not_equal, fill=1.0,
                                   base=0, pattern=[[-1, P]], channel_multiplier=1).then_inc(made, 1)
                pool.affine_select(out=g.below[:], in_=g.below[:], compare_op=ALU.is_gt, fill=0.0,
                                   base=0, pattern=[[-1, P]], channel_multiplier=1).then_inc(made, 1)

            @block.vector
            def _(v):
                v.wait_ge(made, 7)
                v.tensor_copy(g.nodeid[:], itmp[:]).then_inc(dve, 1)
                v.tensor_copy(g.chunkno[:], ktmp[:]).then_inc(dve, 1)
                v.wait_ge(dma, 48)
                v.tensor_copy(g.dstf[:], dtmp[:]).then_inc(dve, 1)
                v.wait_ge(dve, 3)


def node_stats(nc, g, name):
    with Stage(nc, name) as s:
        six = s.sb("six", [P, NB * 6])
        t = s.sb("t", [P, 3, NB])
        dve, var_ready, std_ready = s.sem("dve"), s.sem("var_ready"), s.sem("std_ready")
        v6 = six[:].rearrange("p (b k) -> p k b", k=6)
        with s.block() as block:
            @block.vector
            def _(v):
                ln = Links(v, dve)
                with v.Fori(0, NB // PU) as i:
                    ln.enter(i, PU)
                    for u in range(PU):
                        b = i * PU + u
                        ln.mark(v.bn_stats(six[:, bass.ds(b * 6, 6)], flat(g.x, D)[:, bass.ds(b * D, D)]))
                    ln.leave(NB // PU)
                ln.settle()
                ln.mark(v.tensor_tensor(g.mean[:], v6[:, 1, :], v6[:, 4, :], ALU.add))
                ln.mark(v.tensor_tensor(t[:, 0, :], v6[:, 1, :], v6[:, 4, :], ALU.subtract))
                ln.link(v.tensor_tensor(t[:, 1, :], v6[:, 2, :], v6[:, 5, :], ALU.add))
                ln.mark(v.tensor_scalar(g.mean[:], g.mean[:], 0.5, None, ALU.mult))
                ln.mark(v.tensor_scalar(t[:, 1, :], t[:, 1, :], 1.0 / D, EPS, ALU.mult, ALU.add))
                ln.link(v.tensor_tensor(t[:, 0, :], t[:, 0, :], t[:, 0, :], ALU.mult))
                v.scalar_tensor_tensor(out=t[:, 2, :], in0=t[:, 0, :], scalar=0.25, in1=t[:, 1, :],
                                       op0=ALU.mult, op1=ALU.add).then_inc(var_ready, 1)
                v.wait_ge(std_ready, 1)
                ln.link(v.reciprocal(g.rstd[:], t[:, 2, :]))

            @block.scalar
            def _(act):
                act.wait_ge(var_ready, 1)
                act.activation(t[:, 2, :], t[:, 2, :], ACT.Sqrt).then_inc(std_ready, 1)


def project(nc, g, name, w, width, out_width, finish, per, tables=(), prepare=None, depth=2):
    turns = NB // PU
    with Stage(nc, name) as s:
        xn = [s.sb(f"xn{k}", [P, D]) for k in range(RING)]
        out = [s.sb(f"out{k}", [P, max(out_width, 1)]) for k in range(RING)]
        xt = [s.sb(f"xt{h}", [P, 2, P]) for h in range(2)]
        pt = [s.ps(f"pt{h}") for h in range(2)]
        po = [s.ps(f"po{h}") for h in range(2)]
        normed, turned, copied, product, finished, dve = (s.sem(x) for x in (
            "normed", "turned", "copied", "product", "finished", "dve"))
        stored = s.sems("stored", RING)
        with s.block() as block:
            def rows(b):
                return flat(g.x, D)[:, bass.ds(b * D, D)]

            @block.vector
            def _(v):
                ln = Links(v, dve)
                v.sem_inc(finished, RING)

                def norm(i, u):
                    b = i * PU + u
                    v.wait_ge(finished, i * PU + (u + 1))
                    if prepare is not None:
                        prepare(v, b, xn[u % RING]).then_inc(normed, 1)
                        return
                    v.tensor_scalar(xn[u % RING][:], rows(b), g.mean[:, bass.ds(b, 1)], g.rstd[:, bass.ds(b, 1)],
                                    ALU.subtract, ALU.mult).then_inc(normed, 1)

                def blocks(i, final=False):
                    for u in range(PU):
                        if u + 2 < PU or not final:
                            norm(i, u + 2)
                        v.wait_ge(product, i * PU + (u + 3))
                        if tables:
                            v.wait_ge(stored[u % RING], (i * (PU // RING) + (u // RING + 1)) * (16 * len(tables)))
                        b = i * PU + u
                        finish(v, ln, u % 2, b, rows(b), xn[u % RING], po[u % 2], out[u % RING]).then_inc(finished, 1)

                norm(0, 0)
                norm(0, 1)
                with v.Fori(0, turns - 1) as i:
                    ln.enter(i, PU * per)
                    blocks(i)
                    ln.leave(turns - 1)
                blocks(turns - 1, final=True)
                v.wait_ge(finished, NB + RING)

            @block.tensor
            def _(pe):
                pe.sem_inc(product, 2)

                def turn(i, u):
                    pe.wait_ge(normed, i * PU + (u + 1))
                    pe.wait_ge(copied, i * PU + (u + 1))
                    for k in range(depth):
                        ins = pe.transpose(pt[u % 2][:, k * P:(k + 1) * P], xn[u % RING][:, k * P:(k + 1) * P], g.ident[:])
                    ins.then_inc(turned, 1)

                def blocks(i, final=False):
                    for u in range(PU):
                        if u + 1 < PU or not final:
                            turn(i, u + 1)
                        pe.wait_ge(copied, i * PU + (u + 3))
                        pe.wait_ge(finished, i * PU + (u + RING - 1))
                        for k in range(depth):
                            ins = pe.matmul(po[u % 2][:, 0:width], xt[u % 2][:, k, :], w[:, k, :], start=(k == 0),
                                            stop=(k == depth - 1))
                        ins.then_inc(product, 1)

                turn(0, 0)
                with pe.Fori(0, turns - 1) as i:
                    blocks(i)
                blocks(turns - 1, final=True)

            @block.scalar
            def _(act):
                act.sem_inc(copied, 2)
                with act.Fori(0, turns) as i:
                    for u in range(PU):
                        act.wait_ge(turned, i * PU + (u + 1))
                        act.wait_ge(product, i * PU + (u + 1))
                        act.activation(flat(xt[u % 2], P)[:, 0:depth * P], pt[u % 2][:, 0:depth * P],
                                       ACT.Copy).then_inc(copied, 1)

            if tables:
                @block.sync
                def _(sp):
                    for k in range(RING):
                        sp.sem_inc(stored[k], 16 * len(tables))
                    with sp.Fori(0, turns) as i:
                        for u in range(PU):
                            sp.wait_ge(finished, i * PU + (u + 1 + RING))
                            for to, c0, c1 in tables:
                                sp.dma_start(to[bass.ds((i * PU + u) * P, P), :],
                                             out[u % RING][:, c0:c1]).then_inc(stored[u % RING], 16)
                    for k in range(RING):
                        sp.wait_ge(stored[k], 16 * len(tables) * (NB // RING + 1))


def segments(nc, g, name, dstf, cols, edges, start, end, keys):
    groups = cols * P // P
    with Stage(nc, name) as s:
        firsts = s.sb("firsts", [1, groups])
        firstb = s.sb("firstb", [P, groups])
        c1 = s.sb("c1", [P, NB])
        gi = s.sb("gi", [P, NB], U32)
        rows = s.sb("rows", [P, NB, P])
        one = s.sb("one", [1, 1])
        pb = [s.ps(f"pb{h}") for h in range(2)]
        half = groups // 2
        put, got, made, bc, counted, wrote, dve = (s.sem(x) for x in (
            "put", "got", "made", "bc", "counted", "wrote", "dve"))
        gath = s.gather_sem("gath")
        counts = nc.dram_tensor(f"{name}_counts", (NP + 1, 1), F32, kind="Internal").ap()
        with s.block() as block:
            @block.sync
            def _(sp):
                sp.dma_start(keys.rearrange("(p c) -> p c", p=P), dstf[:]).then_inc(put, 16)
                sp.wait_ge(put, 16)
                with nc.allow_non_contiguous_dma("one key of every 128"):
                    sp.dma_start(firsts[:], keys.rearrange("(a g k) -> a g k", a=1, k=P)[:, :, 0]).then_inc(got, 16)
                    sp.wait_ge(counted, 1)
                    sp.dma_start(counts[0:NP, :].rearrange("(b p) o -> p (b o)", p=P), start[:]).then_inc(wrote, 16)
                    sp.dma_start(counts[NP:NP + 1, :], one[:]).then_inc(wrote, 16)
                    sp.wait_ge(wrote, 32)
                    sp.dma_start(end[:], counts[1:NP + 1, :].rearrange("(b p) o -> p (b o)", p=P)).then_inc(wrote, 16)
                    sp.wait_ge(wrote, 48)

            @block.tensor
            def _(pe):
                pe.wait_ge(got, 16)
                for h in range(2):
                    pe.matmul(pb[h][:, 0:half], g.ones[0:1, :], firsts[:, h * half:(h + 1) * half],
                              start=True, stop=True).then_inc(bc, 1)

            @block.vector
            def _(v):
                ln = Links(v, dve)
                ln.mark(v.memset(one[:], float(edges)))
                v.wait_ge(bc, 2)
                for h in range(2):
                    ln.mark(v.tensor_copy(firstb[:, h * half:(h + 1) * half], pb[h][:, 0:half]))
                ln.settle()
                for b in range(NB):
                    if b % 6 == 0:
                        ln.settle()
                    junk = flat(rows, P)[:, (b % 6) * groups:(b % 6 + 1) * groups]
                    ln.mark(v.tensor_scalar(junk, firstb[:], g.nodeid[:, b:b + 1], 0.0, ALU.is_lt, ALU.add,
                                            accum_out=c1[:, b:b + 1]))
                ln.settle()
                ln.link(v.tensor_scalar(c1[:], c1[:], -1.0, 0.0, ALU.add, ALU.max))
                v.tensor_copy(gi[:], c1[:]).then_inc(made, 1)
                v.wait_ge(gath, 16 * NB)
                ln.link(v.tensor_tensor(rows[:], rows[:], g.nodeid[:].rearrange("p (b o) -> p b o", o=1).to_broadcast([P, NB, P]),
                                        ALU.is_lt))
                ln.link(v.tensor_reduce(start[:], rows[:], AX.X, ALU.add))
                v.scalar_tensor_tensor(out=start[:], in0=c1[:], scalar=float(P), in1=start[:],
                                       op0=ALU.mult, op1=ALU.add).then_inc(counted, 1)

            @block.gpsimd
            def _(pool):
                pool.wait_ge(made, 1)
                for b in range(NB):
                    pool.indirect_dma_start(rows[:, b, :], None, keys.rearrange("(g k) -> g k", k=P),
                                            bass.IndirectOffsetOnAxis(ap=gi[:, b:b + 1], axis=0)).then_inc(gath, 16)
                pool.wait_ge(gath, 16 * NB)


def boundaries(nc, g, name, dstf, cols, reset, keep):
    with Stage(nc, name) as s:
        dve = s.sem("dve")
        with s.block() as block:
            @block.vector
            def _(v):
                ln = Links(v, dve)
                ln.mark(v.memset(keep[:, 0:1], 0.0))
                ln.mark(v.tensor_tensor(keep[:, 1:cols], dstf[:, 1:cols], dstf[:, 0:cols - 1], ALU.is_equal))
                ln.settle()
                ln.link(v.tensor_scalar(reset[:], keep[:], -1.0, BIG, ALU.add, ALU.mult))


def spread(nc, g, name, nodes, heads, dstf, cols, edges, start, end, keep, per_edge):
    with Stage(nc, name) as s:
        table = nc.dram_tensor(f"{name}_table", (NP, heads), F32, kind="Internal").ap()
        firsts = nc.dram_tensor(f"{name}_firsts", (P * cols, heads), F32, kind="Internal").ap()
        zero = s.sb("zero", [P, cols * heads])
        at = s.sb("at", [P, NB], F32)
        empty = s.sb("empty", [P, NB], F32)
        ai = s.sb("ai", [P, NB], U32)
        lane = s.sb("lane", [P, heads])
        li = s.sb("li", [P, 1], U32)
        lf = s.sb("lf", [P, 1], F32)
        zeroed, made, put, loaded, dve = (s.sem(x) for x in ("zeroed", "made", "put", "loaded", "dve"))
        scattered, lane_got = s.gather_sem("scattered"), s.gather_sem("lane_got")
        with s.block() as block:
            @block.vector
            def _(v):
                ln = Links(v, dve)
                v.memset(zero[:], 0.0).then_inc(zeroed, 1)
                ln.mark(v.tensor_tensor(empty[:], start[:], end[:], ALU.is_ge))
                ln.link(v.tensor_scalar(lf[:], dstf[:, 0:1], float(NP - 1), None, ALU.min))
                ln.link(v.scalar_tensor_tensor(out=at[:], in0=empty[:], scalar=float(1 << 20), in1=start[:],
                                               op0=ALU.mult, op1=ALU.add))
                v.tensor_copy(ai[:], at[:]).then_inc(made, 1)
                v.tensor_copy(li[:], lf[:]).then_inc(made, 1)
                v.wait_ge(loaded, 16)
                v.wait_ge(lane_got, 16)
                ln.link(v.tensor_copy(per_edge[:, 0, :], lane[:]))
                for h in range(heads):
                    ln.mark(v.tensor_tensor_scan(per_edge[:, :, h], keep[:], per_edge[:, :, h], 0.0,
                                                 ALU.mult, ALU.add))
                ln.settle()

            @block.sync
            def _(sp):
                sp.wait_ge(zeroed, 1)
                sp.dma_start(firsts.rearrange("(p c) h -> p (c h)", p=P), zero[:]).then_inc(put, 16)
                with nc.allow_non_contiguous_dma("a table of a few columns"):
                    sp.dma_start(table.rearrange("(b p) h -> p b h", p=P), nodes).then_inc(put, 16)
                sp.wait_ge(scattered, 16 * NB)
                sp.dma_start(per_edge[:], firsts.rearrange("(p c) h -> p c h", p=P)).then_inc(loaded, 16)
                sp.wait_ge(loaded, 16)

            @block.gpsimd
            def _(pool):
                pool.wait_ge(made, 2)
                pool.wait_ge(put, 32)
                pool.indirect_dma_start(lane[:], None, table,
                                        bass.IndirectOffsetOnAxis(ap=li[:, 0:1], axis=0)).then_inc(lane_got, 16)
                for b in range(NB):
                    pool.indirect_dma_start(firsts, bass.IndirectOffsetOnAxis(ap=ai[:, b:b + 1], axis=0),
                                            nodes[:, b, :], None, bounds_check=P * cols - 1,
                                            oob_is_err=False).then_inc(scattered, 16)
                pool.wait_ge(scattered, 16 * NB)


def carry_in(nc, g, name, dstf, cols, last, feats, heads, sums):
    width = feats + 2 * heads
    fh = feats // heads
    top = slice(feats + heads, width)
    with Stage(nc, name) as s:
        diag = s.sb("diag", [P, P])
        same = s.sb("same", [P, P])
        off = s.sb("off", [P, P])
        mm = s.sb("mm", [P, heads, P])
        em = s.sb("em", [P, heads, P])
        et = s.sb("et", [P, heads, P])
        nmax = s.sb("nmax", [P, heads])
        carried = s.sb("carried", [P, width])
        row = s.sb("row", [P, width])
        run = s.sb("run", [P, cols])
        at, base = s.sb("at", [P, 1]), s.sb("base", [P, 1], I32)
        ai = s.sb("ai", [P, 1], U32)
        m = s.sb("m", [P, 3, heads])
        pr = s.ps("pr")
        pt = s.ps("pt")
        pc = s.ps("pc")
        based, found, dd, rowed, maxed, exped, turned, copied, summed, factors, merged, dve = (s.sem(x) for x in (
            "based", "found", "dd", "rowed", "maxed", "exped", "turned", "copied", "summed", "factors", "merged", "dve"))
        got, put = s.gather_sem("got"), s.gather_sem("put")
        with s.block() as block:
            @block.gpsimd
            def _(pool):
                pool.iota(base[:], [[0, 1]], base=-1, channel_multiplier=cols).then_inc(based, 1)
                pool.wait_ge(found, 1)
                pool.indirect_dma_start(row[:], None, sums, bass.IndirectOffsetOnAxis(ap=ai[:, 0:1], axis=0)).then_inc(got, 16)
                pool.wait_ge(merged, 1)
                pool.indirect_dma_start(sums, bass.IndirectOffsetOnAxis(ap=ai[:, 0:1], axis=0), row[:], None).then_inc(put, 16)
                pool.wait_ge(put, 16)

            @block.vector
            def _(v):
                ln = Links(v, dve)
                ln.link(v.tensor_scalar(run[:], dstf[:], dstf[:, 0:1], 0.0, ALU.is_equal, ALU.add, accum_out=at[:]))
                v.wait_ge(based, 1)
                ln.link(v.tensor_copy(nmax[:, 0:1], base[:]))
                ln.link(v.tensor_tensor(at[:], at[:], nmax[:, 0:1], ALU.add))
                v.tensor_copy(ai[:], at[:]).then_inc(found, 1)
                for h in range(-1, heads):
                    column = dstf[:, cols - 1:cols] if h < 0 else last[:, feats + heads + h:feats + heads + h + 1]
                    if h >= 0:
                        v.wait_ge(rowed, h + 1)
                    v.tensor_scalar(diag[:], g.ident[:], column, None, ALU.mult).then_inc(dd, 1)
                    v.wait_ge(rowed, h + 2)
                    if h < 0:
                        ln.link(v.tensor_scalar(same[:], pr[:, 0:P], dstf[:, 0:1], None, ALU.is_equal))
                        ln.link(v.tensor_tensor(same[:], same[:], g.below[:], ALU.mult))
                        ln.link(v.tensor_scalar(off[:], same[:], -1.0, BIG, ALU.add, ALU.mult))
                    else:
                        ln.link(v.tensor_tensor(mm[:, h, :], pr[:, 0:P], off[:], ALU.add))
                ln.link(v.tensor_reduce(carried[:, top], mm[:], AX.X, ALU.max))
                v.tensor_scalar(nmax[:], carried[:, top], -1.0, None, ALU.mult).then_inc(maxed, 1)
                v.wait_ge(got, 16)
                ln.link(v.tensor_tensor(m[:, 2, :], carried[:, top], row[:, top], ALU.max))
                ln.mark(v.tensor_tensor(m[:, 0, :], row[:, top], m[:, 2, :], ALU.subtract))
                ln.mark(v.tensor_tensor(m[:, 1, :], carried[:, top], m[:, 2, :], ALU.subtract))
                ln.settle()
                ln.link(v.tensor_copy(row[:, top], m[:, 2, :]))
                v.sem_inc(factors, 1)
                v.wait_ge(exped, 1)
                for h in range(heads):
                    ln.mark(v.tensor_tensor(em[:, h, :], em[:, h, :], same[:], ALU.mult))
                ln.settle()
                v.sem_inc(exped, 1)
                v.wait_ge(turned, 1)
                v.tensor_copy(flat(et, P), pt[:, 0:heads * P]).then_inc(copied, 1)
                v.wait_ge(summed, 1)
                ln.link(v.tensor_copy(carried[:, 0:feats + heads], pc[:, 0:feats + heads]))
                v.wait_ge(factors, 2)
                for h in range(heads):
                    for part in (slice(h * fh, (h + 1) * fh), slice(feats + h, feats + h + 1)):
                        ln.mark(v.tensor_scalar(row[:, part], row[:, part], m[:, 0, h:h + 1], None, ALU.mult))
                ln.settle()
                for h in range(heads):
                    for part in (slice(h * fh, (h + 1) * fh), slice(feats + h, feats + h + 1)):
                        ln.mark(v.scalar_tensor_tensor(out=row[:, part], in0=carried[:, part], scalar=m[:, 1, h:h + 1],
                                                       in1=row[:, part], op0=ALU.mult, op1=ALU.add))
                ln.settle()
                v.sem_inc(merged, 1)

            @block.tensor
            def _(pe):
                for h in range(heads + 1):
                    pe.wait_ge(dd, h + 1)
                    if h:
                        pe.wait_ge(dve, 6 + h - 1)
                    pe.matmul(pr[:, 0:P], g.ones[:], diag[:], start=True, stop=True).then_inc(rowed, 1)
                pe.wait_ge(exped, 2)
                for h in range(heads):
                    ins = pe.transpose(pt[:, h * P:(h + 1) * P], em[:, h, :], g.ident[:])
                ins.then_inc(turned, 1)
                pe.wait_ge(copied, 1)
                for h in range(heads):
                    pe.matmul(pc[:, h * fh:(h + 1) * fh], et[:, h, :], last[:, h * fh:(h + 1) * fh], start=True, stop=True)
                    ins = pe.matmul(pc[:, feats + h:feats + h + 1], et[:, h, :], last[:, feats + h:feats + h + 1],
                                    start=True, stop=True)
                ins.then_inc(summed, 1)

            @block.scalar
            def _(act):
                act.wait_ge(maxed, 1)
                for h in range(heads):
                    ins = act.activation(em[:, h, :], mm[:, h, :], ACT.Exp, bias=nmax[:, h:h + 1])
                ins.then_inc(exped, 1)
                act.wait_ge(factors, 1)
                act.activation(m[:, 0:2, :], m[:, 0:2, :], ACT.Exp).then_inc(factors, 1)


def gather_ends(nc, g, name, s, end, table, rows):
    e1 = s.sb("e1", [P, NB])
    ei = s.sb("ei", [P, NB], U32)
    made, dve, got = s.sem("made"), s.sem("gdve"), s.gather_sem("got")
    with s.block() as block:
        @block.vector
        def _(v):
            ln = Links(v, dve)
            ln.link(v.tensor_scalar(e1[:], end[:], -1.0, 0.0, ALU.add, ALU.max))
            v.tensor_copy(ei[:], e1[:]).then_inc(made, 1)

        @block.gpsimd
        def _(pool):
            pool.wait_ge(made, 1)
            for b in range(NB):
                pool.indirect_dma_start(rows[:, b, :], None, table,
                                        bass.IndirectOffsetOnAxis(ap=ei[:, b:b + 1], axis=0)).then_inc(got, 16)
            pool.wait_ge(got, 16 * NB)


def merge(nc, g, s, feats, heads, rows, extra=None, eps=0.0):
    fh = feats // heads
    parts = [rows] + ([extra] if extra is not None else [])
    mt = s.sb("mt", [P, NB, heads])
    dve, act_s, ready = s.sem("mdve"), s.sem("mact"), s.sem("mready")
    mx = [x[:, :, feats + heads:feats + 2 * heads] for x in parts]
    with s.block() as block:
        @block.vector
        def _(v):
            ln = Links(v, dve)
            if extra is not None:
                ln.link(v.tensor_tensor(mt[:], mx[0], mx[1], ALU.max))
                for m in mx:
                    ln.mark(v.tensor_tensor(m, m, mt[:], ALU.subtract))
                ln.settle()
                v.sem_inc(ready, 1)
                v.wait_ge(act_s, len(parts))
                for h in range(heads):
                    for x in parts:
                        f = x[:, :, feats + heads + h:feats + heads + h + 1]
                        ln.mark(v.tensor_tensor(x[:, :, h * fh:(h + 1) * fh], x[:, :, h * fh:(h + 1) * fh],
                                                f.to_broadcast([P, NB, fh]), ALU.mult))
                        ln.mark(v.tensor_tensor(x[:, :, feats + h:feats + h + 1], x[:, :, feats + h:feats + h + 1], f, ALU.mult))
                ln.settle()
                ln.link(v.tensor_tensor(rows[:, :, 0:feats + heads], rows[:, :, 0:feats + heads],
                                        extra[:, :, 0:feats + heads], ALU.add))
            ln.link(v.tensor_scalar(mt[:], rows[:, :, feats:feats + heads], eps, None, ALU.add))
            ln.link(v.reciprocal(mt[:], mt[:]))
            for h in range(heads):
                ln.mark(v.tensor_tensor(rows[:, :, h * fh:(h + 1) * fh], rows[:, :, h * fh:(h + 1) * fh],
                                        mt[:, :, h:h + 1].to_broadcast([P, NB, fh]), ALU.mult))
            ln.settle()

        if extra is not None:
            @block.scalar
            def _(act):
                act.wait_ge(ready, 1)
                for m in mx:
                    act.activation(m, m, ACT.Exp).then_inc(act_s, 1)


def gat_weights(nc, g, s, w, wew):
    att = s.sb("att", [P, 3 * D])
    junk = s.sb("junk", [P, D])
    got, dve = s.sem("wgot"), s.sem("wdve")
    with s.block() as block:
        @block.sync
        def _(sp):
            sp.dma_start(w[:, :, 0:D], g.W_func.rearrange("(k p) n -> p k n", p=P)).then_inc(got, 16)
            sp.dma_start(att[:], g.W_att.rearrange("n o -> (n o)").partition_broadcast(P)).then_inc(got, 16)
            sp.wait_ge(got, 32)

        @block.vector
        def _(v):
            ln = Links(v, dve)
            v.wait_ge(got, 32)
            ln.mark(v.tensor_copy(wew[:], att[:, 2 * D:]))
            for k in range(2):
                for j in range(2):
                    ln.link(v.tensor_tensor_reduce(junk[:], w[:, k, 0:D], att[:, j * D:(j + 1) * D], 1.0, 0.0,
                                                   ALU.mult, ALU.add, w[:, k, D + j:D + j + 1]))


def gat_edges(nc, g, s, wew, sdst, keep, reset, ztable, sums, last):
    W = D + 2
    turns = C // BC // 2
    ea = [s.sb(f"ea{h}", [P, BC, D]) for h in range(2)]
    zg = [s.sb(f"zg{h}", [P, BC, W]) for h in range(2)]
    ob = [s.sb(f"ob{h}", [P, BC, W]) for h in range(2)]
    ix = [s.sb(f"ix{h}", [P, BC], U32) for h in range(2)]
    ew = s.sb("ew", [P, BC])
    sc = s.sb("sc", [P, BC])
    lk = s.sb("lk", [P, BC])
    mb = [s.sb(f"mb{h}", [P, BC + 1]) for h in range(2)]
    wd = [s.sb(f"wd{h}", [P, 2, BC]) for h in range(2)]
    scored, weighed, done, ea_used = (s.sems(x) for x in ("scored", "weighed", "done", "ea_used"))
    ea_got, stored, scaled = (s.sems(x) for x in ("ea_got", "stored", "scaled"))
    z_got = [s.gather_sem(f"z_got{h}") for h in range(2)]
    dve, ixd, passed, lastd = s.sem("dve"), s.sem("ixd"), s.sem("passed"), s.sem("lastd")
    rows = g.edge256.rearrange("(p c) d -> p c d", p=P)
    out = sums.rearrange("(p c) w -> p c w", p=P)
    with s.block() as block:
        @block.sync
        def _(sp):
            def load(h, turn, c0):
                sp.wait_ge(ea_used[h], turn + 1)
                sp.dma_start(ea[h][:], rows[:, bass.ds(c0, BC), :]).then_inc(ea_got[h], 16)

            def store(h, turn, c0):
                sp.wait_ge(done[h], turn + 2)
                sp.dma_start(out[:, bass.ds(c0, BC), :], ob[h][:]).then_inc(stored[h], 16)

            for h in range(2):
                sp.sem_inc(stored[h], 16)
            load(0, 0, 0)
            with sp.Fori(0, turns - 1) as i:
                load(1, i, (i * 2 + 1) * BC)
                store(0, i, i * 2 * BC)
                load(0, i + 1, (i * 2 + 2) * BC)
                store(1, i, (i * 2 + 1) * BC)
            load(1, turns - 1, (turns * 2 - 1) * BC)
            for h in range(2):
                store(h, turns - 1, (turns * 2 - 2 + h) * BC)
            for h in range(2):
                sp.wait_ge(stored[h], 16 * (turns + 1))

        @block.gpsimd
        def _(pool):
            with pool.Fori(0, turns) as i:
                for h in range(2):
                    gate(pool, done[h], i + 1, passed)
                    pool.tensor_copy(ix[h][:], g.src[:, bass.ds((i * 2 + h) * BC, BC)]).then_inc(ixd, 1)
                    gate(pool, ixd, i * 2 + h + 1, passed)
                    for k in range(BC):
                        pool.indirect_dma_start(zg[h][:, k, :], None, ztable,
                                                bass.IndirectOffsetOnAxis(ap=ix[h][:, k:k + 1], axis=0)).then_inc(z_got[h], 16)
            for h in range(2):
                pool.wait_ge(z_got[h], 16 * BC * turns)

        @block.vector
        def _(v):
            ln = Links(v, dve)
            for h in range(2):
                v.sem_inc(scored[h], 1)
                v.sem_inc(done[h], 1)
                v.sem_inc(ea_used[h], 1)
            ln.mark(v.memset(mb[1][:], 0.0))
            ln.link(v.memset(ob[1][:, BC - 1, :], 0.0))
            with v.Fori(0, turns) as i:
                ln.enter(i, 2 * (8 + BC))
                for h in range(2):
                    cols = bass.ds((i * 2 + h) * BC, BC)
                    v.wait_ge(ea_got[h], (i + 1) * 16)
                    for k in range(BC):
                        ins = v.tensor_tensor_reduce(ea[h][:, k, :], ea[h][:, k, :], wew[:], 1.0, 0.0,
                                                     ALU.mult, ALU.add, ew[:, k:k + 1])
                    ins.then_inc(ea_used[h], 1)
                    v.wait_ge(ea_used[h], i + 2)
                    ln.link(v.tensor_tensor(sc[:], ew[:], sdst[:, cols], ALU.add))
                    v.wait_ge(z_got[h], (i + 1) * (16 * BC))
                    ln.link(v.tensor_tensor(sc[:], sc[:], zg[h][:, :, D], ALU.add))
                    ln.mark(v.tensor_copy(mb[h][:, 0:1], mb[1 - h][:, BC:BC + 1]))
                    ln.link(v.scalar_tensor_tensor(out=lk[:], in0=sc[:], scalar=0.01, in1=sc[:],
                                                   op0=ALU.mult, op1=ALU.max))
                    ln.link(v.tensor_tensor_scan(mb[h][:, 1:BC + 1], reset[:, cols], lk[:], mb[h][:, 0:1],
                                                 ALU.add, ALU.max))
                    v.wait_ge(weighed[h], i + 1)
                    ln.link(v.tensor_tensor(wd[h][:, 0, :], mb[h][:, 0:BC], mb[h][:, 1:BC + 1], ALU.subtract))
                    ln.link(v.tensor_tensor(wd[h][:, 0, :], wd[h][:, 0, :], reset[:, cols], ALU.add))
                    v.tensor_tensor(wd[h][:, 1, :], lk[:], mb[h][:, 1:BC + 1], ALU.subtract).then_inc(scored[h], 1)
                    v.wait_ge(stored[h], (i + 1) * 16)
                    ln.mark(v.tensor_copy(ob[h][:, :, D + 1], mb[h][:, 1:BC + 1]))
                    v.wait_ge(weighed[h], i + 2)
                    v.wait_ge(done[1 - h], i + 1 + h)
                    ln.settle()
                    before = ob[1 - h][:, BC - 1, :]
                    ln.link(v.tensor_tensor_scan(ob[h][:, :, D], wd[h][:, 0, :], wd[h][:, 1, :],
                                                 before[:, D:D + 1], ALU.mult, ALU.add))
                    for k in range(BC):
                        v.wait_ge(scaled[h], i * BC + (k + 1))
                        ins = v.scalar_tensor_tensor(out=ob[h][:, k, 0:D], in0=before[:, 0:D], scalar=wd[h][:, 0, k:k + 1],
                                                     in1=zg[h][:, k, 0:D], op0=ALU.mult, op1=ALU.add)
                        before = ob[h][:, k, :]
                        if k < BC - 1:
                            ln.link(ins)
                        else:
                            ins.then_inc(done[h], 1)
                ln.leave(turns)
            v.wait_ge(done[1], turns + 1)
            v.tensor_copy(last[:], ob[1][:, BC - 1, :]).then_inc(lastd, 1)
            v.wait_ge(lastd, 1)

        @block.scalar
        def _(act):
            for h in range(2):
                act.sem_inc(weighed[h], 1)
            with act.Fori(0, turns) as i:
                for h in range(2):
                    act.wait_ge(scored[h], i + 2)
                    act.activation(flat(wd[h], BC), flat(wd[h], BC), ACT.Exp).then_inc(weighed[h], 1)
                    act.wait_ge(weighed[h], i + 2)
                    act.wait_ge(z_got[h], (i + 1) * (16 * BC))
                    for k in range(BC):
                        act.activation(zg[h][:, k, 0:D], zg[h][:, k, 0:D], ACT.Copy,
                                       scale=wd[h][:, 1, k:k + 1]).then_inc(scaled[h], 1)


def l0_gnn(nc, g):
    W = D + 2
    ztable = nc.dram_tensor("ztable", (NP, W), F32, kind="Internal").ap()
    sums = nc.dram_tensor("gat_sums", (P * C, W), F32, kind="Internal").ap()
    node_stats(nc, g, "st0")
    with Stage(nc, "g0") as s:
        last = s.sb("last", [P, W])
        with Stage(nc, "g0e") as s1:
            wew = s1.sb("wew", [P, D])
            sdst = s1.sb("sdst", [P, C])
            sdn = s1.sb("sdn", [P, NB, 1])
            keep = s1.sb("keep", [P, C])
            reset = s1.sb("reset", [P, C])
            with Stage(nc, "g0w") as s2:
                w = s2.sb("w", [P, 2, W])
                gat_weights(nc, g, s2, w, wew)

                def z_rows(v, ln, h, b, rows, xn, po, out):
                    ln.mark(v.tensor_scalar(flat(sdn, 1)[:, bass.ds(b, 1)], po[:, D + 1:W], 0.0, None, ALU.add))
                    return v.tensor_copy(out[:], po[:, 0:W])

                project(nc, g, "z", w, W, W, z_rows, 1, [(ztable, 0, W)])
            segments(nc, g, "seg", g.dstf, C, E, g.start, g.end, g.keys)
            boundaries(nc, g, "bnd", g.dstf, C, reset, keep)
            spread(nc, g, "sd", sdn[:], 1, g.dstf, C, E, g.start, g.end, keep,
                   sdst[:].rearrange("p (c o) -> p c o", o=1))
            gat_edges(nc, g, s1, wew, sdst, keep, reset, ztable, sums, last)
        carry_in(nc, g, "car0", g.dstf, C, last, D, 1, sums)
        rows = s.sb("rows", [P, NB, W])
        with Stage(nc, "g0f") as s1:
            gather_ends(nc, g, "end0", s1, g.end, sums, rows)
            merge(nc, g, s1, D, 1, rows)
        w = s.sb("wself", [P, 2, D])
        t = [s.sb(f"t{h}", [P, D]) for h in range(2)]
        some = s.sb("some", [P, NB])
        none = s.sb("none", [P, NB])
        got, dv = s.sem("sgot"), s.sem("sdv")
        with s.block() as block:
            @block.sync
            def _(sp):
                sp.dma_start(w[:], g.W_self.rearrange("(k p) n -> p k n", p=P)).then_inc(got, 16)
                sp.wait_ge(got, 16)

            @block.vector
            def _(v):
                ln = Links(v, dv)
                ln.mark(v.tensor_tensor(some[:], g.end[:], g.start[:], ALU.is_gt))
                ln.mark(v.tensor_tensor(none[:], g.end[:], g.start[:], ALU.is_le))
                ln.settle()

        def h_new(v, ln, h, b, rows_x, xn, po, out):
            u = t[h]
            agg = flat(rows, W)[:, bass.ds(b * W, D)]
            ln.link(v.tensor_tensor(u[:], po[:, 0:D], agg, ALU.add))
            ln.link(v.tensor_scalar(u[:], u[:], some[:, bass.ds(b, 1)], None, ALU.mult))
            ln.link(v.scalar_tensor_tensor(out=u[:], in0=xn[:], scalar=none[:, bass.ds(b, 1)], in1=u[:],
                                           op0=ALU.mult, op1=ALU.add))
            ln.link(v.scalar_tensor_tensor(out=u[:], in0=u[:], scalar=0.0, in1=xn[:], op0=ALU.max, op1=ALU.add))
            return v.tensor_tensor(rows_x, rows_x, u[:], ALU.add)

        project(nc, g, "hs", w, D, 0, h_new, 4)


SUPER = 5
HC = 4


def mlp(nc, g, s, name, w1, b1, w2, b2, biased, gates, groups, func, keep_normed):
    turns = NB // SUPER
    width = SUPER * P
    hw = width // 2
    uses = 2 * HC
    xn = s.sb("xn", [P, SUPER, D])
    xt = s.sb("xt", [P, 2, width])
    ht = [s.sb(f"ht{k}", [P, HC, width]) for k in range(2)]
    t = [s.sb(f"t{k}", [P, D]) for k in range(2)]
    pt = [s.ps(f"pt{k}") for k in range(2)]
    ph = [s.ps(f"ph{k}") for k in range(4)]
    py = [s.ps(f"py{k}") for k in range(2)]
    normed, turned, copied, hidden, acted, out_ready, out_read, dve = (s.sem(x) for x in (
        "normed", "turned", "copied", "hidden", "acted", "out_ready", "out_read", "mdve"))
    HU = uses * groups
    YU = SUPER * groups
    with s.block() as block:
        @block.vector
        def _(v):
            ln = Links(v, dve)
            v.sem_inc(out_read, 2)

            def norm(i):
                for j in range(SUPER):
                    b = i * SUPER + j
                    rows = flat(g.x, D)[:, bass.ds(b * D, D)]
                    ln.mark(v.tensor_scalar(xn[:, j, :], rows, g.mean[:, bass.ds(b, 1)], g.rstd[:, bass.ds(b, 1)],
                                            ALU.subtract, ALU.mult))
                ln.settle()
                v.sem_inc(normed, 1)
                if keep_normed:
                    for j in range(SUPER):
                        rows = flat(g.x, D)[:, bass.ds((i * SUPER + j) * D, D)]
                        ln.mark(v.tensor_tensor(rows, rows, xn[:, j, :], ALU.add))
                    ln.settle()

            def outputs(i):
                for q in range(groups):
                    for j in range(SUPER):
                        n = q * SUPER + j
                        b = i * SUPER + j
                        rows = flat(g.x, D)[:, bass.ds(b * D, D)]
                        gate_ = gates[:, bass.ds(b * groups + q, 1)]
                        v.wait_ge(out_ready, i * YU + (10 + n + 1))
                        src = py[n % 2][:, 0:D]
                        if biased[q]:
                            ln.link(v.tensor_tensor(t[n % 2][:], src, b2[:, q, :], ALU.add))
                            src = t[n % 2][:]
                        ln.mark(v.scalar_tensor_tensor(out=rows, in0=src, scalar=gate_, in1=rows,
                                                       op0=ALU.mult, op1=ALU.add))
                        ln.settle()
                        v.sem_inc(out_read, 1)

            per = SUPER * (2 if keep_normed else 1) + sum(SUPER * (2 if z else 1) for z in biased)
            norm(0)
            with v.Fori(0, turns - 1) as i:
                ln.enter(i, per)
                v.wait_ge(turned, i * SUPER + SUPER)
                norm(i + 1)
                outputs(i)
                ln.leave(turns - 1)
            outputs(turns - 1)

        @block.tensor
        def _(pe):
            pe.sem_inc(out_ready, 10)

            def turn(i, first=False):
                pe.wait_ge(normed, i + 1)
                for j in range(SUPER):
                    if j >= 2:
                        pe.wait_ge(copied, i * SUPER + (j - 1))
                    elif not first:
                        pe.wait_ge(copied, i * SUPER)
                    pe.transpose(pt[j % 2][:, 0:P], xn[:, j, 0:P], g.ident[:])
                    pe.transpose(pt[j % 2][:, P:D], xn[:, j, P:D], g.ident[:]).then_inc(turned, 1)

            def hide(i, q):
                if q == 0:
                    pe.wait_ge(copied, i * SUPER + SUPER)
                for c in range(HC):
                    for z in range(2):
                        u = q * uses + 2 * c + z
                        ch = q * HC + c
                        pe.wait_ge(acted, i * HU + (u + 1))
                        for k in range(2):
                            ins = pe.matmul(ph[u % 4][:, 0:hw], w1[:, k, ch * P:(ch + 1) * P],
                                            xt[:, k, z * hw:(z + 1) * hw], start=(k == 0), stop=(k == 1))
                        ins.then_inc(hidden, 1)

            def down(i, q):
                pe.wait_ge(acted, i * HU + ((q + 1) * uses + 4))
                for j in range(SUPER):
                    n = q * SUPER + j
                    pe.wait_ge(out_read, i * YU + (n + 1))
                    for c in range(HC):
                        ins = pe.matmul(py[n % 2][:, 0:D], ht[q % 2][:, c, j * P:(j + 1) * P], w2[:, q * HC + c, :],
                                        start=(c == 0), stop=(c == HC - 1))
                    ins.then_inc(out_ready, 1)

            def body(i, more):
                for q in range(groups):
                    hide(i, q)
                    if q:
                        down(i, q - 1)
                if more:
                    turn(i + 1)
                down(i, groups - 1)

            turn(0, True)
            with pe.Fori(0, turns - 1) as i:
                body(i, True)
            body(turns - 1, False)

        @block.scalar
        def _(act):
            act.sem_inc(acted, 4)

            def copy(i):
                for j in range(SUPER):
                    act.wait_ge(turned, i * SUPER + (j + 1))
                    act.activation(xt[:, :, j * P:(j + 1) * P], pt[j % 2][:, 0:D].rearrange("p (k n) -> p k n", k=2),
                                   ACT.Copy).then_inc(copied, 1)

            def act_groups(i):
                for q in range(groups):
                    act.wait_ge(out_ready, i * YU + (q * SUPER + 5))
                    for c in range(HC):
                        for z in range(2):
                            u = q * uses + 2 * c + z
                            act.wait_ge(hidden, i * HU + (u + 1))
                            act.activation(ht[q % 2][:, c, z * hw:(z + 1) * hw], ph[u % 4][:, 0:hw], func,
                                           bias=b1[:, q * HC + c:q * HC + c + 1]).then_inc(acted, 1)

            copy(0)
            with act.Fori(0, turns - 1) as i:
                act_groups(i)
                copy(i + 1)
            act_groups(turns - 1)


def router(nc, g, wgt):
    with Stage(nc, "rt") as s:
        wr = s.sb("wr", [P, D])
        br = s.sb("br", [P, 1])
        xn = [s.sb(f"xn{h}", [P, D]) for h in range(2)]
        acc = [s.sb(f"acc{h}", [P, 1]) for h in range(2)]
        got, dve = s.sem("got"), s.sem("dve")
        with s.block() as block:
            @block.sync
            def _(sp):
                sp.dma_start(wr[:], g.ins["L0_ffn_wr"].rearrange("n o -> (n o)").partition_broadcast(P)).then_inc(got, 16)
                sp.dma_start(br[:], g.ins["L0_ffn_br"].partition_broadcast(P)).then_inc(got, 16)
                sp.wait_ge(got, 32)

            @block.vector
            def _(v):
                ln = Links(v, dve)
                v.wait_ge(got, 32)
                with v.Fori(0, NB // 2) as i:
                    ln.enter(i, 6)
                    for h in range(2):
                        b = i * 2 + h
                        ln.mark(v.tensor_scalar(xn[h][:], flat(g.x, D)[:, bass.ds(b * D, D)], g.mean[:, bass.ds(b, 1)],
                                                g.rstd[:, bass.ds(b, 1)], ALU.subtract, ALU.mult))
                    ln.settle()
                    for h in range(2):
                        ln.mark(v.tensor_tensor_reduce(xn[h][:], xn[h][:], wr[:], 1.0, 0.0, ALU.mult, ALU.add, acc[h][:]))
                    ln.settle()
                    for h in range(2):
                        ln.mark(v.tensor_scalar(wgt[:, bass.ds(i * 2 + h, 1)], acc[h][:], br[:], None, ALU.add))
                    ln.leave(NB // 2)
                ln.settle()


def choose(nc, g, wgt, count, chosen):
    with Stage(nc, "ch") as s:
        u = s.sb("u", [P, NB], I32)
        half = s.sb("half", [P, NB], I32)
        keys = s.sb("keys", [P, 3, NB])
        mask = s.sb("mask", [P, NB])
        key = s.sb("key", [P, NB])
        junk = s.sb("junk", [P, NB])
        sure = s.sb("sure", [P, NB])
        missing, low, step, cand, cnt, take = (s.sb(n, [P, 1]) for n in ("missing", "low", "step", "cand", "cnt", "take"))
        pc = s.ps("pc")
        counted, summed, dve = s.sem("counted"), s.sem("summed"), s.sem("dve")
        bits = [16, 16, 13]
        with s.block() as block:
            @block.vector
            def _(v):
                ln = Links(v, dve)
                wi = wgt[:].bitcast(I32)
                ln.link(v.tensor_scalar(u[:], wi, 31, -2147483648, ALU.arith_shift_right, ALU.bitwise_or))
                ln.link(v.tensor_tensor(u[:], u[:], wi, ALU.bitwise_xor))
                ln.link(v.tensor_scalar(half[:], u[:], 16, None, ALU.logical_shift_right))
                ln.link(v.tensor_copy(keys[:, 0, :], half[:]))
                ln.link(v.tensor_scalar(half[:], u[:], 65535, None, ALU.bitwise_and))
                ln.mark(v.tensor_copy(keys[:, 1, :], half[:]))
                ln.mark(v.tensor_scalar(keys[:, 2, :], g.nodeid[:], -1.0, float(NP), ALU.mult, ALU.add))
                ln.mark(v.tensor_scalar(mask[:], g.nodeid[:], float(N), None, ALU.is_lt))
                ln.mark(v.memset(chosen[:], 0.0))
                ln.mark(v.memset(missing[:], float(count)))
                done = 0
                for level in range(3):
                    ln.settle()
                    ln.link(v.scalar_tensor_tensor(out=key[:], in0=keys[:, level, :], scalar=1.0, in1=mask[:],
                                                   op0=ALU.add, op1=ALU.mult))
                    ln.mark(v.tensor_scalar(key[:], key[:], -1.0, None, ALU.add))
                    ln.mark(v.memset(low[:], 0.0))
                    ln.mark(v.memset(step[:], float(2 ** (bits[level] - 1))))
                    ln.settle()
                    with v.Fori(0, bits[level]) as i:
                        ln.enter(i, 4)
                        ln.link(v.tensor_tensor(cand[:], low[:], step[:], ALU.add))
                        v.tensor_scalar(junk[:], key[:], cand[:], 0.0, ALU.is_ge, ALU.add,
                                        accum_out=cnt[:]).then_inc(counted, 1)
                        v.wait_ge(summed, i + (done + 1))
                        ln.link(v.tensor_scalar(take[:], pc[:, 0:1], missing[:], step[:], ALU.is_ge, ALU.mult))
                        ln.mark(v.tensor_tensor(low[:], low[:], take[:], ALU.add))
                        ln.mark(v.tensor_scalar(step[:], step[:], 0.5, None, ALU.mult))
                        ln.settle()
                        ln.leave(bits[level])
                    done += bits[level]
                    ln.link(v.tensor_scalar(sure[:], key[:], low[:], None, ALU.is_gt if level < 2 else ALU.is_ge))
                    ln.link(v.tensor_tensor(chosen[:], chosen[:], sure[:], ALU.add))
                    if level < 2:
                        ln.link(v.tensor_scalar(junk[:], key[:], low[:], 0.0, ALU.is_gt, ALU.add, accum_out=cnt[:]))
                        v.sem_inc(counted, 1)
                        v.wait_ge(summed, done + 1)
                        done += 1
                        ln.mark(v.tensor_tensor(missing[:], missing[:], pc[:, 0:1], ALU.subtract))
                        ln.mark(v.tensor_scalar(mask[:], key[:], low[:], None, ALU.is_equal))
                ln.settle()

            @block.tensor
            def _(pe):
                done = 0
                for level in range(3):
                    with pe.Fori(0, bits[level]) as i:
                        pe.wait_ge(counted, i + (done + 1))
                        pe.matmul(pc[:, 0:1], g.ones[:], cnt[:], start=True, stop=True).then_inc(summed, 1)
                    done += bits[level]
                    if level < 2:
                        pe.wait_ge(counted, done + 1)
                        pe.matmul(pc[:, 0:1], g.ones[:], cnt[:], start=True, stop=True).then_inc(summed, 1)
                        done += 1


def l0_ffn(nc, g):
    S, H = N, 4 * D
    kept = max(1, S // 2) - 1
    node_stats(nc, g, "st1")
    with Stage(nc, "f0") as s:
        wgt = s.sb("wgt", [P, NB])
        chosen = s.sb("chosen", [P, NB])
        gates = s.sb("gates", [P, NB, 2])
        w1 = s.sb("w1", [P, 2, H])
        w2 = s.sb("w2", [P, H // P, D])
        b1 = s.sb("b1", [P, H // P])
        b2 = s.sb("b2", [P, 2, D])
        got, dv = s.sem("got"), s.sem("dv")
        router(nc, g, wgt)
        choose(nc, g, wgt, kept, chosen)
        with s.block() as block:
            @block.sync
            def _(sp):
                sp.dma_start(w1[:], g.ins["L0_ffn_w1"].rearrange("(k p) n -> p k n", p=P)).then_inc(got, 16)
                sp.dma_start(w2[:], g.ins["L0_ffn_w2"].rearrange("(k p) n -> p k n", p=P)).then_inc(got, 16)
                with nc.allow_non_contiguous_dma("biases, one for a lane"):
                    sp.dma_start(b1[:], g.ins["L0_ffn_b1"].rearrange("(k p) -> p k", p=P)).then_inc(got, 16)
                sp.dma_start(b2[:, 0, :], g.ins["L0_ffn_b2"].partition_broadcast(P)).then_inc(got, 16)
                sp.wait_ge(got, 64)

            @block.vector
            def _(v):
                for q in range(2):
                    v.tensor_tensor(gates[:, :, q], wgt[:], chosen[:], ALU.mult).then_inc(dv, 1)
                v.wait_ge(dv, 2)

        mlp(nc, g, s, "mlp0", w1, b1, w2, b2, (True, False), flat(gates, 2), 2, ACT.Gelu_apprx_tanh, True)


MSG = 128
HEADS = 4
OUTC = MSG // HEADS
RAD = 64
GC = 4


def message_weights(nc, g, w, bias, wedge, wback, wout, wskip):
    with Stage(nc, "mw") as s:
        n2m = s.sb("n2m", [P, D])
        four = s.sb("four", [P, 4, P])
        fourt = s.sb("fourt", [P, 4 * P])
        we = s.sb("we", [P, RAD])
        wet = s.sb("wet", [RAD, P])
        ed = s.sb("ed", [RAD, RAD])
        m2n = s.sb("m2n", [P, 2, P])
        beta = s.sb("beta", [P, 3, P])
        pa, pb, pc, pd, pe_ = s.ps("pa"), s.ps("pb"), s.ps("pc"), s.ps("pd"), s.ps("pe")
        pf = s.ps("pf")
        got, turned, copied, made, dve = (s.sem(x) for x in ("got", "turned", "copied", "made", "dve"))
        I = g.ins
        with s.block() as block:
            @block.sync
            def _(sp):
                sp.dma_start(n2m[:], I["L1_gnn_W_n2m"]).then_inc(got, 16)
                for k, n in enumerate(("Wq", "Wk", "Wv", "Wskip")):
                    sp.dma_start(four[:, k, :], I["L1_gnn_" + n]).then_inc(got, 16)
                for k, n in enumerate(("bq", "bk", "bv", "bskip")):
                    sp.dma_start(bias[:, k * P:(k + 1) * P], I["L1_gnn_" + n].partition_broadcast(P)).then_inc(got, 16)
                sp.dma_start(we[:], I["L1_gnn_We"]).then_inc(got, 16)
                sp.dma_start(ed[:], I["L1_gnn_W_edge"]).then_inc(got, 16)
                sp.dma_start(m2n[:], I["L1_gnn_W_m2n"].rearrange("(k p) m -> p k m", p=P)).then_inc(got, 16)
                sp.dma_start(flat(beta, P), I["L1_gnn_Wbeta"].rearrange("o n -> (o n)").partition_broadcast(P)).then_inc(got, 16)
                sp.wait_ge(got, 16 * 13)

            @block.tensor
            def _(pe):
                pe.wait_ge(got, 16 * 13)
                for k in range(4):
                    pe.transpose(pa[:, k * P:(k + 1) * P], four[:, k, :], g.ident[:])
                pe.transpose(pb[0:RAD, 0:P], we[:], g.ident[:])
                for k in range(2):
                    ins = pe.transpose(pc[:, k * P:(k + 1) * P], m2n[:, k, :], g.ident[:])
                ins.then_inc(turned, 1)
                pe.wait_ge(copied, 2)
                pe.matmul(pd[:, :], n2m[:, 0:P], fourt[:], start=True, stop=True)
                pe.matmul(pe_[:, :], n2m[:, P:D], fourt[:], start=True, stop=True)
                pe.matmul(pf[0:RAD, 0:P], ed[:], wet[:], start=True, stop=True).then_inc(made, 1)

            @block.vector
            def _(v):
                ln = Links(v, dve)
                v.wait_ge(turned, 1)
                v.tensor_copy(fourt[:], pa[:]).then_inc(copied, 1)
                v.tensor_copy(wet[:], pb[0:RAD, 0:P]).then_inc(copied, 1)
                ln.mark(v.tensor_copy(wback[:, 0, :], pc[:, 0:D]))
                ln.mark(v.tensor_tensor(wout[:], beta[:, 0, :], beta[:, 2, :], ALU.add))
                ln.mark(v.tensor_tensor(wskip[:], beta[:, 1, :], beta[:, 2, :], ALU.subtract))
                v.wait_ge(made, 1)
                ln.mark(v.tensor_copy(w[:, 0, :], pd[:]))
                ln.mark(v.tensor_copy(w[:, 1, :], pe_[:]))
                ln.mark(v.tensor_copy(wedge[:], pf[0:RAD, 0:P]))
                ln.settle()


def attend_edges(nc, g, s, wedge, reset, qtable, kvtable, dsti, sums, last):
    W = MSG + 2 * HEADS
    turns = C // BC // 2
    groups = [range(k, min(k + GC, BC)) for k in range(0, BC, GC)]
    NG = len(groups)
    ea = [s.sb(f"ea{h}", [P, BC, RAD]) for h in range(2)]
    kv = [s.sb(f"kv{h}", [P, BC, 2, MSG]) for h in range(2)]
    qd = [s.sb(f"qd{h}", [P, BC, MSG]) for h in range(2)]
    ob = [s.sb(f"ob{h}", [P, BC, W]) for h in range(2)]
    ix = [s.sb(f"ix{h}", [P, 2, BC], U32) for h in range(2)]
    eat = [s.sb(f"eat{h}", [RAD, GC * P]) for h in range(2)]
    sc = s.sb("sc", [P, HEADS, BC])
    mb = [s.sb(f"mb{h}", [P, HEADS, BC + 1]) for h in range(2)]
    wd = [s.sb(f"wd{h}", [P, 2, HEADS, BC]) for h in range(2)]
    pt = [s.ps(f"pt{h}") for h in range(2)]
    pe_ = [s.ps(f"pe{h}") for h in range(2)]
    scored, weighed, done, ea_used = (s.sems(x) for x in ("scored", "weighed", "done", "ea_used"))
    ea_got, stored = (s.sems(x) for x in ("ea_got", "stored"))
    got = [s.gather_sem(f"got{h}") for h in range(2)]
    turned, copied, e_ready, e_read = (s.sem(x) for x in ("turned", "copied", "e_ready", "e_read"))
    dve, ixd, passed, lastd = s.sem("dve"), s.sem("ixd"), s.sem("passed"), s.sem("lastd")
    pe_passed = s.sem("pe_passed")
    rows = g.edge64.rearrange("(p c) d -> p c d", p=P)
    out = sums.rearrange("(p c) w -> p c w", p=P)
    with s.block() as block:
        @block.sync
        def _(sp):
            def load(h, turn, c0):
                sp.wait_ge(ea_used[h], turn + 1)
                sp.dma_start(ea[h][:], rows[:, bass.ds(c0, BC), :]).then_inc(ea_got[h], 16)

            def store(h, turn, c0):
                sp.wait_ge(done[h], turn + 2)
                sp.dma_start(out[:, bass.ds(c0, BC), :], ob[h][:]).then_inc(stored[h], 16)

            for h in range(2):
                sp.sem_inc(stored[h], 16)
            load(0, 0, 0)
            with sp.Fori(0, turns - 1) as i:
                load(1, i, (i * 2 + 1) * BC)
                store(0, i, i * 2 * BC)
                load(0, i + 1, (i * 2 + 2) * BC)
                store(1, i, (i * 2 + 1) * BC)
            load(1, turns - 1, (turns * 2 - 1) * BC)
            for h in range(2):
                store(h, turns - 1, (turns * 2 - 2 + h) * BC)
            for h in range(2):
                sp.wait_ge(stored[h], 16 * (turns + 1))

        @block.gpsimd
        def _(pool):
            with pool.Fori(0, turns) as i:
                for h in range(2):
                    cols = bass.ds((i * 2 + h) * BC, BC)
                    gate(pool, done[h], i + 1, passed)
                    pool.tensor_copy(ix[h][:, 0, :], g.src[:, cols]).then_inc(ixd, 1)
                    pool.tensor_copy(ix[h][:, 1, :], dsti[:, cols]).then_inc(ixd, 1)
                    gate(pool, ixd, i * 4 + 2 * h + 2, passed)
                    for k in range(BC):
                        pool.indirect_dma_start(kv[h][:, k, :, :].rearrange("p a b -> p (a b)"), None, kvtable,
                                                bass.IndirectOffsetOnAxis(ap=ix[h][:, 0, k:k + 1], axis=0)).then_inc(got[h], 16)
                        pool.indirect_dma_start(qd[h][:, k, :], None, qtable,
                                                bass.IndirectOffsetOnAxis(ap=ix[h][:, 1, k:k + 1], axis=0)).then_inc(got[h], 16)
            for h in range(2):
                pool.wait_ge(got[h], 32 * BC * turns)

        @block.tensor
        def _(pe):
            pe.sem_inc(e_ready, 2)
            for h in range(2):
                pe.sem_inc(ea_used[h], 1)
            with pe.Fori(0, turns) as i:
                for h in range(2):
                    pe.wait_ge(ea_got[h], (i + 1) * 16)
                    for gi, cols in enumerate(groups):
                        n = h * NG + gi
                        gate(pe, copied, i * (2 * NG) + (n + 1), pe_passed)
                        for z, k in enumerate(cols):
                            ins = pe.transpose(pt[n % 2][0:RAD, z * P:(z + 1) * P], ea[h][:, k, :], g.ident[:])
                        ins.then_inc(turned, 1)
                        pe.wait_ge(copied, i * (2 * NG) + (n + 3))
                        pe.wait_ge(e_read, i * (2 * NG) + (n + 1))
                        for z, k in enumerate(cols):
                            ins = pe.matmul(pe_[n % 2][:, z * P:(z + 1) * P], eat[n % 2][:, z * P:(z + 1) * P], wedge[:],
                                            start=True, stop=True)
                        ins.then_inc(e_ready, 1)
                    pe.sem_inc(ea_used[h], 1)

        @block.scalar
        def _(act):
            act.sem_inc(copied, 2)
            for h in range(2):
                act.sem_inc(weighed[h], 1)
            with act.Fori(0, turns) as i:
                for h in range(2):
                    for gi, cols in enumerate(groups):
                        n = h * NG + gi
                        wide = len(cols) * P
                        act.wait_ge(turned, i * (2 * NG) + (n + 1))
                        act.wait_ge(e_ready, i * (2 * NG) + (n + 1))
                        act.activation(eat[n % 2][:, 0:wide], pt[n % 2][0:RAD, 0:wide], ACT.Copy).then_inc(copied, 1)
                    act.wait_ge(scored[h], i + 2)
                    both = wd[h][:].rearrange("p a h c -> p (a h c)")
                    act.activation(both, both, ACT.Exp).then_inc(weighed[h], 1)

        @block.vector
        def _(v):
            ln = Links(v, dve)
            v.sem_inc(e_read, 2)
            for h in range(2):
                v.sem_inc(scored[h], 1)
                v.sem_inc(done[h], 1)
            ln.mark(v.memset(mb[1][:], 0.0))
            ln.link(v.memset(ob[1][:, BC - 1, :], 0.0))
            with v.Fori(0, turns) as i:
                ln.enter(i, 2 * (6 + 4 * HEADS + 2 * BC - 1))
                for h in range(2):
                    cs = bass.ds((i * 2 + h) * BC, BC)
                    v.wait_ge(got[h], (i + 1) * (32 * BC))
                    for gi, cols in enumerate(groups):
                        n = h * NG + gi
                        nc_ = len(cols)
                        part = kv[h][:, cols[0]:cols[0] + nc_, :, :]
                        e = pe_[n % 2][:, 0:nc_ * P].rearrange("p (c o m) -> p c o m", o=1, m=P).to_broadcast([P, nc_, 2, P])
                        v.wait_ge(e_ready, i * (2 * NG) + (n + 3))
                        v.tensor_tensor(part, part, e, ALU.add).then_inc(e_read, 1)
                    v.wait_ge(e_read, i * (2 * NG) + (2 + (h + 1) * NG))
                    ln.link(v.tensor_tensor(qd[h][:], qd[h][:], kv[h][:, :, 0, :], ALU.mult))
                    ln.mark(v.tensor_reduce(sc[:].rearrange("p h c -> p c h"), qd[h][:].rearrange("p c (h d) -> p c h d", h=HEADS),
                                            AX.X, ALU.add))
                    ln.link(v.tensor_copy(mb[h][:, :, 0:1], mb[1 - h][:, :, BC:BC + 1]))
                    for a in range(HEADS):
                        ln.mark(v.tensor_tensor_scan(mb[h][:, a, 1:BC + 1], reset[:, cs], sc[:, a, :], mb[h][:, a, 0:1],
                                                     ALU.add, ALU.max))
                    ln.settle()
                    v.wait_ge(weighed[h], i + 1)
                    ln.link(v.tensor_tensor(wd[h][:, 0, :, :], mb[h][:, :, 0:BC], mb[h][:, :, 1:BC + 1], ALU.subtract))
                    for a in range(HEADS):
                        ln.mark(v.tensor_tensor(wd[h][:, 0, a, :], wd[h][:, 0, a, :], reset[:, cs], ALU.add))
                    ln.link(v.tensor_tensor(wd[h][:, 1, :, :], sc[:], mb[h][:, :, 1:BC + 1], ALU.subtract))
                    v.sem_inc(scored[h], 1)
                    v.wait_ge(stored[h], (i + 1) * 16)
                    ln.mark(v.tensor_copy(ob[h][:, :, MSG + HEADS:].rearrange("p c h -> p h c"), mb[h][:, :, 1:BC + 1]))
                    v.wait_ge(weighed[h], i + 2)
                    v.wait_ge(done[1 - h], i + 1 + h)
                    ln.settle()
                    before = ob[1 - h][:, BC - 1, :]
                    for a in range(HEADS):
                        ln.mark(v.tensor_tensor_scan(ob[h][:, :, MSG + a], wd[h][:, 0, a, :], wd[h][:, 1, a, :],
                                                     before[:, MSG + a:MSG + a + 1], ALU.mult, ALU.add))
                    for a in range(HEADS):
                        vv = kv[h][:, :, 1, a * OUTC:(a + 1) * OUTC]
                        ln.mark(v.tensor_tensor(vv, vv, wd[h][:, 1, a, :].rearrange("p (c o) -> p c o", o=1)
                                                .to_broadcast([P, BC, OUTC]), ALU.mult))
                    ln.settle()
                    for k in range(BC):
                        decay = wd[h][:, 0, :, k:k + 1].to_broadcast([P, HEADS, OUTC])
                        to = ob[h][:, k, 0:MSG]
                        ln.link(v.tensor_tensor(to.rearrange("p (h d) -> p h d", h=HEADS),
                                                before[:, 0:MSG].rearrange("p (h d) -> p h d", h=HEADS), decay, ALU.mult))
                        ins = v.tensor_tensor(to, to, kv[h][:, k, 1, :], ALU.add)
                        before = ob[h][:, k, :]
                        if k < BC - 1:
                            ln.link(ins)
                        else:
                            ins.then_inc(done[h], 1)
                ln.leave(turns)
            v.wait_ge(done[1], turns + 1)
            v.tensor_copy(last[:], ob[1][:, BC - 1, :]).then_inc(lastd, 1)
            v.wait_ge(lastd, 1)


def l1_gnn(nc, g):
    W = MSG + 2 * HEADS
    scale = float(1.0 / np.sqrt(np.float32(OUTC)))
    qtable = nc.dram_tensor("qtable", (NP, MSG), F32, kind="Internal").ap()
    kvtable = nc.dram_tensor("kvtable", (NP, 2 * MSG), F32, kind="Internal").ap()
    sums = nc.dram_tensor("msg_sums", (P * C, W), F32, kind="Internal").ap()
    if l0_gnn not in STAGES:
        segments(nc, g, "seg", g.dstf, C, E, g.start, g.end, g.keys)
    node_stats(nc, g, "st2")
    with Stage(nc, "g1") as s:
        last = s.sb("last", [P, W])
        wback = s.sb("wback", [P, 1, D])
        wedge = s.sb("wedge", [RAD, P])
        wout = s.sb("wout", [P, MSG])
        wskip = s.sb("wskip", [P, MSG])
        xr = s.sb("xr", [P, NB, MSG])
        with Stage(nc, "g1p") as s1:
            w = s1.sb("w", [P, 2, 4 * MSG])
            bias = s1.sb("bias", [P, 4 * MSG])
            message_weights(nc, g, w, bias, wedge, wback, wout, wskip)

            def rows4(v, ln, h, b, rows, xn, po, out):
                ln.mark(v.tensor_tensor(flat(xr, MSG)[:, bass.ds(b * MSG, MSG)], po[:, 3 * MSG:], bias[:, 3 * MSG:], ALU.add))
                ln.link(v.tensor_tensor(out[:], po[:, 0:3 * MSG], bias[:, 0:3 * MSG], ALU.add))
                return v.tensor_scalar(out[:, 0:MSG], out[:, 0:MSG], scale, None, ALU.mult)

            project(nc, g, "qkv", w, 4 * MSG, 3 * MSG, rows4, 2, [(qtable, 0, MSG), (kvtable, MSG, 3 * MSG)])
        with Stage(nc, "g1e") as s1:
            keep = s1.sb("keep", [P, C])
            reset = s1.sb("reset", [P, C])
            dsti = s1.sb("dsti", [P, C], U32)
            dv = s1.sem("dv")
            boundaries(nc, g, "bnd1", g.dstf, C, reset, keep)
            with s1.block() as block:
                @block.vector
                def _(v):
                    ln = Links(v, dv)
                    ln.link(v.tensor_scalar(keep[:], g.dstf[:], float(NP - 1), None, ALU.min))
                    ln.link(v.tensor_copy(dsti[:], keep[:]))
            attend_edges(nc, g, s1, wedge, reset, qtable, kvtable, dsti, sums, last)
        carry_in(nc, g, "car1", g.dstf, C, last, MSG, HEADS, sums)
        rows = s.sb("rows", [P, NB, W])
        with Stage(nc, "g1f") as s1:
            gather_ends(nc, g, "end1", s1, g.end, sums, rows)
            merge(nc, g, s1, MSG, HEADS, rows, eps=1e-16)
            some = s1.sb("some", [P, NB])
            beta = s1.sb("beta", [P, 2, NB])
            dv, logit, exped = s1.sem("bdv"), s1.sem("logit"), s1.sem("exped")
            tmp = s1.sb("tmp", [P, NB, MSG])[:]
            o = rows[:, :, 0:MSG]

            def wide(t):
                return t.rearrange("p (b o) -> p b o", o=1).to_broadcast([P, NB, MSG])

            def tall(t):
                return t[:].rearrange("p (o m) -> p o m", o=1).to_broadcast([P, NB, MSG])

            with s1.block() as block:
                @block.vector
                def _(v):
                    ln = Links(v, dv)
                    ln.link(v.tensor_tensor(some[:], g.end[:], g.start[:], ALU.is_gt))
                    ln.link(v.tensor_tensor(o, o, wide(some[:]), ALU.mult))
                    ln.link(v.tensor_tensor(tmp, o, tall(wout), ALU.mult))
                    ln.link(v.tensor_reduce(beta[:, 0, :], tmp, AX.X, ALU.add))
                    ln.link(v.tensor_tensor(tmp, xr[:], tall(wskip), ALU.mult))
                    ln.link(v.tensor_reduce(beta[:, 1, :], tmp, AX.X, ALU.add))
                    v.tensor_tensor(beta[:, 0, :], beta[:, 0, :], beta[:, 1, :], ALU.add).then_inc(logit, 1)
                    v.wait_ge(exped, 1)
                    ln.link(v.tensor_scalar(beta[:, 0, :], beta[:, 0, :], 1.0, None, ALU.add))
                    ln.link(v.reciprocal(beta[:, 0, :], beta[:, 0, :]))
                    ln.link(v.tensor_scalar(beta[:, 1, :], beta[:, 0, :], -1.0, 1.0, ALU.mult, ALU.add))
                    ln.mark(v.tensor_tensor(xr[:], xr[:], wide(beta[:, 0, :]), ALU.mult))
                    ln.link(v.tensor_tensor(o, o, wide(beta[:, 1, :]), ALU.mult))
                    ln.link(v.tensor_tensor(xr[:], xr[:], o, ALU.add))

                @block.scalar
                def _(act):
                    act.wait_ge(logit, 1)
                    act.activation(beta[:, 0, :], beta[:, 0, :], ACT.Exp, scale=-1.0).then_inc(exped, 1)

        def mixed(v, b, to):
            return v.tensor_scalar(to[:, 0:MSG], flat(xr, MSG)[:, bass.ds(b * MSG, MSG)], 0.0, None, ALU.add)

        def add(v, ln, h, b, rows_x, xn, po, out):
            return v.tensor_tensor(rows_x, rows_x, po[:, 0:D], ALU.add)

        project(nc, g, "back", wback, D, 0, add, 0, prepare=mixed, depth=1)


EXPERTS = 4
GH = 4
ID_BITS = 13
BC2 = 32


def sort_edges(nc, g, dstf, src):
    bits_j, bits = C2.bit_length() - 1, E2.bit_length() - 1
    chunks = C2 // P
    with Stage(nc, "so") as s:
        ends = s.sb("ends", [P, 2, C2], I32)
        buf = [s.sb(f"buf{k}", [P, C2]) for k in range(2)]
        lane = s.sb("lane", [P, 1], I32)
        bit = s.sb("bit", [P, 1], I32)
        signs = s.sb("signs", [P, bits - bits_j])
        flips = s.sb("flips", [P, bits - bits_j])
        pt = s.ps("pt", [P, C2])
        got, made, ready, turned, dve = (s.sem(x) for x in ("got", "made", "ready", "turned", "dve"))
        trips = [b for k in range(bits_j + 1, bits + 1) for b in range(2)]
        source = []
        with s.block() as block:
            @block.sync
            def _(sp):
                sp.dma_start(ends[:], g.ins["L1_ffn_edge_index"].rearrange("z (p c) -> p z c", p=P)).then_inc(got, 16)
                sp.wait_ge(got, 16)

            @block.gpsimd
            def _(pool):
                pool.iota(lane[:], [[0, 1]], base=0, channel_multiplier=1).then_inc(made, 1)

            @block.vector
            def _(v):
                ln = Links(v, dve)
                v.wait_ge(made, 1)
                for k in range(bits - bits_j):
                    ln.link(v.tensor_scalar(bit[:], lane[:], k, 1, ALU.logical_shift_right, ALU.bitwise_and))
                    ln.link(v.tensor_copy(signs[:, k:k + 1], bit[:]))
                ln.link(v.tensor_scalar(signs[:], signs[:], -2.0, 1.0, ALU.mult, ALU.add))
                ln.mark(v.tensor_copy(flips[:, 0:1], signs[:, 0:1]))
                ln.mark(v.tensor_tensor(flips[:, 1:], signs[:, 1:], signs[:, 0:-1], ALU.mult))
                v.wait_ge(got, 16)
                ln.link(v.tensor_scalar(ends[:, 0, :], ends[:, 0, :], float(N - 1), None, ALU.min))
                ln.link(v.tensor_scalar(ends[:, 1, :], ends[:, 1, :], float(2 ** ID_BITS - 1), None, ALU.min))
                ln.link(v.tensor_scalar(ends[:, 1, :], ends[:, 1, :], ID_BITS, 1 << 28,
                                        ALU.logical_shift_left, ALU.bitwise_or))
                at = 0
                ln.link(v.tensor_tensor(buf[at][:].bitcast(I32), ends[:, 1, :], ends[:, 0, :], ALU.bitwise_or))
                trip = 0

                def compare(lo, hi, to_lo, to_hi, up):
                    ln.mark(v.tensor_tensor(to_lo, lo, hi, ALU.min if up else ALU.max))
                    ln.mark(v.tensor_tensor(to_hi, lo, hi, ALU.max if up else ALU.min))

                def stage(src_, dst_, stride):
                    a, b = (t.rearrange("p (m z i) -> p m z i", z=2, i=stride) for t in (src_, dst_))
                    compare(a[:, :, 0, :], a[:, :, 1, :], b[:, :, 0, :], b[:, :, 1, :], True)
                    ln.settle()

                for k in range(1, bits + 1):
                    if k >= bits_j:
                        j = k - bits_j
                        factor = flips[:, j:j + 1] if k < bits else signs[:, j - 1:j]
                        ln.link(v.tensor_scalar(buf[1 - at][:], buf[at][:], factor, None, ALU.mult))
                        at = 1 - at
                    if k > bits_j:
                        v.sem_inc(ready, 1)
                        source.append(at)
                        trip += 1
                        v.wait_ge(turned, trip)
                        ln.link(v.tensor_copy(buf[1 - at][:], pt[:]))
                        at = 1 - at
                        frm = buf[at][:]
                        for b in range(k - bits_j - 1, -1, -1):
                            stage(frm, buf[1 - at][:], 2 ** b)
                            at = 1 - at
                            frm = buf[at][:]
                        v.sem_inc(ready, 1)
                        source.append(at)
                        trip += 1
                        v.wait_ge(turned, trip)
                        ln.link(v.tensor_copy(buf[1 - at][:], pt[:]))
                        at = 1 - at
                        frm = buf[at][:]
                    else:
                        frm = buf[at][:]
                    for b in range(min(k, bits_j) - 1, -1, -1):
                        if k < bits_j:
                            w = [t.rearrange("p (o d m z i) -> p o d m z i", d=2, m=2 ** (k - 1 - b), z=2, i=2 ** b)
                                 for t in (frm, buf[1 - at][:])]
                            for d in range(2):
                                compare(w[0][:, :, d, :, 0, :], w[0][:, :, d, :, 1, :],
                                        w[1][:, :, d, :, 0, :], w[1][:, :, d, :, 1, :], d == 0)
                            ln.settle()
                        else:
                            stage(frm, buf[1 - at][:], 2 ** b)
                        at = 1 - at
                        frm = buf[at][:]
                keys = buf[at][:].bitcast(I32)
                ln.mark(v.tensor_scalar(ends[:, 0, :], keys, 2 ** ID_BITS - 1, None, ALU.bitwise_and))
                ln.mark(v.tensor_scalar(ends[:, 1, :], keys, ID_BITS, 2 ** ID_BITS - 1,
                                        ALU.logical_shift_right, ALU.bitwise_and))
                ln.settle()
                ln.mark(v.tensor_copy(src[:], ends[:, 0, :]))
                ln.mark(v.tensor_copy(dstf[:], ends[:, 1, :]))
                ln.settle()

            @block.tensor
            def _(pe):
                for trip, at in enumerate(source):
                    pe.wait_ge(ready, trip + 1)
                    for c in range(chunks):
                        ins = pe.transpose(pt[:, c * P:(c + 1) * P], buf[at][:, c * P:(c + 1) * P], g.ident[:])
                    ins.then_inc(turned, 1)


def route_and_hide(nc, g, s, table, adst, reset, src, sums, last, w1, b1, w2, b2, loaded, outputs):
    F = GH * EXPERTS
    W, T = F + 2 * GH, F + GH
    steps = C2 // BC2
    turns = NB // SUPER
    assert steps == 2 + 3 * turns
    width = SUPER * P
    hw = width // 2
    uses = 2 * HC
    HU, YU = uses * EXPERTS, SUPER * EXPERTS
    ge = [s.sb(f"ge{k}", [P, BC2, T]) for k in range(3)]
    ob = [s.sb(f"ob{k}", [P, BC2, W]) for k in range(3)]
    ix = [s.sb(f"ix{k}", [P, BC2], U32) for k in range(3)]
    mb = [s.sb(f"mb{k}", [P, GH, BC2 + 1]) for k in range(3)]
    sc = s.sb("sc", [P, GH, BC2])
    lk = s.sb("lk", [P, GH, BC2])
    wd = s.sb("wd", [P, 2, GH, BC2])
    xn = s.sb("xn", [P, SUPER, D])
    xt = s.sb("xt", [P, 2, width])
    ht = [s.sb(f"ht{k}", [P, HC, width]) for k in range(2)]
    yb = [s.sb(f"yb{k}", [P, SUPER, D]) for k in range(2)]
    pt = [s.ps(f"pt{k}") for k in range(2)]
    ph = [s.ps(f"ph{k}") for k in range(4)]
    py = [s.ps(f"py{k}") for k in range(2)]
    scored, weighed, done, ixd, passed, lastd = (s.sem(x) for x in ("scored", "weighed", "done", "ixd", "passed", "lastd"))
    got, stored = [s.gather_sem(f"got{k}") for k in range(3)], s.sems("stored", 3)
    normed, turned, copied, hidden, acted, out_ready, out_read, dve = (s.sem(x) for x in (
        "normed", "turned", "copied", "hidden", "acted", "out_ready", "out_read", "dve"))
    y_stored = s.sems("y_stored")
    out = sums.rearrange("(p c) w -> p c w", p=P)
    with s.block() as block:
        @block.gpsimd
        def _(pool):
            def gather(i, t0):
                t, k = i * 3 + t0, t0 % 3
                gate(pool, done, t + 1, passed)
                pool.tensor_copy(ix[k][:], src[:, bass.ds(t * BC2, BC2)]).then_inc(ixd, 1)
                gate(pool, ixd, t + 1, passed)
                for c in range(BC2):
                    pool.indirect_dma_start(ge[k][:, c, :], None, table,
                                            bass.IndirectOffsetOnAxis(ap=ix[k][:, c:c + 1], axis=0)).then_inc(got[k], 16)

            gather(0, 0)
            gather(0, 1)
            with pool.Fori(0, turns) as i:
                for t0 in (2, 3, 4):
                    gather(i, t0)
            for k in range(3):
                pool.wait_ge(got[k], 16 * BC2 * ((steps - k + 2) // 3))

        @block.sync
        def _(sp):
            def store(i, t0):
                t, k = i * 3 + t0, t0 % 3
                sp.wait_ge(done, t + 4)
                sp.dma_start(out[:, bass.ds(t * BC2, BC2), :], ob[k][:]).then_inc(stored[k], 16)

            def store_outputs(i, q):
                sp.wait_ge(out_read, i * YU + ((q + 1) * SUPER + 2))
                sp.dma_start(outputs[bass.ds((i * EXPERTS + q) * P, P), :], flat(yb[q % 2], D)).then_inc(y_stored[q % 2], 16)

            for k in range(3):
                sp.sem_inc(stored[k], 16)
            for z in range(2):
                sp.sem_inc(y_stored[z], 16)
            store(0, 0)
            store(0, 1)
            with sp.Fori(0, turns) as i:
                for q in range(EXPERTS):
                    store_outputs(i, q)
                    if q < 3:
                        store(i, q + 2)
            for k in range(3):
                sp.wait_ge(stored[k], 16 * ((steps - k + 2) // 3 + 1))
            for z in range(2):
                sp.wait_ge(y_stored[z], 16 * (2 * turns + 1))

        @block.vector
        def _(v):
            ln = Links(v, dve)
            v.sem_inc(out_read, 2)
            v.sem_inc(done, 3)

            def norm(i):
                for j in range(SUPER):
                    b = i * SUPER + j
                    rows = flat(g.x, D)[:, bass.ds(b * D, D)]
                    ins = v.tensor_scalar(xn[:, j, :], rows, g.mean[:, bass.ds(b, 1)], g.rstd[:, bass.ds(b, 1)],
                                          ALU.subtract, ALU.mult)
                ins.then_inc(normed, 1)

            def add_bias(i, q):
                v.wait_ge(y_stored[q % 2], (i * 2 + (q // 2 + 1)) * 16)
                for j in range(SUPER):
                    n = q * SUPER + j
                    v.wait_ge(out_ready, i * YU + (10 + n + 1))
                    v.tensor_tensor(yb[q % 2][:, j, :], py[n % 2][:, 0:D], b2[:, q, :], ALU.add).then_inc(out_read, 1)

            def step(i, t0):
                t, k, use = i * 3 + t0, t0 % 3, i + t0 // 3
                last_k = (t0 + 2) % 3
                cs = bass.ds(t * BC2, BC2)
                v.wait_ge(got[k], (use + 1) * (16 * BC2))
                ln.link(v.tensor_tensor(sc[:].rearrange("p h c -> p c h"), ge[k][:, :, F:T], adst[:, cs, :], ALU.add))
                ln.mark(v.tensor_copy(mb[k][:, :, 0:1], mb[last_k][:, :, BC2:BC2 + 1]))
                ln.link(v.scalar_tensor_tensor(out=lk[:], in0=sc[:], scalar=0.2, in1=sc[:], op0=ALU.mult, op1=ALU.max))
                for a in range(GH):
                    ln.mark(v.tensor_tensor_scan(mb[k][:, a, 1:BC2 + 1], reset[:, cs], lk[:, a, :], mb[k][:, a, 0:1],
                                                 ALU.add, ALU.max))
                ln.settle()
                ln.mark(v.tensor_tensor(wd[:, 1, :, :], lk[:], mb[k][:, :, 1:BC2 + 1], ALU.subtract))
                ln.link(v.tensor_tensor(wd[:, 0, :, :], mb[k][:, :, 0:BC2], mb[k][:, :, 1:BC2 + 1], ALU.subtract))
                for a in range(GH):
                    ins = v.tensor_tensor(wd[:, 0, a, :], wd[:, 0, a, :], reset[:, cs], ALU.add)
                ins.then_inc(scored, 1)
                v.wait_ge(stored[k], (use + 1) * 16)
                ln.mark(v.tensor_copy(ob[k][:, :, F + GH:].rearrange("p c h -> p h c"), mb[k][:, :, 1:BC2 + 1]))
                v.wait_ge(weighed, t + 1)
                v.wait_ge(done, t + 3)
                ln.settle()
                before = ob[last_k][:, BC2 - 1, :]
                for a in range(GH):
                    ln.mark(v.tensor_tensor_scan(ob[k][:, :, F + a], wd[:, 0, a, :], wd[:, 1, a, :],
                                                 before[:, F + a:F + a + 1], ALU.mult, ALU.add))
                for a in range(GH):
                    vv = ge[k][:, :, a * EXPERTS:(a + 1) * EXPERTS]
                    ln.mark(v.tensor_tensor(vv, vv, wd[:, 1, a, :].rearrange("p (c o) -> p c o", o=1)
                                            .to_broadcast([P, BC2, EXPERTS]), ALU.mult))
                ln.settle()
                for f in range(F):
                    ins = v.tensor_tensor_scan(ob[k][:, :, f], wd[:, 0, f // EXPERTS, :], ge[k][:, :, f],
                                               before[:, f:f + 1], ALU.mult, ALU.add)
                ins.then_inc(done, 1)

            def turn(i, more):
                if more:
                    v.wait_ge(turned, i * SUPER + SUPER)
                    norm(i + 1)
                for q in range(EXPERTS):
                    add_bias(i, q)
                    if q < 3:
                        step(i, q + 2)

            ln.mark(v.memset(mb[2][:], 0.0))
            ln.link(v.memset(ob[2][:, BC2 - 1, :], 0.0))
            norm(0)
            step(0, 0)
            step(0, 1)
            with v.Fori(0, turns - 1) as i:
                ln.enter(i, 3 * (6 + 3 * GH))
                turn(i, True)
                ln.leave(turns - 1)
            turn(turns - 1, False)
            v.wait_ge(done, steps + 3)
            v.tensor_copy(last[:], ob[(steps - 1) % 3][:, BC2 - 1, :]).then_inc(lastd, 1)
            v.wait_ge(lastd, 1)

        @block.tensor
        def _(pe):
            pe.sem_inc(out_ready, 10)
            pe.wait_ge(loaded, 16 * (3 * EXPERTS + 1))

            def turn(i, first=False):
                pe.wait_ge(normed, i + 1)
                for j in range(SUPER):
                    if j >= 2:
                        pe.wait_ge(copied, i * SUPER + (j - 1))
                    elif not first:
                        pe.wait_ge(copied, i * SUPER)
                    pe.transpose(pt[j % 2][:, 0:P], xn[:, j, 0:P], g.ident[:])
                    pe.transpose(pt[j % 2][:, P:D], xn[:, j, P:D], g.ident[:]).then_inc(turned, 1)

            def hide(i, q):
                if q == 0:
                    pe.wait_ge(copied, i * SUPER + SUPER)
                for c in range(HC):
                    for z in range(2):
                        u = q * uses + 2 * c + z
                        ch = q * HC + c
                        pe.wait_ge(acted, i * HU + (u + 1))
                        for k in range(2):
                            ins = pe.matmul(ph[u % 4][:, 0:hw], w1[:, k, ch * P:(ch + 1) * P],
                                            xt[:, k, z * hw:(z + 1) * hw], start=(k == 0), stop=(k == 1))
                        ins.then_inc(hidden, 1)

            def down(i, q):
                pe.wait_ge(acted, i * HU + ((q + 1) * uses + 4))
                for j in range(SUPER):
                    n = q * SUPER + j
                    pe.wait_ge(out_read, i * YU + (n + 1))
                    for c in range(HC):
                        ins = pe.matmul(py[n % 2][:, 0:D], ht[q % 2][:, c, j * P:(j + 1) * P], w2[:, q * HC + c, :],
                                        start=(c == 0), stop=(c == HC - 1))
                    ins.then_inc(out_ready, 1)

            def body(i, more):
                for q in range(EXPERTS):
                    hide(i, q)
                    if q:
                        down(i, q - 1)
                if more:
                    turn(i + 1)
                down(i, EXPERTS - 1)

            turn(0, True)
            with pe.Fori(0, turns - 1) as i:
                body(i, True)
            body(turns - 1, False)

        @block.scalar
        def _(act):
            act.sem_inc(acted, 4)

            def copy(i):
                for j in range(SUPER):
                    act.wait_ge(turned, i * SUPER + (j + 1))
                    act.activation(xt[:, :, j * P:(j + 1) * P], pt[j % 2][:, 0:D].rearrange("p (k n) -> p k n", k=2),
                                   ACT.Copy).then_inc(copied, 1)

            def hide(i, q):
                act.wait_ge(out_ready, i * YU + (q * SUPER + 5))
                for c in range(HC):
                    for z in range(2):
                        u = q * uses + 2 * c + z
                        act.wait_ge(hidden, i * HU + (u + 1))
                        act.activation(ht[q % 2][:, c, z * hw:(z + 1) * hw], ph[u % 4][:, 0:hw], ACT.Gelu,
                                       bias=b1[:, q * HC + c:q * HC + c + 1]).then_inc(acted, 1)

            def weigh(i, t0):
                act.wait_ge(scored, i * 3 + (t0 + 1))
                both = wd[:].rearrange("p a h c -> p (a h c)")
                act.activation(both, both, ACT.Exp).then_inc(weighed, 1)

            def turn(i):
                for q in range(EXPERTS):
                    hide(i, q)
                    if q:
                        weigh(i, q + 1)

            weigh(0, 0)
            weigh(0, 1)
            copy(0)
            with act.Fori(0, turns - 1) as i:
                turn(i)
                copy(i + 1)
            turn(turns - 1)


def combine(nc, g, gates, outputs):
    turns = NB // SUPER
    with Stage(nc, "cb") as s:
        y = [s.sb(f"y{h}", [P, EXPERTS, SUPER * D]) for h in range(2)]
        loaded, used, dve = s.sems("loaded"), s.sems("used"), s.sem("dve")
        with s.block() as block:
            @block.sync
            def _(sp):
                with sp.Fori(0, turns // 2) as i:
                    for h in range(2):
                        sp.wait_ge(used[h], i + 1)
                        sp.dma_start(y[h][:], outputs[bass.ds((i * 2 + h) * (EXPERTS * P), EXPERTS * P), :]
                                     .rearrange("(q p) w -> p q w", p=P)).then_inc(loaded[h], 16)

            @block.vector
            def _(v):
                ln = Links(v, dve)
                for h in range(2):
                    v.sem_inc(used[h], 1)
                with v.Fori(0, turns // 2) as i:
                    ln.enter(i, 2 * EXPERTS * SUPER)
                    for h in range(2):
                        v.wait_ge(loaded[h], (i + 1) * 16)
                        for q in range(EXPERTS):
                            for j in range(SUPER):
                                b = (i * 2 + h) * SUPER + j
                                rows = flat(g.x, D)[:, bass.ds(b * D, D)]
                                ln.mark(v.scalar_tensor_tensor(out=rows, in0=y[h][:, q, j * D:(j + 1) * D],
                                                               scalar=gates[:, bass.ds(b * EXPERTS + q, 1)], in1=rows,
                                                               op0=ALU.mult, op1=ALU.add))
                            ln.settle()
                        v.sem_inc(used[h], 1)
                    ln.leave(turns // 2)


def routing_weights(nc, g, w):
    F = GH * EXPERTS
    with Stage(nc, "rw") as s:
        att = s.sb("att", [P, 2, F])
        tmp = s.sb("tmp", [P, 2, 2, F])
        got, dve = s.sem("got"), s.sem("dve")
        with s.block() as block:
            @block.sync
            def _(sp):
                sp.dma_start(w[:, :, 0:F], g.ins["L1_ffn_W_gat"].rearrange("(k p) n -> p k n", p=P)).then_inc(got, 16)
                for z, n in enumerate(("att_src", "att_dst")):
                    sp.dma_start(att[:, z, :], g.ins["L1_ffn_" + n].rearrange("h e -> (h e)").partition_broadcast(P)).then_inc(got, 16)
                sp.wait_ge(got, 48)

            @block.vector
            def _(v):
                ln = Links(v, dve)
                v.wait_ge(got, 48)
                for k in range(2):
                    for z in range(2):
                        ln.mark(v.tensor_tensor(tmp[:, k, z, :], w[:, k, 0:F], att[:, z, :], ALU.mult))
                ln.settle()
                for k in range(2):
                    ln.mark(v.tensor_reduce(w[:, k, F:F + 2 * GH].rearrange("p (z h) -> p z h", z=2),
                                            tmp[:, k, :, :].rearrange("p z (h e) -> p z h e", h=GH), AX.X, ALU.add))
                ln.settle()


def expert_gates(nc, g, s, rows, gates):
    F = GH * EXPERTS
    W = F + 2 * GH
    par = s.sb("par", [P, 3, F])
    c = s.sb("c", [P, NB, F])
    sq = s.sb("sq", [P, NB, F])
    m = s.sb("m", [P, NB])
    r = s.sb("r", [P, NB])
    sc = s.sb("sc", [P, NB, EXPERTS])
    better = s.sb("better", [P, NB, EXPERTS])
    cmp_ = s.sb("cmp", [P, NB])
    got, rooted, exped, std, ex, dve = (s.sem(x) for x in ("egot", "rooted", "exped", "estd", "eex", "edve"))

    def wide(t, n):
        return t.rearrange("p (b o) -> p b o", o=1).to_broadcast([P, NB, n])

    def tall(t):
        return t.rearrange("p (o m) -> p o m", o=1).to_broadcast([P, NB, F])

    with s.block() as block:
        @block.sync
        def _(sp):
            for z, n in enumerate(("b_gat", "ln_gamma", "ln_beta")):
                sp.dma_start(par[:, z, :], g.ins["L1_ffn_" + n].partition_broadcast(P)).then_inc(got, 16)
            sp.wait_ge(got, 48)

        @block.vector
        def _(v):
            ln = Links(v, dve)
            v.wait_ge(got, 48)
            ln.link(v.tensor_tensor(c[:], rows[:, :, 0:F], tall(par[:, 0, :]), ALU.add))
            ln.link(v.tensor_reduce(m[:], c[:], AX.X, ALU.add))
            ln.link(v.tensor_scalar(m[:], m[:], 1.0 / F, None, ALU.mult))
            ln.link(v.tensor_tensor(c[:], c[:], wide(m[:], F), ALU.subtract))
            ln.link(v.tensor_tensor(sq[:], c[:], c[:], ALU.mult))
            ln.link(v.tensor_reduce(r[:], sq[:], AX.X, ALU.add))
            v.tensor_scalar(r[:], r[:], 1.0 / F, EPS, ALU.mult, ALU.add).then_inc(std, 1)
            v.wait_ge(rooted, 1)
            ln.link(v.reciprocal(r[:], r[:]))
            ln.link(v.tensor_tensor(c[:], c[:], wide(r[:], F), ALU.mult))
            ln.link(v.tensor_tensor(c[:], c[:], tall(par[:, 1, :]), ALU.mult))
            ln.link(v.tensor_tensor(c[:], c[:], tall(par[:, 2, :]), ALU.add))
            ln.link(v.tensor_reduce(sc[:], c[:].rearrange("p b (h e) -> p b e h", h=GH), AX.X, ALU.add))
            ln.mark(v.tensor_scalar(sc[:], sc[:], 1.0 / GH, None, ALU.mult))
            ln.mark(v.memset(better[:], 0.0))
            ln.settle()
            for e in range(EXPERTS):
                for f in range(EXPERTS):
                    if f != e:
                        ln.link(v.tensor_tensor(cmp_[:], sc[:, :, f], sc[:, :, e], ALU.is_ge if f < e else ALU.is_gt))
                        ln.link(v.tensor_tensor(better[:, :, e], better[:, :, e], cmp_[:], ALU.add))
            ln.mark(v.tensor_scalar(better[:], better[:], 1.5, None, ALU.is_lt))
            ln.link(v.tensor_reduce(m[:], sc[:], AX.X, ALU.max))
            v.tensor_tensor(sc[:], sc[:], wide(m[:], EXPERTS), ALU.subtract).then_inc(ex, 1)
            v.wait_ge(exped, 1)
            ln.link(v.tensor_tensor(sc[:], sc[:], better[:], ALU.mult))
            ln.link(v.tensor_reduce(m[:], sc[:], AX.X, ALU.add))
            ln.link(v.reciprocal(m[:], m[:]))
            ln.link(v.tensor_tensor(gates[:], sc[:], wide(m[:], EXPERTS), ALU.mult))

        @block.scalar
        def _(act):
            act.wait_ge(std, 1)
            act.activation(r[:], r[:], ACT.Sqrt).then_inc(rooted, 1)
            act.wait_ge(ex, 1)
            act.activation(sc[:], sc[:], ACT.Exp).then_inc(exped, 1)


def l1_ffn(nc, g):
    F = GH * EXPERTS
    W, T = F + 2 * GH, F + GH
    table = nc.dram_tensor("rtable", (NP, T), F32, kind="Internal").ap()
    sums = nc.dram_tensor("route_sums", (E2, W), F32, kind="Internal").ap()
    outputs = nc.dram_tensor("expert_outputs", (NB // SUPER * EXPERTS * P, SUPER * D), F32, kind="Internal").ap()
    keys = nc.dram_tensor("keys2", (E2,), F32, kind="Internal").ap()
    node_stats(nc, g, "st3")
    with Stage(nc, "x1") as s:
        gates = s.sb("gates", [P, NB, EXPERTS])
        with Stage(nc, "x1r") as sr:
            start, end = sr.sb("start", [P, NB]), sr.sb("end", [P, NB])
            own = sr.sb("own", [P, NB, W])
            last = sr.sb("last", [P, W])
            H = 2 * D
            w1 = sr.sb("w1", [P, 2, EXPERTS * H])
            w2 = sr.sb("w2", [P, EXPERTS * H // P, D])
            b1 = sr.sb("b1", [P, EXPERTS * H // P])
            b2 = sr.sb("b2", [P, EXPERTS, D])
            loaded = sr.sem("loaded")
            with sr.block() as block:
                @block.sync
                def _(sp):
                    for e in range(EXPERTS):
                        sp.dma_start(w1[:, :, e * H:(e + 1) * H], g.ins["L1_ffn_W1"][e].rearrange("(k p) n -> p k n", p=P)).then_inc(loaded, 16)
                        sp.dma_start(w2[:, e * HC:(e + 1) * HC, :], g.ins["L1_ffn_W2"][e].rearrange("(k p) n -> p k n", p=P)).then_inc(loaded, 16)
                        sp.dma_start(b2[:, e, :], g.ins["L1_ffn_b2"][e].partition_broadcast(P)).then_inc(loaded, 16)
                    with nc.allow_non_contiguous_dma("biases, one for a lane"):
                        sp.dma_start(b1[:], g.ins["L1_ffn_b1"].rearrange("e (k p) -> p (e k)", p=P)).then_inc(loaded, 16)
            with Stage(nc, "x1e") as s1:
                dstf = s1.sb("dstf", [P, C2])
                src = s1.sb("src", [P, C2], U32)
                keep = s1.sb("keep", [P, C2])
                reset = s1.sb("reset", [P, C2])
                adst = s1.sb("adst", [P, C2, GH])
                adn = s1.sb("adn", [P, NB, GH])
                w = s1.sb("w", [P, 2, W])
                dv = s1.sem("dv")
                sort_edges(nc, g, dstf, src)
                routing_weights(nc, g, w)

                def route_rows(v, ln, h, b, rows, xn, po, out):
                    ln.mark(v.tensor_scalar(flat(own, W)[:, bass.ds(b * W, W)], po[:, 0:W], 0.0, None, ALU.add))
                    ln.mark(v.tensor_scalar(flat(adn, GH)[:, bass.ds(b * GH, GH)], po[:, T:W], 0.0, None, ALU.add))
                    return v.tensor_copy(out[:], po[:, 0:T])

                project(nc, g, "rt1", w, W, T, route_rows, 2, [(table, 0, T)])
                segments(nc, g, "seg2", dstf, C2, E2, start, end, keys)
                boundaries(nc, g, "bnd2", dstf, C2, reset, keep)
                spread(nc, g, "ad", adn[:], GH, dstf, C2, E2, start, end, keep, adst[:])
                with Stage(nc, "x1l") as s2:
                    route_and_hide(nc, g, s2, table, adst, reset, src, sums, last, w1, b1, w2, b2, loaded, outputs)
                carry_in(nc, g, "car2", dstf, C2, last, F, GH, sums)
                with s1.block() as block:
                    @block.vector
                    def _(v):
                        ln = Links(v, dv)
                        m = own[:, :, F + GH:]
                        ln.link(v.tensor_tensor(m, m, own[:, :, F:F + GH], ALU.add))
                        ln.link(v.scalar_tensor_tensor(out=m, in0=m, scalar=0.2, in1=m, op0=ALU.mult, op1=ALU.max))
                        ln.link(v.memset(own[:, :, F:F + GH], 1.0))
            rows = sr.sb("rows", [P, NB, W])
            with Stage(nc, "x1g") as s1:
                gather_ends(nc, g, "end2", s1, end, sums, rows)
                none = s1.sb("none", [P, NB])
                dv2 = s1.sem("dv2")
                with s1.block() as block:
                    @block.vector
                    def _(v):
                        ln = Links(v, dv2)
                        ln.link(v.tensor_tensor(none[:], end[:], start[:], ALU.is_le))
                        ln.link(v.tensor_scalar(none[:], none[:], -BIG, None, ALU.mult))
                        ln.link(v.tensor_tensor(rows[:, :, F + GH:], rows[:, :, F + GH:],
                                                none[:].rearrange("p (b o) -> p b o", o=1).to_broadcast([P, NB, GH]), ALU.add))
                merge(nc, g, s1, F, GH, rows, extra=own, eps=1e-16)
                expert_gates(nc, g, s1, rows, gates)
        combine(nc, g, flat(gates, EXPERTS), outputs)


STAGES = [l0_gnn, l0_ffn, l1_gnn, l1_ffn]


def store_nodes(nc, g):
    with Stage(nc, "out") as s:
        put = s.sem("put")
        full = N // P
        with s.block() as block:
            @block.sync
            def _(sp):
                sp.dma_start(g.out[0:full * P, :].rearrange("(b p) d -> p b d", p=P),
                             g.x[:, 0:full, :]).then_inc(put, 16)
                sp.dma_start(g.out[full * P:N, :], g.x[0:N - full * P, full, :]).then_inc(put, 16)
                sp.wait_ge(put, 32)


def program(nc, ins, out):
    Stage.used.clear()
    g = G()
    g.out = out
    g.in_x, g.in_src, g.in_dst, g.edge256, g.edge64 = (ins[n] for n in ("x", "src", "dst", "edge_attr_256", "edge_attr_64"))
    g.ins = ins
    g.W_self, g.W_func, g.W_att = (ins["L0_gnn_" + n] for n in ("W_self", "W_func", "W_att"))
    with Stage(nc, "g") as s:
        g.x = s.sb("x", [P, NB, D])
        g.mean, g.rstd, g.start, g.end, g.nodeid = (s.sb(n, [P, NB]) for n in ("mean", "rstd", "start", "end", "nodeid"))
        g.src = s.sb("src", [P, C], U32)
        g.dstf = s.sb("dstf", [P, C])
        g.ident, g.ones, g.below, g.chunkno = (s.sb(n, [P, P]) for n in ("ident", "ones", "below", "chunkno"))
        g.keys = nc.dram_tensor("keys", (P * C,), F32, kind="Internal").ap()
        load_nodes(nc, g)
        for stage in STAGES:
            stage(nc, g)
            recycle(nc)
        store_nodes(nc, g)


def kernel(**inputs):
    import concourse.bacc as _bacc
    from concourse.bass_utils import run_bass_kernel_spmd as _run

    nc = _bacc.Bacc("TRN2", target_bir_lowering=False, num_devices=1)

    def lay_out(name, a):
        a = np.ascontiguousarray(a)
        if name == "x":
            a = np.concatenate([a, np.zeros((NP - N, D), a.dtype)])
        elif name in ("src", "dst"):
            a = np.concatenate([a, np.full(P * C - E, NP if name == "dst" else 0, a.dtype)]).reshape(P, C)
        elif name.startswith("edge_attr"):
            a = np.concatenate([a, np.zeros((P * C - E, a.shape[1]), a.dtype)])
        return a

    arrays, ins = {}, {}
    for name, a in inputs.items():
        a = lay_out(name, a)
        arrays[f"in_{name}"] = a
        ins[name] = nc.dram_tensor(f"in_{name}", a.shape, mybir.dt.from_np(a.dtype), kind="ExternalInput").ap()
    out = nc.dram_tensor("out_0", (N, D), F32, kind="ExternalOutput").ap()
    program(nc, ins, out)
    r = _run(nc, [arrays], core_ids=[0])
    return r.results[0]["out_0"]
```

```python
from contextlib import ExitStack

import numpy as np

import concourse.bass as bass
from concourse import mybir

ALU = mybir.AluOpType
ACT = mybir.ActivationFunctionType
AX = mybir.AxisListType
F32 = mybir.dt.float32
I32 = mybir.dt.int32
U32 = mybir.dt.uint32

P = 128
N = 6250
D = 256
NB = 50
NP = NB * P
E = 100000
C = 782
BC = 17
E2 = 131072
C2 = E2 // P
ID_BITS = 13
PU = 10
RING = 5
VB = 24
BIG = 1e30
EPS = 1e-5


class Links:

    def __init__(self, eng, sem):
        self.eng, self.sem, self.n, self.turns = eng, sem, 0, 0

    def mark(self, ins):
        ins.then_inc(self.sem, 1)
        self.n += 1

    def settle(self, n=None):
        self.eng.wait_ge(self.sem, self.turns + (self.n if n is None else n))

    def link(self, ins):
        self.mark(ins)
        self.settle()

    def enter(self, i, per, first=0):
        self.start, self.per, self.turns = self.n, per, i * per
        self.n -= first * per
        self.base = self.n

    def leave(self, count):
        assert self.n - self.base == self.per, f"{self.n - self.base} links in the body"
        self.n, self.turns = self.start + self.per * count, 0


class Stage:

    used = []

    def __init__(self, nc, name):
        self.nc, self.name, self.stack = nc, name, ExitStack()

    def __enter__(self):
        return self

    def __exit__(self, *a):
        return self.stack.__exit__(*a)

    def sb(self, name, shape, dt=F32):
        return self.stack.enter_context(self.nc.sbuf_tensor(f"{self.name}_{name}", shape, dt))

    def ps(self, name, shape=(P, 512), dt=F32):
        return self.stack.enter_context(self.nc.psum_tensor(f"{self.name}_{name}", list(shape), dt))

    def sem(self, name):
        sem = self.nc.alloc_semaphore(f"{self.name}_{name}")
        Stage.used.append(sem)
        return sem

    def gather_sem(self, name):
        return self.nc.alloc_semaphore(f"{self.name}_{name}")

    def sems(self, name, n=2):
        return [self.sem(f"{name}{i}") for i in range(n)]

    def block(self):
        return self.nc.Block()


def recycle(nc):
    numbers = sorted(s.num for s in Stage.used)
    with nc.Block() as block:
        @block.gpsimd
        def _(pool):
            while numbers:
                n = 1
                while n < len(numbers) and numbers[n] == numbers[0] + n:
                    n += 1
                pool.sem_clear(range(numbers[0], numbers[0] + n))
                del numbers[:n]
    for s in Stage.used:
        nc.release_semaphore(s)
    Stage.used.clear()


def gate(eng, sem, value, passed):
    eng.wait_ge(sem, value)
    eng.sem_inc(passed, 1)


def flat(t, w):
    return t[:].rearrange("p a b -> p (a b)")


class G:
    pass


def load_nodes(nc, g):
    with Stage(nc, "ld") as s:
        dma, made, dve = s.sem("dma"), s.sem("made"), s.sem("dve")
        g.x_loaded = s.sem("x_loaded")
        itmp = s.sb("itmp", [P, NB], I32)
        ktmp = s.sb("ktmp", [P, P], I32)
        dtmp = s.sb("dtmp", [P, C], I32)
        with s.block() as block:
            @block.sync
            def _(sp):
                sp.dma_start(dtmp[:], g.in_dst).then_inc(dma, 16)
                sp.dma_start(g.src[:], g.in_src.bitcast(U32)).then_inc(dma, 16)
                sp.wait_ge(dma, 32)

            @block.scalar
            def _(act):
                act.wait_ge(dma, 32)
                act.dma_start(g.x[:], g.in_x.rearrange("(b p) d -> p b d", p=P)).then_inc(g.x_loaded, 16)

            @block.gpsimd
            def _(pool):
                pool.memset(g.ident[:], 0.0).then_inc(made, 1)
                pool.memset(g.ones[:], 1.0).then_inc(made, 1)
                pool.memset(g.below[:], 1.0).then_inc(made, 1)
                pool.iota(itmp[:], [[P, NB]], base=0, channel_multiplier=1).then_inc(made, 1)
                pool.iota(ktmp[:], [[1, P]], base=1, channel_multiplier=0).then_inc(made, 1)
                pool.wait_ge(made, 5)
                pool.affine_select(out=g.ident[:], in_=g.ident[:], compare_op=ALU.not_equal, fill=1.0,
                                   base=0, pattern=[[-1, P]], channel_multiplier=1).then_inc(made, 1)
                pool.affine_select(out=g.below[:], in_=g.below[:], compare_op=ALU.is_gt, fill=0.0,
                                   base=0, pattern=[[-1, P]], channel_multiplier=1).then_inc(made, 1)

            @block.vector
            def _(v):
                v.wait_ge(made, 7)
                v.tensor_copy(g.nodeid[:], itmp[:]).then_inc(dve, 1)
                v.tensor_copy(g.chunkno[:], ktmp[:]).then_inc(dve, 1)
                v.wait_ge(dma, 32)
                v.tensor_copy(g.dstf[:], dtmp[:]).then_inc(dve, 1)
                v.wait_ge(dve, 3)


class Stats:

    def __init__(self, g, s):
        self.g = g
        self.six = s.sb("six", [P, NB * 6])
        self.t = s.sb("t", [P, 3, NB])
        self.dve, self.var_ready, self.std_ready = s.sem("sdve"), s.sem("var_ready"), s.sem("std_ready")

    def vector(self, v):
        g, t, six = self.g, self.t, self.six
        v6 = six[:].rearrange("p (b k) -> p k b", k=6)
        ln = Links(v, self.dve)
        if g.x_loaded is not None:
            v.wait_ge(g.x_loaded, 16)
            g.x_loaded = None
        with v.Fori(0, NB // PU) as i:
            ln.enter(i, PU)
            for u in range(PU):
                b = i * PU + u
                ln.mark(v.bn_stats(six[:, bass.ds(b * 6, 6)], flat(g.x, D)[:, bass.ds(b * D, D)]))
            ln.leave(NB // PU)
        ln.settle()
        ln.mark(v.tensor_tensor(g.mean[:], v6[:, 1, :], v6[:, 4, :], ALU.add))
        ln.mark(v.tensor_tensor(t[:, 0, :], v6[:, 1, :], v6[:, 4, :], ALU.subtract))
        ln.link(v.tensor_tensor(t[:, 1, :], v6[:, 2, :], v6[:, 5, :], ALU.add))
        ln.mark(v.tensor_scalar(g.mean[:], g.mean[:], 0.5, None, ALU.mult))
        ln.mark(v.tensor_scalar(t[:, 1, :], t[:, 1, :], 1.0 / D, EPS, ALU.mult, ALU.add))
        ln.link(v.tensor_tensor(t[:, 0, :], t[:, 0, :], t[:, 0, :], ALU.mult))
        v.scalar_tensor_tensor(out=t[:, 2, :], in0=t[:, 0, :], scalar=0.25, in1=t[:, 1, :],
                               op0=ALU.mult, op1=ALU.add).then_inc(self.var_ready, 1)
        v.wait_ge(self.std_ready, 1)
        ln.link(v.reciprocal(g.rstd[:], t[:, 2, :]))

    def scalar(self, act):
        act.wait_ge(self.var_ready, 1)
        act.activation(self.t[:, 2, :], self.t[:, 2, :], ACT.Sqrt).then_inc(self.std_ready, 1)


def node_stats(nc, g, name):
    with Stage(nc, name) as s:
        stats = Stats(g, s)
        with s.block() as block:
            @block.vector
            def _(v):
                stats.vector(v)

            @block.scalar
            def _(act):
                stats.scalar(act)


def project(nc, g, name, w, width, out_width, finish, per, tables=(), prepare=None, depth=2,
            beside=None, ready=None):
    turns = NB // PU
    with Stage(nc, name) as s:
        xn = [s.sb(f"xn{k}", [P, D]) for k in range(RING)]
        out = [s.sb(f"out{k}", [P, max(out_width, 1)]) for k in range(RING)]
        xt = [s.sb(f"xt{h}", [P, 2, P]) for h in range(2)]
        pt = [s.ps(f"pt{h}") for h in range(2)]
        po = [s.ps(f"po{h}") for h in range(2)]
        normed, turned, copied, product, finished, dve = (s.sem(x) for x in (
            "normed", "turned", "copied", "product", "finished", "dve"))
        stored = s.sems("stored", RING)
        with s.block() as block:
            def rows(b):
                return flat(g.x, D)[:, bass.ds(b * D, D)]

            @block.vector
            def _(v):
                ln = Links(v, dve)
                v.sem_inc(finished, RING)

                def norm(i, u):
                    b = i * PU + u
                    v.wait_ge(finished, i * PU + (u + 1))
                    if prepare is not None:
                        prepare(v, b, xn[u % RING]).then_inc(normed, 1)
                        return
                    v.tensor_scalar(xn[u % RING][:], rows(b), g.mean[:, bass.ds(b, 1)], g.rstd[:, bass.ds(b, 1)],
                                    ALU.subtract, ALU.mult).then_inc(normed, 1)

                def blocks(i, final=False):
                    for u in range(PU):
                        if u + 2 < PU or not final:
                            norm(i, u + 2)
                        v.wait_ge(product, i * PU + (u + 3))
                        if tables:
                            v.wait_ge(stored[u % RING], (i * (PU // RING) + (u // RING + 1)) * (16 * len(tables)))
                        if ready is not None:
                            ready(v, i, u)
                        b = i * PU + u
                        finish(v, ln, u % 2, b, rows(b), xn[u % RING], po[u % 2], out[u % RING]).then_inc(finished, 1)

                norm(0, 0)
                norm(0, 1)
                with v.Fori(0, turns - 1) as i:
                    ln.enter(i, PU * per)
                    blocks(i)
                    ln.leave(turns - 1)
                blocks(turns - 1, final=True)
                v.wait_ge(finished, NB + RING)

            @block.tensor
            def _(pe):
                pe.sem_inc(product, 2)

                def turn(i, u):
                    pe.wait_ge(normed, i * PU + (u + 1))
                    pe.wait_ge(copied, i * PU + (u + 1))
                    for k in range(depth):
                        ins = pe.transpose(pt[u % 2][:, k * P:(k + 1) * P], xn[u % RING][:, k * P:(k + 1) * P], g.ident[:])
                    ins.then_inc(turned, 1)

                def blocks(i, final=False):
                    for u in range(PU):
                        if u + 1 < PU or not final:
                            turn(i, u + 1)
                        pe.wait_ge(copied, i * PU + (u + 3))
                        pe.wait_ge(finished, i * PU + (u + RING - 1))
                        for k in range(depth):
                            ins = pe.matmul(po[u % 2][:, 0:width], xt[u % 2][:, k, :], w[:, k, :], start=(k == 0),
                                            stop=(k == depth - 1))
                        ins.then_inc(product, 1)

                turn(0, 0)
                with pe.Fori(0, turns - 1) as i:
                    blocks(i)
                blocks(turns - 1, final=True)

            @block.scalar
            def _(act):
                act.sem_inc(copied, 2)
                with act.Fori(0, turns) as i:
                    for u in range(PU):
                        act.wait_ge(turned, i * PU + (u + 1))
                        act.wait_ge(product, i * PU + (u + 1))
                        act.activation(flat(xt[u % 2], P)[:, 0:depth * P], pt[u % 2][:, 0:depth * P],
                                       ACT.Copy).then_inc(copied, 1)

            if beside is not None:
                @block.gpsimd
                def _(pool):
                    beside(pool, lambda b: pool.wait_ge(finished, b + 1 + RING))

            if tables:
                @block.sync
                def _(sp):
                    for k in range(RING):
                        sp.sem_inc(stored[k], 16 * len(tables))
                    with sp.Fori(0, turns) as i:
                        for u in range(PU):
                            sp.wait_ge(finished, i * PU + (u + 1 + RING))
                            for to, c0, c1 in tables:
                                sp.dma_start(to[bass.ds((i * PU + u) * P, P), :],
                                             out[u % RING][:, c0:c1]).then_inc(stored[u % RING], 16)
                    for k in range(RING):
                        sp.wait_ge(stored[k], 16 * len(tables) * (NB // RING + 1))


class EdgeSort:

    WITHIN = range(1, C2.bit_length())
    ACROSS = range(C2.bit_length(), E2.bit_length())

    def __init__(self, nc, g, s, resume):
        self.nc, self.g, self.s, self.resume = nc, g, s, resume
        self.bits_j, self.bits = C2.bit_length() - 1, E2.bit_length() - 1
        self.buf = [s.sb(f"sort{k}", [P, C2]) for k in range(2)]
        self.lane, self.bit = s.sb("sort_lane", [P, 1], I32), s.sb("sort_bit", [P, 1], I32)
        self.signs, self.flips = (s.sb(f"sort_{n}", [P, self.bits - self.bits_j]) for n in ("signs", "flips"))
        self.pt = s.ps("sort_pt", [P, C2])
        self.got, self.made, self.ready, self.turned, self.stored, dve = (s.sem("sort_" + x) for x in (
            "got", "made", "ready", "turned", "stored", "dve"))
        self.dve = dve
        self.at = 0
        self.source = []

    def load(self, sp):
        if self.resume:
            sp.dma_start(self.buf[0][:].bitcast(I32), self.g.sorted_keys.rearrange("(p c) -> p c", p=P)).then_inc(self.got, 16)
            return
        for k in range(2):
            sp.dma_start(self.buf[k][:].bitcast(I32),
                         self.g.ins["L1_ffn_edge_index"][k].rearrange("(p c) -> p c", p=P)).then_inc(self.got, 16)

    def number_lanes(self, pool):
        pool.iota(self.lane[:], [[0, 1]], base=0, channel_multiplier=1).then_inc(self.made, 1)

    def start(self, v):
        self.ln = ln = Links(v, self.dve)
        signs, flips = self.signs, self.flips
        src, dst = (self.buf[k][:].bitcast(I32) for k in range(2))
        v.wait_ge(self.made, 1)
        for k in range(self.bits - self.bits_j):
            ln.link(v.tensor_scalar(self.bit[:], self.lane[:], k, 1, ALU.logical_shift_right, ALU.bitwise_and))
            ln.link(v.tensor_copy(signs[:, k:k + 1], self.bit[:]))
        ln.link(v.tensor_scalar(signs[:], signs[:], -2.0, 1.0, ALU.mult, ALU.add))
        ln.mark(v.tensor_copy(flips[:, 0:1], signs[:, 0:1]))
        ln.mark(v.tensor_tensor(flips[:, 1:], signs[:, 1:], signs[:, 0:-1], ALU.mult))
        if self.resume:
            v.wait_ge(self.got, 16)
            ln.settle()
            return
        v.wait_ge(self.got, 32)
        ln.mark(v.tensor_scalar(src, src, float(N - 1), None, ALU.min))
        ln.link(v.tensor_scalar(dst, dst, float(2 ** ID_BITS - 1), None, ALU.min))
        ln.link(v.tensor_scalar(dst, dst, ID_BITS, 1 << 28, ALU.logical_shift_left, ALU.bitwise_or))
        ln.link(v.tensor_tensor(src, dst, src, ALU.bitwise_or))

    def compare(self, v, lo, hi, to_lo, to_hi, up):
        self.ln.mark(v.tensor_tensor(to_lo, lo, hi, ALU.min if up else ALU.max))
        self.ln.mark(v.tensor_tensor(to_hi, lo, hi, ALU.max if up else ALU.min))

    def stage(self, v, stride):
        a, b = (self.buf[k][:].rearrange("p (m z i) -> p m z i", z=2, i=stride) for k in (self.at, 1 - self.at))
        self.compare(v, a[:, :, 0, :], a[:, :, 1, :], b[:, :, 0, :], b[:, :, 1, :], True)
        self.ln.settle()
        self.at = 1 - self.at

    def trip(self, v):
        v.sem_inc(self.ready, 1)
        self.source.append(self.at)
        v.wait_ge(self.turned, len(self.source))
        self.ln.link(v.tensor_copy(self.buf[1 - self.at][:], self.pt[:]))
        self.at = 1 - self.at

    def stages(self, v, phases):
        ln, bits, bits_j = self.ln, self.bits, self.bits_j
        for k in phases:
            if k >= bits_j:
                j = k - bits_j
                factor = self.flips[:, j:j + 1] if k < bits else self.signs[:, j - 1:j]
                ln.link(v.tensor_scalar(self.buf[1 - self.at][:], self.buf[self.at][:], factor, None, ALU.mult))
                self.at = 1 - self.at
            if k > bits_j:
                self.trip(v)
                for b in range(k - bits_j - 1, -1, -1):
                    self.stage(v, 2 ** b)
                    yield
                self.trip(v)
            for b in range(min(k, bits_j) - 1, -1, -1):
                if k < bits_j:
                    w = [self.buf[t][:].rearrange("p (o d m z i) -> p o d m z i", d=2, m=2 ** (k - 1 - b), z=2, i=2 ** b)
                         for t in (self.at, 1 - self.at)]
                    for d in range(2):
                        self.compare(v, w[0][:, :, d, :, 0, :], w[0][:, :, d, :, 1, :],
                                     w[1][:, :, d, :, 0, :], w[1][:, :, d, :, 1, :], d == 0)
                    ln.settle()
                    self.at = 1 - self.at
                else:
                    self.stage(v, 2 ** b)
                yield

    def transpose(self, pe):
        for trip, at in enumerate(self.source):
            pe.wait_ge(self.ready, trip + 1)
            for c in range(C2 // P):
                ins = pe.transpose(self.pt[:, c * P:(c + 1) * P], self.buf[at][:, c * P:(c + 1) * P], self.g.ident[:])
            ins.then_inc(self.turned, 1)

    def store(self):
        with self.s.block() as block:
            @block.sync
            def _(sp):
                sp.dma_start(self.g.sorted_keys.rearrange("(p c) -> p c", p=P),
                             self.buf[self.at][:].bitcast(I32)).then_inc(self.stored, 16)
                sp.wait_ge(self.stored, 16)


def segments(nc, g, name, dstf, cols, edges, start, end, keys):
    groups = cols * P // P
    with Stage(nc, name) as s:
        firsts = s.sb("firsts", [1, groups])
        firstb = s.sb("firstb", [P, groups])
        c1 = s.sb("c1", [P, NB])
        gi = s.sb("gi", [P, NB], U32)
        rows = s.sb("rows", [P, NB, P])
        one = s.sb("one", [1, 1])
        half_less = s.sb("half_less", [P, NB])
        junk2 = [s.sb(f"junk{k}", [P, groups]) for k in range(2)]
        spread_out, signed = s.sem("spread_out"), s.sem("signed")
        pb = [s.ps(f"pb{h}") for h in range(2)]
        half = groups // 2
        put, got, made, bc, counted, wrote, dve = (s.sem(x) for x in (
            "put", "got", "made", "bc", "counted", "wrote", "dve"))
        gath = s.gather_sem("gath")
        stats = Stats(g, s)
        with s.block() as block:
            @block.sync
            def _(sp):
                sp.dma_start(keys.rearrange("(p c) -> p c", p=P), dstf[:]).then_inc(put, 16)
                sp.wait_ge(put, 16)
                with nc.allow_non_contiguous_dma("one key of every 128"):
                    sp.dma_start(firsts[:], keys.rearrange("(a g k) -> a g k", a=1, k=P)[:, :, 0]).then_inc(got, 16)
                    sp.wait_ge(counted, 1)
                    sp.dma_start(end[0:P - 1, :], start[1:P, :]).then_inc(wrote, 16)
                    sp.dma_start(end[P - 1:P, 0:NB - 1], start[0:1, 1:NB]).then_inc(wrote, 16)
                    sp.dma_start(end[P - 1:P, NB - 1:NB], one[:]).then_inc(wrote, 16)
                    sp.wait_ge(wrote, 48)

            @block.tensor
            def _(pe):
                pe.wait_ge(got, 16)
                for h in range(2):
                    pe.matmul(pb[h][:, 0:half], g.ones[0:1, :], firsts[:, h * half:(h + 1) * half],
                              start=True, stop=True).then_inc(bc, 1)

            @block.vector
            def _(v):
                ln = Links(v, dve)
                ln.mark(v.memset(one[:], float(edges)))
                v.wait_ge(bc, 2)
                for h in range(2):
                    ln.mark(v.tensor_copy(firstb[:, h * half:(h + 1) * half], pb[h][:, 0:half]))
                ln.settle()
                ln.mark(v.tensor_scalar(half_less[:], g.nodeid[:], -0.5, None, ALU.add))
                ln.settle()
                v.sem_inc(spread_out, 1)
                for b in range(VB):
                    if b % 6 == 0:
                        ln.settle()
                    junk = flat(rows, P)[:, (b % 6) * groups:(b % 6 + 1) * groups]
                    ln.mark(v.tensor_scalar(junk, firstb[:], g.nodeid[:, b:b + 1], 0.0, ALU.is_lt, ALU.add,
                                            accum_out=c1[:, b:b + 1]))
                ln.settle()
                v.wait_ge(signed, NB - VB)
                ln.link(v.tensor_scalar(c1[:, VB:], c1[:, VB:], 0.5, 0.5 * groups, ALU.mult, ALU.add))
                ln.link(v.tensor_scalar(c1[:], c1[:], -1.0, 0.0, ALU.add, ALU.max))
                v.tensor_copy(gi[:], c1[:]).then_inc(made, 1)
                stats.vector(v)
                v.wait_ge(gath, 16 * NB)
                ln.link(v.tensor_tensor(rows[:], rows[:], g.nodeid[:].rearrange("p (b o) -> p b o", o=1).to_broadcast([P, NB, P]),
                                        ALU.is_lt))
                ln.link(v.tensor_reduce(start[:], rows[:], AX.X, ALU.add))
                v.scalar_tensor_tensor(out=start[:], in0=c1[:], scalar=float(P), in1=start[:],
                                       op0=ALU.mult, op1=ALU.add).then_inc(counted, 1)

            @block.scalar
            def _(act):
                act.wait_ge(spread_out, 1)
                for b in range(VB, NB):
                    if b >= VB + 2:
                        act.wait_ge(signed, b - VB - 1)
                    act.activation(junk2[b % 2][:], firstb[:], ACT.Sign, bias=half_less[:, b:b + 1], scale=-1.0,
                                   accum_out=c1[:, b:b + 1]).then_inc(signed, 1)
                stats.scalar(act)

            @block.gpsimd
            def _(pool):
                pool.wait_ge(made, 1)
                for b in range(NB):
                    pool.indirect_dma_start(rows[:, b, :], None, keys.rearrange("(g k) -> g k", k=P),
                                            bass.IndirectOffsetOnAxis(ap=gi[:, b:b + 1], axis=0)).then_inc(gath, 16)
                pool.wait_ge(gath, 16 * NB)


def boundaries(nc, g, name, dstf, cols, reset, keep):
    with Stage(nc, name) as s:
        dve = s.sem("dve")
        with s.block() as block:
            @block.vector
            def _(v):
                ln = Links(v, dve)
                ln.mark(v.memset(keep[:, 0:1], 0.0))
                ln.mark(v.tensor_tensor(keep[:, 1:cols], dstf[:, 1:cols], dstf[:, 0:cols - 1], ALU.is_equal))
                ln.settle()
                ln.link(v.tensor_scalar(reset[:], keep[:], -1.0, BIG, ALU.add, ALU.mult))


class Spread:

    def __init__(self, nc, g, name, width, dstf, cols, start, end, firsts, zeroed=None):
        self.nc, self.name, self.cols, self.firsts = nc, name, cols, firsts
        self.s = s = Stage(nc, name)
        at, empty = s.sb("at", [P, NB]), s.sb("empty", [P, NB])
        lf = s.sb("lf", [P, 1])
        self.ai, self.li = s.sb("ai", [P, NB], U32), s.sb("li", [P, 1], U32)
        self.lane = s.sb("lane", [P, width])
        made, put, dve = s.sem("made"), s.sem("put"), s.sem("dve")
        self.scattered, self.lane_got = s.gather_sem("scattered"), s.gather_sem("lane_got")
        with Stage(nc, name + "z") as s1, s1.block() as block:
            if zeroed is None:
                zero = s1.sb("zero", [P, cols * width])

            @block.vector
            def _(v):
                ln = Links(v, dve)
                if zeroed is None:
                    v.memset(zero[:], 0.0).then_inc(made, 1)
                ln.mark(v.tensor_tensor(empty[:], start[:], end[:], ALU.is_ge))
                ln.link(v.tensor_scalar(lf[:], dstf[:, 0:1], float(NP - 1), None, ALU.min))
                ln.link(v.scalar_tensor_tensor(out=at[:], in0=empty[:], scalar=float(1 << 20), in1=start[:],
                                               op0=ALU.mult, op1=ALU.add))
                ln.mark(v.tensor_copy(self.ai[:], at[:]))
                ln.mark(v.tensor_copy(self.li[:], lf[:]))
                ln.settle()

            @block.sync
            def _(sp):
                if zeroed is None:
                    sp.wait_ge(made, 1)
                    sp.dma_start(firsts.rearrange("(p c) h -> p (c h)", p=P), zero[:]).then_inc(put, 16)
                    sp.wait_ge(put, 16)

    def scatter(self, pool, finished, nodes):
        for b in range(NB):
            finished(b)
            pool.indirect_dma_start(self.firsts, bass.IndirectOffsetOnAxis(ap=self.ai[:, b:b + 1], axis=0),
                                    nodes[:, b, :], None, bounds_check=P * self.cols - 1,
                                    oob_is_err=False).then_inc(self.scattered, 16)
        pool.wait_ge(self.scattered, 16 * NB)

    def lanes(self, table, nodes=None):
        put = self.s.sem("lane_put")
        with self.s.block() as block:
            @block.sync
            def _(sp):
                if nodes is not None:
                    with self.nc.allow_non_contiguous_dma("a table of a few columns"):
                        sp.dma_start(table.rearrange("(b p) h -> p b h", p=P), nodes).then_inc(put, 16)
                else:
                    sp.sem_inc(put, 16)
                sp.wait_ge(self.lane_got, 16)
                with self.nc.allow_non_contiguous_dma("a row of each lane"):
                    sp.dma_start(self.firsts.rearrange("(p c) h -> p c h", p=P)[:, 0, :], self.lane[:]).then_inc(put, 16)
                sp.wait_ge(put, 32)

            @block.gpsimd
            def _(pool):
                pool.wait_ge(put, 16)
                pool.indirect_dma_start(self.lane[:], None, table,
                                        bass.IndirectOffsetOnAxis(ap=self.li[:, 0:1], axis=0)).then_inc(self.lane_got, 16)
                pool.wait_ge(self.lane_got, 16)

    def carry(self, keep, per_edge):
        loaded, dve = self.s.sem("loaded"), self.s.sem("cdve")
        with self.s.block() as block:
            @block.sync
            def _(sp):
                sp.dma_start(per_edge[:], self.firsts.rearrange("(p c) h -> p c h", p=P)).then_inc(loaded, 16)
                sp.wait_ge(loaded, 16)

            @block.vector
            def _(v):
                ln = Links(v, dve)
                v.wait_ge(loaded, 16)
                for h in range(per_edge.shape[2]):
                    ln.mark(v.tensor_tensor_scan(per_edge[:, :, h], keep[:], per_edge[:, :, h], 0.0,
                                                 ALU.mult, ALU.add))
                ln.settle()


def carry_in(nc, g, name, dstf, cols, last, feats, heads, sums):
    width = feats + 2 * heads
    fh = feats // heads
    top = slice(feats + heads, width)
    with Stage(nc, name) as s:
        diag = s.sb("diag", [P, P])
        same = s.sb("same", [P, P])
        off = s.sb("off", [P, P])
        mm = s.sb("mm", [P, heads, P])
        em = s.sb("em", [P, heads, P])
        et = s.sb("et", [P, heads, P])
        nmax = s.sb("nmax", [P, heads])
        carried = s.sb("carried", [P, width])
        row = s.sb("row", [P, width])
        run = s.sb("run", [P, cols])
        at, base = s.sb("at", [P, 1]), s.sb("base", [P, 1], I32)
        ai = s.sb("ai", [P, 1], U32)
        m = s.sb("m", [P, 3, heads])
        pr = s.ps("pr")
        pt = s.ps("pt")
        pc = s.ps("pc")
        based, found, dd, rowed, maxed, exped, turned, copied, summed, factors, merged, dve = (s.sem(x) for x in (
            "based", "found", "dd", "rowed", "maxed", "exped", "turned", "copied", "summed", "factors", "merged", "dve"))
        got, put = s.gather_sem("got"), s.gather_sem("put")
        with s.block() as block:
            @block.gpsimd
            def _(pool):
                pool.iota(base[:], [[0, 1]], base=-1, channel_multiplier=cols).then_inc(based, 1)
                pool.wait_ge(found, 1)
                pool.indirect_dma_start(row[:], None, sums, bass.IndirectOffsetOnAxis(ap=ai[:, 0:1], axis=0)).then_inc(got, 16)
                pool.wait_ge(merged, 1)
                pool.indirect_dma_start(sums, bass.IndirectOffsetOnAxis(ap=ai[:, 0:1], axis=0), row[:], None).then_inc(put, 16)
                pool.wait_ge(put, 16)

            @block.vector
            def _(v):
                ln = Links(v, dve)
                ln.link(v.tensor_scalar(run[:], dstf[:], dstf[:, 0:1], 0.0, ALU.is_equal, ALU.add, accum_out=at[:]))
                v.wait_ge(based, 1)
                ln.link(v.tensor_copy(nmax[:, 0:1], base[:]))
                ln.link(v.tensor_tensor(at[:], at[:], nmax[:, 0:1], ALU.add))
                v.tensor_copy(ai[:], at[:]).then_inc(found, 1)
                for h in range(-1, heads):
                    column = dstf[:, cols - 1:cols] if h < 0 else last[:, feats + heads + h:feats + heads + h + 1]
                    if h >= 0:
                        v.wait_ge(rowed, h + 1)
                    v.tensor_scalar(diag[:], g.ident[:], column, None, ALU.mult).then_inc(dd, 1)
                    v.wait_ge(rowed, h + 2)
                    if h < 0:
                        ln.link(v.tensor_scalar(same[:], pr[:, 0:P], dstf[:, 0:1], None, ALU.is_equal))
                        ln.link(v.tensor_tensor(same[:], same[:], g.below[:], ALU.mult))
                        ln.link(v.tensor_scalar(off[:], same[:], -1.0, BIG, ALU.add, ALU.mult))
                    else:
                        ln.link(v.tensor_tensor(mm[:, h, :], pr[:, 0:P], off[:], ALU.add))
                ln.link(v.tensor_reduce(carried[:, top], mm[:], AX.X, ALU.max))
                v.tensor_scalar(nmax[:], carried[:, top], -1.0, None, ALU.mult).then_inc(maxed, 1)
                v.wait_ge(got, 16)
                ln.link(v.tensor_tensor(m[:, 2, :], carried[:, top], row[:, top], ALU.max))
                ln.mark(v.tensor_tensor(m[:, 0, :], row[:, top], m[:, 2, :], ALU.subtract))
                ln.mark(v.tensor_tensor(m[:, 1, :], carried[:, top], m[:, 2, :], ALU.subtract))
                ln.settle()
                ln.link(v.tensor_copy(row[:, top], m[:, 2, :]))
                v.sem_inc(factors, 1)
                v.wait_ge(exped, 1)
                for h in range(heads):
                    ln.mark(v.tensor_tensor(em[:, h, :], em[:, h, :], same[:], ALU.mult))
                ln.settle()
                v.sem_inc(exped, 1)
                v.wait_ge(turned, 1)
                v.tensor_copy(flat(et, P), pt[:, 0:heads * P]).then_inc(copied, 1)
                v.wait_ge(summed, 1)
                ln.link(v.tensor_copy(carried[:, 0:feats + heads], pc[:, 0:feats + heads]))
                v.wait_ge(factors, 2)
                for h in range(heads):
                    for part in (slice(h * fh, (h + 1) * fh), slice(feats + h, feats + h + 1)):
                        ln.mark(v.tensor_scalar(row[:, part], row[:, part], m[:, 0, h:h + 1], None, ALU.mult))
                ln.settle()
                for h in range(heads):
                    for part in (slice(h * fh, (h + 1) * fh), slice(feats + h, feats + h + 1)):
                        ln.mark(v.scalar_tensor_tensor(out=row[:, part], in0=carried[:, part], scalar=m[:, 1, h:h + 1],
                                                       in1=row[:, part], op0=ALU.mult, op1=ALU.add))
                ln.settle()
                v.sem_inc(merged, 1)

            @block.tensor
            def _(pe):
                for h in range(heads + 1):
                    pe.wait_ge(dd, h + 1)
                    if h:
                        pe.wait_ge(dve, 6 + h - 1)
                    pe.matmul(pr[:, 0:P], g.ones[:], diag[:], start=True, stop=True).then_inc(rowed, 1)
                pe.wait_ge(exped, 2)
                for h in range(heads):
                    ins = pe.transpose(pt[:, h * P:(h + 1) * P], em[:, h, :], g.ident[:])
                ins.then_inc(turned, 1)
                pe.wait_ge(copied, 1)
                for h in range(heads):
                    pe.matmul(pc[:, h * fh:(h + 1) * fh], et[:, h, :], last[:, h * fh:(h + 1) * fh], start=True, stop=True)
                    ins = pe.matmul(pc[:, feats + h:feats + h + 1], et[:, h, :], last[:, feats + h:feats + h + 1],
                                    start=True, stop=True)
                ins.then_inc(summed, 1)

            @block.scalar
            def _(act):
                act.wait_ge(maxed, 1)
                for h in range(heads):
                    ins = act.activation(em[:, h, :], mm[:, h, :], ACT.Exp, bias=nmax[:, h:h + 1])
                ins.then_inc(exped, 1)
                act.wait_ge(factors, 1)
                act.activation(m[:, 0:2, :], m[:, 0:2, :], ACT.Exp).then_inc(factors, 1)


class Ends:

    def __init__(self, nc, s, end, table, rows):
        self.table, self.rows = table, rows
        e1 = s.sb("e1", [P, NB])
        self.ei = s.sb("ei", [P, NB], U32)
        dve = s.sem("gdve")
        self.got = [s.gather_sem(f"got{u}") for u in range(PU)]
        with s.block() as block:
            @block.vector
            def _(v):
                ln = Links(v, dve)
                ln.link(v.tensor_scalar(e1[:], end[:], -1.0, 0.0, ALU.add, ALU.max))
                ln.link(v.tensor_copy(self.ei[:], e1[:]))

    def gather(self, pool, finished=None):
        for b in range(NB):
            if b >= PU:
                pool.wait_ge(self.got[b % PU], 16 * (b // PU))
            pool.indirect_dma_start(self.rows[:, b, :], None, self.table,
                                    bass.IndirectOffsetOnAxis(ap=self.ei[:, b:b + 1], axis=0)).then_inc(self.got[b % PU], 16)
        for u in range(PU):
            pool.wait_ge(self.got[u], 16 * (NB // PU))

    def ready(self, v, i, u):
        v.wait_ge(self.got[u], i * 16 + 16)


def gather_ends(nc, s, end, table, rows):
    ends = Ends(nc, s, end, table, rows)
    with s.block() as block:
        @block.gpsimd
        def _(pool):
            ends.gather(pool)


def merge(nc, g, s, feats, heads, rows, extra, eps):
    fh = feats // heads
    parts = [rows, extra]
    mt = s.sb("mt", [P, NB, heads])
    dve, act_s, ready = s.sem("mdve"), s.sem("mact"), s.sem("mready")
    mx = [x[:, :, feats + heads:feats + 2 * heads] for x in parts]
    with s.block() as block:
        @block.vector
        def _(v):
            ln = Links(v, dve)
            ln.link(v.tensor_tensor(mt[:], mx[0], mx[1], ALU.max))
            for m in mx:
                ln.mark(v.tensor_tensor(m, m, mt[:], ALU.subtract))
            ln.settle()
            v.sem_inc(ready, 1)
            v.wait_ge(act_s, len(parts))
            for h in range(heads):
                for x in parts:
                    f = x[:, :, feats + heads + h:feats + heads + h + 1]
                    ln.mark(v.tensor_tensor(x[:, :, h * fh:(h + 1) * fh], x[:, :, h * fh:(h + 1) * fh],
                                            f.to_broadcast([P, NB, fh]), ALU.mult))
                    ln.mark(v.tensor_tensor(x[:, :, feats + h:feats + h + 1], x[:, :, feats + h:feats + h + 1], f, ALU.mult))
            ln.settle()
            ln.link(v.tensor_tensor(rows[:, :, 0:feats + heads], rows[:, :, 0:feats + heads],
                                    extra[:, :, 0:feats + heads], ALU.add))
            ln.link(v.tensor_scalar(mt[:], rows[:, :, feats:feats + heads], eps, None, ALU.add))
            ln.link(v.reciprocal(mt[:], mt[:]))
            for h in range(heads):
                ln.mark(v.tensor_tensor(rows[:, :, h * fh:(h + 1) * fh], rows[:, :, h * fh:(h + 1) * fh],
                                        mt[:, :, h:h + 1].to_broadcast([P, NB, fh]), ALU.mult))
            ln.settle()

        @block.scalar
        def _(act):
            act.wait_ge(ready, 1)
            for m in mx:
                act.activation(m, m, ACT.Exp).then_inc(act_s, 1)


ZC = 17
QZ = C // ZC


def zero_queries(sp, g, zero, zeroed):
    rows = g.qfirst.rearrange("(p c) w -> p (c w)", p=P)
    with sp.Fori(0, QZ) as i:
        sp.dma_start(rows[:, bass.ds(i * (ZC * P), ZC * P)], zero[:]).then_inc(zeroed, 16)
    sp.wait_ge(zeroed, 16 * QZ)


def gat_weights(nc, g, s, w, wew):
    att = s.sb("att", [P, 3 * D])
    junk = s.sb("junk", [P, D])
    got, dve = s.sem("wgot"), s.sem("wdve")
    with s.block() as block:
        @block.sync
        def _(sp):
            sp.dma_start(w[:, :, 0:D], g.W_func.rearrange("(k p) n -> p k n", p=P)).then_inc(got, 16)
            sp.dma_start(att[:], g.W_att.rearrange("n o -> (n o)").partition_broadcast(P)).then_inc(got, 16)
            sp.wait_ge(got, 32)

        @block.vector
        def _(v):
            ln = Links(v, dve)
            v.wait_ge(got, 32)
            ln.mark(v.tensor_copy(wew[:], att[:, 2 * D:]))
            for k in range(2):
                for j in range(2):
                    ln.link(v.tensor_tensor_reduce(junk[:], w[:, k, 0:D], att[:, j * D:(j + 1) * D], 1.0, 0.0,
                                                   ALU.mult, ALU.add, w[:, k, D + j:D + j + 1]))


def gat_edges(nc, g, s, wew, sdst, keep, reset, ztable, sums, last):
    W = D + 2
    turns = C // BC // 2
    ea = [s.sb(f"ea{h}", [P, BC, D]) for h in range(2)]
    zg = [s.sb(f"zg{h}", [P, BC, W]) for h in range(2)]
    ob = [s.sb(f"ob{h}", [P, BC, W]) for h in range(2)]
    ix = [s.sb(f"ix{h}", [P, BC], U32) for h in range(2)]
    ew = s.sb("ew", [P, BC])
    sc = s.sb("sc", [P, BC])
    lk = s.sb("lk", [P, BC])
    mb = [s.sb(f"mb{h}", [P, BC + 1]) for h in range(2)]
    wd = [s.sb(f"wd{h}", [P, 2, BC]) for h in range(2)]
    scored, weighed, done, ea_used = (s.sems(x) for x in ("scored", "weighed", "done", "ea_used"))
    ea_got, stored, scaled = (s.sems(x) for x in ("ea_got", "stored", "scaled"))
    z_got = [s.gather_sem(f"z_got{h}") for h in range(2)]
    dve, ixd, passed, lastd = s.sem("dve"), s.sem("ixd"), s.sem("passed"), s.sem("lastd")
    rows = g.edge256.rearrange("(p c) d -> p c d", p=P)
    out = sums.rearrange("(p c) w -> p c w", p=P)
    with s.block() as block:
        @block.sync
        def _(sp):
            def load(h, turn, c0):
                sp.wait_ge(ea_used[h], turn + 1)
                sp.dma_start(ea[h][:], rows[:, bass.ds(c0, BC), :]).then_inc(ea_got[h], 16)

            def store(h, turn, c0):
                sp.wait_ge(done[h], turn + 2)
                sp.dma_start(out[:, bass.ds(c0, BC), :], ob[h][:]).then_inc(stored[h], 16)

            for h in range(2):
                sp.sem_inc(stored[h], 16)
            load(0, 0, 0)
            with sp.Fori(0, turns - 1) as i:
                load(1, i, (i * 2 + 1) * BC)
                store(0, i, i * 2 * BC)
                load(0, i + 1, (i * 2 + 2) * BC)
                store(1, i, (i * 2 + 1) * BC)
            load(1, turns - 1, (turns * 2 - 1) * BC)
            for h in range(2):
                store(h, turns - 1, (turns * 2 - 2 + h) * BC)
            for h in range(2):
                sp.wait_ge(stored[h], 16 * (turns + 1))

        @block.gpsimd
        def _(pool):
            with pool.Fori(0, turns) as i:
                for h in range(2):
                    gate(pool, done[h], i + 1, passed)
                    pool.tensor_copy(ix[h][:], g.src[:, bass.ds((i * 2 + h) * BC, BC)]).then_inc(ixd, 1)
                    gate(pool, ixd, i * 2 + h + 1, passed)
                    for k in range(BC):
                        pool.indirect_dma_start(zg[h][:, k, :], None, ztable,
                                                bass.IndirectOffsetOnAxis(ap=ix[h][:, k:k + 1], axis=0)).then_inc(z_got[h], 16)
            for h in range(2):
                pool.wait_ge(z_got[h], 16 * BC * turns)

        @block.vector
        def _(v):
            ln = Links(v, dve)
            for h in range(2):
                v.sem_inc(scored[h], 1)
                v.sem_inc(done[h], 1)
                v.sem_inc(ea_used[h], 1)
            ln.mark(v.memset(mb[1][:], 0.0))
            ln.link(v.memset(ob[1][:, BC - 1, :], 0.0))
            with v.Fori(0, turns) as i:
                ln.enter(i, 2 * (8 + BC))
                for h in range(2):
                    cols = bass.ds((i * 2 + h) * BC, BC)
                    v.wait_ge(ea_got[h], (i + 1) * 16)
                    for k in range(BC):
                        ins = v.tensor_tensor_reduce(ea[h][:, k, :], ea[h][:, k, :], wew[:], 1.0, 0.0,
                                                     ALU.mult, ALU.add, ew[:, k:k + 1])
                    ins.then_inc(ea_used[h], 1)
                    v.wait_ge(ea_used[h], i + 2)
                    ln.link(v.tensor_tensor(sc[:], ew[:], sdst[:, cols], ALU.add))
                    v.wait_ge(z_got[h], (i + 1) * (16 * BC))
                    ln.link(v.tensor_tensor(sc[:], sc[:], zg[h][:, :, D], ALU.add))
                    ln.mark(v.tensor_copy(mb[h][:, 0:1], mb[1 - h][:, BC:BC + 1]))
                    ln.link(v.scalar_tensor_tensor(out=lk[:], in0=sc[:], scalar=0.01, in1=sc[:],
                                                   op0=ALU.mult, op1=ALU.max))
                    ln.link(v.tensor_tensor_scan(mb[h][:, 1:BC + 1], reset[:, cols], lk[:], mb[h][:, 0:1],
                                                 ALU.add, ALU.max))
                    v.wait_ge(weighed[h], i + 1)
                    ln.link(v.tensor_tensor(wd[h][:, 0, :], mb[h][:, 0:BC], mb[h][:, 1:BC + 1], ALU.subtract))
                    ln.link(v.tensor_tensor(wd[h][:, 0, :], wd[h][:, 0, :], reset[:, cols], ALU.add))
                    v.tensor_tensor(wd[h][:, 1, :], lk[:], mb[h][:, 1:BC + 1], ALU.subtract).then_inc(scored[h], 1)
                    v.wait_ge(stored[h], (i + 1) * 16)
                    ln.mark(v.tensor_copy(ob[h][:, :, D + 1], mb[h][:, 1:BC + 1]))
                    v.wait_ge(weighed[h], i + 2)
                    v.wait_ge(done[1 - h], i + 1 + h)
                    ln.settle()
                    before = ob[1 - h][:, BC - 1, :]
                    ln.link(v.tensor_tensor_scan(ob[h][:, :, D], wd[h][:, 0, :], wd[h][:, 1, :],
                                                 before[:, D:D + 1], ALU.mult, ALU.add))
                    for k in range(BC):
                        v.wait_ge(scaled[h], i * BC + (k + 1))
                        ins = v.scalar_tensor_tensor(out=ob[h][:, k, 0:D], in0=before[:, 0:D], scalar=wd[h][:, 0, k:k + 1],
                                                     in1=zg[h][:, k, 0:D], op0=ALU.mult, op1=ALU.add)
                        before = ob[h][:, k, :]
                        if k < BC - 1:
                            ln.link(ins)
                        else:
                            ins.then_inc(done[h], 1)
                ln.leave(turns)
            v.wait_ge(done[1], turns + 1)
            v.tensor_copy(last[:], ob[1][:, BC - 1, :]).then_inc(lastd, 1)
            v.wait_ge(lastd, 1)

        @block.scalar
        def _(act):
            for h in range(2):
                act.sem_inc(weighed[h], 1)
            with act.Fori(0, turns) as i:
                for h in range(2):
                    act.wait_ge(scored[h], i + 2)
                    act.activation(flat(wd[h], BC), flat(wd[h], BC), ACT.Exp).then_inc(weighed[h], 1)
                    act.wait_ge(weighed[h], i + 2)
                    act.wait_ge(z_got[h], (i + 1) * (16 * BC))
                    for k in range(BC):
                        act.activation(zg[h][:, k, 0:D], zg[h][:, k, 0:D], ACT.Copy,
                                       scale=wd[h][:, 1, k:k + 1]).then_inc(scaled[h], 1)


def l0_gnn(nc, g):
    W = D + 2
    ztable = nc.dram_tensor("ztable", (NP, W), F32, kind="Internal").ap()
    sums = nc.dram_tensor("gat_sums", (P * C, W), F32, kind="Internal").ap()
    with Stage(nc, "g0") as s:
        last = s.sb("last", [P, W])
        with Stage(nc, "g0e") as s1:
            wew = s1.sb("wew", [P, D])
            sdst = s1.sb("sdst", [P, C])
            sdn = s1.sb("sdn", [P, NB, 1])
            keep = s1.sb("keep", [P, C])
            reset = s1.sb("reset", [P, C])
            segments(nc, g, "seg", g.dstf, C, E, g.start, g.end, g.keys)
            boundaries(nc, g, "bnd", g.dstf, C, reset, keep)
            sd = nc.dram_tensor("sd_table", (NP, 1), F32, kind="Internal").ap()
            firsts = nc.dram_tensor("sd_firsts", (P * C, 1), F32, kind="Internal").ap()
            spread = Spread(nc, g, "sd", 1, g.dstf, C, g.start, g.end, firsts)
            with spread.s:
                with Stage(nc, "g0w") as s2:
                    w = s2.sb("w", [P, 2, W])
                    gat_weights(nc, g, s2, w, wew)

                    def z_rows(v, ln, h, b, rows, xn, po, out):
                        ln.mark(v.tensor_scalar(flat(sdn, 1)[:, bass.ds(b, 1)], po[:, D + 1:W], 0.0, None, ALU.add))
                        return v.tensor_copy(out[:], po[:, 0:W])

                    project(nc, g, "z", w, W, W, z_rows, 1, [(ztable, 0, W)],
                            beside=lambda pool, finished: spread.scatter(pool, finished, sdn))
                spread.lanes(sd, sdn[:])
                spread.carry(keep, sdst[:].rearrange("p (c o) -> p c o", o=1))
            gat_edges(nc, g, s1, wew, sdst, keep, reset, ztable, sums, last)
        carry_in(nc, g, "car0", g.dstf, C, last, D, 1, sums)
        rows = s.sb("rows", [P, NB, W])
        ends = Ends(nc, s, g.end, sums, rows)
        w = s.sb("wself", [P, 2, D])
        t = [s.sb(f"t{h}", [P, D]) for h in range(2)]
        r = [s.sb(f"r{h}", [P, 1]) for h in range(2)]
        some = s.sb("some", [P, NB])
        none = s.sb("none", [P, NB])
        got, dv = s.sem("sgot"), s.sem("sdv")
        with s.block() as block:
            @block.sync
            def _(sp):
                sp.dma_start(w[:], g.W_self.rearrange("(k p) n -> p k n", p=P)).then_inc(got, 16)
                sp.wait_ge(got, 16)

            @block.vector
            def _(v):
                ln = Links(v, dv)
                ln.mark(v.tensor_tensor(some[:], g.end[:], g.start[:], ALU.is_gt))
                ln.mark(v.tensor_tensor(none[:], g.end[:], g.start[:], ALU.is_le))
                ln.settle()

        def h_new(v, ln, h, b, rows_x, xn, po, out):
            u = t[h]
            row = flat(rows, W)
            ln.mark(v.reciprocal(r[h][:], row[:, bass.ds(b * W + D, 1)]))
            inverse = ln.n
            ln.mark(v.tensor_tensor(rows_x, rows_x, xn[:], ALU.add))
            ln.settle(inverse)
            ln.link(v.scalar_tensor_tensor(out=u[:], in0=row[:, bass.ds(b * W, D)], scalar=r[h][:], in1=po[:, 0:D],
                                           op0=ALU.mult, op1=ALU.add))
            ln.link(v.tensor_scalar(u[:], u[:], some[:, bass.ds(b, 1)], None, ALU.mult))
            ln.link(v.scalar_tensor_tensor(out=u[:], in0=xn[:], scalar=none[:, bass.ds(b, 1)], in1=u[:],
                                           op0=ALU.mult, op1=ALU.add))
            return v.scalar_tensor_tensor(out=rows_x, in0=u[:], scalar=0.0, in1=rows_x, op0=ALU.max, op1=ALU.add)

        project(nc, g, "hs", w, D, 0, h_new, 5, beside=ends.gather, ready=ends.ready)


SUPER = 5
HC = 4


def mlp(nc, g, s, name, w1, b1, w2, b2, biased, gates, groups, func, keep_normed, beside):
    turns = NB // SUPER
    width = SUPER * P
    hw = width // 2
    uses = 2 * HC
    xn = s.sb("xn", [P, SUPER, D])
    xt = s.sb("xt", [P, 2, width])
    ht = [s.sb(f"ht{k}", [P, HC, width]) for k in range(2)]
    t = [s.sb(f"t{k}", [P, D]) for k in range(2)]
    pt = [s.ps(f"pt{k}") for k in range(2)]
    ph = [s.ps(f"ph{k}") for k in range(4)]
    py = [s.ps(f"py{k}") for k in range(2)]
    normed, turned, copied, hidden, acted, out_ready, out_read, dve = (s.sem(x) for x in (
        "normed", "turned", "copied", "hidden", "acted", "out_ready", "out_read", "mdve"))
    HU = uses * groups
    YU = SUPER * groups
    with s.block() as block:
        @block.sync
        def _(sp):
            beside(sp)

        @block.vector
        def _(v):
            ln = Links(v, dve)
            v.sem_inc(out_read, 2)

            def norm(i):
                for j in range(SUPER):
                    b = i * SUPER + j
                    rows = flat(g.x, D)[:, bass.ds(b * D, D)]
                    ln.mark(v.tensor_scalar(xn[:, j, :], rows, g.mean[:, bass.ds(b, 1)], g.rstd[:, bass.ds(b, 1)],
                                            ALU.subtract, ALU.mult))
                ln.settle()
                v.sem_inc(normed, 1)
                if keep_normed:
                    for j in range(SUPER):
                        rows = flat(g.x, D)[:, bass.ds((i * SUPER + j) * D, D)]
                        ln.mark(v.tensor_tensor(rows, rows, xn[:, j, :], ALU.add))
                    ln.settle()

            def outputs(i):
                for q in range(groups):
                    for j in range(SUPER):
                        n = q * SUPER + j
                        b = i * SUPER + j
                        rows = flat(g.x, D)[:, bass.ds(b * D, D)]
                        gate_ = gates[:, bass.ds(b * groups + q, 1)]
                        v.wait_ge(out_ready, i * YU + (10 + n + 1))
                        src = py[n % 2][:, 0:D]
                        if biased[q]:
                            ln.link(v.tensor_tensor(t[n % 2][:], src, b2[:, q, :], ALU.add))
                            src = t[n % 2][:]
                        ln.mark(v.scalar_tensor_tensor(out=rows, in0=src, scalar=gate_, in1=rows,
                                                       op0=ALU.mult, op1=ALU.add))
                        ln.settle()
                        v.sem_inc(out_read, 1)

            per = SUPER * (2 if keep_normed else 1) + sum(SUPER * (2 if z else 1) for z in biased)
            norm(0)
            with v.Fori(0, turns - 1) as i:
                ln.enter(i, per)
                v.wait_ge(turned, i * SUPER + SUPER)
                norm(i + 1)
                outputs(i)
                ln.leave(turns - 1)
            outputs(turns - 1)

        @block.tensor
        def _(pe):
            pe.sem_inc(out_ready, 10)

            def turn(i, first=False):
                pe.wait_ge(normed, i + 1)
                for j in range(SUPER):
                    if j >= 2:
                        pe.wait_ge(copied, i * SUPER + (j - 1))
                    elif not first:
                        pe.wait_ge(copied, i * SUPER)
                    pe.transpose(pt[j % 2][:, 0:P], xn[:, j, 0:P], g.ident[:])
                    pe.transpose(pt[j % 2][:, P:D], xn[:, j, P:D], g.ident[:]).then_inc(turned, 1)

            def hide(i, q):
                if q == 0:
                    pe.wait_ge(copied, i * SUPER + SUPER)
                for c in range(HC):
                    for z in range(2):
                        u = q * uses + 2 * c + z
                        ch = q * HC + c
                        pe.wait_ge(acted, i * HU + (u + 1))
                        for k in range(2):
                            ins = pe.matmul(ph[u % 4][:, 0:hw], w1[:, k, ch * P:(ch + 1) * P],
                                            xt[:, k, z * hw:(z + 1) * hw], start=(k == 0), stop=(k == 1))
                        ins.then_inc(hidden, 1)

            def down(i, q):
                pe.wait_ge(acted, i * HU + ((q + 1) * uses + 4))
                for j in range(SUPER):
                    n = q * SUPER + j
                    pe.wait_ge(out_read, i * YU + (n + 1))
                    for c in range(HC):
                        ins = pe.matmul(py[n % 2][:, 0:D], ht[q % 2][:, c, j * P:(j + 1) * P], w2[:, q * HC + c, :],
                                        start=(c == 0), stop=(c == HC - 1))
                    ins.then_inc(out_ready, 1)

            def body(i, more):
                for q in range(groups):
                    hide(i, q)
                    if q:
                        down(i, q - 1)
                if more:
                    turn(i + 1)
                down(i, groups - 1)

            turn(0, True)
            with pe.Fori(0, turns - 1) as i:
                body(i, True)
            body(turns - 1, False)

        @block.scalar
        def _(act):
            act.sem_inc(acted, 4)

            def copy(i):
                for j in range(SUPER):
                    act.wait_ge(turned, i * SUPER + (j + 1))
                    act.activation(xt[:, :, j * P:(j + 1) * P], pt[j % 2][:, 0:D].rearrange("p (k n) -> p k n", k=2),
                                   ACT.Copy).then_inc(copied, 1)

            def act_groups(i):
                for q in range(groups):
                    act.wait_ge(out_ready, i * YU + (q * SUPER + 5))
                    for c in range(HC):
                        for z in range(2):
                            u = q * uses + 2 * c + z
                            act.wait_ge(hidden, i * HU + (u + 1))
                            act.activation(ht[q % 2][:, c, z * hw:(z + 1) * hw], ph[u % 4][:, 0:hw], func,
                                           bias=b1[:, q * HC + c:q * HC + c + 1]).then_inc(acted, 1)

            copy(0)
            with act.Fori(0, turns - 1) as i:
                act_groups(i)
                copy(i + 1)
            act_groups(turns - 1)


def router(nc, g, wgt):
    with Stage(nc, "rt") as s:
        wr = s.sb("wr", [P, D])
        br = s.sb("br", [P, 1])
        xn = s.sb("xn", [P, PU, D])
        dots = s.sb("dots", [P, PU])
        got, dve = s.sem("got"), s.sem("dve")
        with s.block() as block:
            @block.sync
            def _(sp):
                sp.dma_start(wr[:], g.ins["L0_ffn_wr"].rearrange("n o -> (n o)").partition_broadcast(P)).then_inc(got, 16)
                sp.dma_start(br[:], g.ins["L0_ffn_br"].partition_broadcast(P)).then_inc(got, 16)
                sp.wait_ge(got, 32)

            @block.vector
            def _(v):
                ln = Links(v, dve)
                v.wait_ge(got, 32)
                with v.Fori(0, NB // PU) as i:
                    ln.enter(i, 2 * PU + 1)
                    for u in range(PU):
                        b = i * PU + u
                        ln.mark(v.tensor_scalar(xn[:, u, :], flat(g.x, D)[:, bass.ds(b * D, D)], g.mean[:, bass.ds(b, 1)],
                                                g.rstd[:, bass.ds(b, 1)], ALU.subtract, ALU.mult))
                    ln.settle()
                    for u in range(PU):
                        ln.mark(v.tensor_tensor_reduce(xn[:, u, :], xn[:, u, :], wr[:], 1.0, 0.0, ALU.mult, ALU.add,
                                                       dots[:, u:u + 1]))
                    ln.settle()
                    ln.mark(v.tensor_scalar(wgt[:, bass.ds(i * PU, PU)], dots[:], br[:], None, ALU.add))
                    ln.leave(NB // PU)
                ln.settle()


def choose(nc, g, wgt, count, chosen):
    with Stage(nc, "ch") as s:
        sort = EdgeSort(nc, g, s, resume=False)
        u = s.sb("u", [P, NB], I32)
        half = s.sb("half", [P, NB], I32)
        keys = s.sb("keys", [P, 3, NB])
        mask = s.sb("mask", [P, NB])
        key = s.sb("key", [P, NB])
        junk = s.sb("junk", [P, NB])
        sure = s.sb("sure", [P, NB])
        missing, low, step, cand, cnt, take = (s.sb(n, [P, 1]) for n in ("missing", "low", "step", "cand", "cnt", "take"))
        pc = s.ps("pc")
        counted, summed, dve = s.sem("counted"), s.sem("summed"), s.sem("dve")
        bits = [16, 16, 13]
        with s.block() as block:
            @block.sync
            def _(sp):
                sort.load(sp)

            @block.gpsimd
            def _(pool):
                sort.number_lanes(pool)

            @block.vector
            def _(v):
                ln = Links(v, dve)
                sort.start(v)
                stages = sort.stages(v, sort.WITHIN)
                wi = wgt[:].bitcast(I32)
                ln.link(v.tensor_scalar(u[:], wi, 31, -2147483648, ALU.arith_shift_right, ALU.bitwise_or))
                ln.link(v.tensor_tensor(u[:], u[:], wi, ALU.bitwise_xor))
                ln.link(v.tensor_scalar(half[:], u[:], 16, None, ALU.logical_shift_right))
                ln.link(v.tensor_copy(keys[:, 0, :], half[:]))
                ln.link(v.tensor_scalar(half[:], u[:], 65535, None, ALU.bitwise_and))
                ln.mark(v.tensor_copy(keys[:, 1, :], half[:]))
                ln.mark(v.tensor_scalar(keys[:, 2, :], g.nodeid[:], -1.0, float(NP), ALU.mult, ALU.add))
                ln.mark(v.tensor_scalar(mask[:], g.nodeid[:], float(N), None, ALU.is_lt))
                ln.mark(v.memset(chosen[:], 0.0))
                ln.mark(v.memset(missing[:], float(count)))
                done = 0
                for level in range(3):
                    ln.settle()
                    ln.link(v.scalar_tensor_tensor(out=key[:], in0=keys[:, level, :], scalar=1.0, in1=mask[:],
                                                   op0=ALU.add, op1=ALU.mult))
                    ln.mark(v.tensor_scalar(key[:], key[:], -1.0, None, ALU.add))
                    ln.mark(v.memset(low[:], 0.0))
                    ln.mark(v.memset(step[:], float(2 ** (bits[level] - 1))))
                    ln.settle()
                    for i in range(bits[level]):
                        ln.link(v.tensor_tensor(cand[:], low[:], step[:], ALU.add))
                        v.tensor_scalar(junk[:], key[:], cand[:], 0.0, ALU.is_ge, ALU.add,
                                        accum_out=cnt[:]).then_inc(counted, 1)
                        next(stages, None)
                        v.wait_ge(summed, i + (done + 1))
                        ln.link(v.tensor_scalar(take[:], pc[:, 0:1], missing[:], step[:], ALU.is_ge, ALU.mult))
                        ln.mark(v.tensor_tensor(low[:], low[:], take[:], ALU.add))
                        ln.mark(v.tensor_scalar(step[:], step[:], 0.5, None, ALU.mult))
                        ln.settle()
                    done += bits[level]
                    ln.link(v.tensor_scalar(sure[:], key[:], low[:], None, ALU.is_gt if level < 2 else ALU.is_ge))
                    ln.link(v.tensor_tensor(chosen[:], chosen[:], sure[:], ALU.add))
                    if level < 2:
                        ln.link(v.tensor_scalar(junk[:], key[:], low[:], 0.0, ALU.is_gt, ALU.add, accum_out=cnt[:]))
                        v.sem_inc(counted, 1)
                        next(stages, None)
                        v.wait_ge(summed, done + 1)
                        done += 1
                        ln.mark(v.tensor_tensor(missing[:], missing[:], pc[:, 0:1], ALU.subtract))
                        ln.mark(v.tensor_scalar(mask[:], key[:], low[:], None, ALU.is_equal))
                ln.settle()
                for _ in stages:
                    pass

            @block.tensor
            def _(pe):
                done = 0
                for level in range(3):
                    with pe.Fori(0, bits[level]) as i:
                        pe.wait_ge(counted, i + (done + 1))
                        pe.matmul(pc[:, 0:1], g.ones[:], cnt[:], start=True, stop=True).then_inc(summed, 1)
                    done += bits[level]
                    if level < 2:
                        pe.wait_ge(counted, done + 1)
                        pe.matmul(pc[:, 0:1], g.ones[:], cnt[:], start=True, stop=True).then_inc(summed, 1)
                        done += 1
        sort.store()


def l0_ffn(nc, g):
    S, H = N, 4 * D
    kept = max(1, S // 2) - 1
    node_stats(nc, g, "st1")
    with Stage(nc, "f0") as s:
        wgt = s.sb("wgt", [P, NB])
        chosen = s.sb("chosen", [P, NB])
        gates = s.sb("gates", [P, NB, 2])
        w1 = s.sb("w1", [P, 2, H])
        w2 = s.sb("w2", [P, H // P, D])
        b1 = s.sb("b1", [P, H // P])
        b2 = s.sb("b2", [P, 2, D])
        zero = s.sb("zero", [P, ZC * P])
        got, dv, zeroed = s.sem("got"), s.sem("dv"), s.sem("zeroed")
        with s.block() as block:
            @block.scalar
            def _(act):
                act.dma_start(w1[:], g.ins["L0_ffn_w1"].rearrange("(k p) n -> p k n", p=P)).then_inc(got, 16)
                act.dma_start(w2[:], g.ins["L0_ffn_w2"].rearrange("(k p) n -> p k n", p=P)).then_inc(got, 16)
                with nc.allow_non_contiguous_dma("biases, one for a lane"):
                    act.dma_start(b1[:], g.ins["L0_ffn_b1"].rearrange("(k p) -> p k", p=P)).then_inc(got, 16)
                act.dma_start(b2[:, 0, :], g.ins["L0_ffn_b2"].partition_broadcast(P)).then_inc(got, 16)

        router(nc, g, wgt)
        choose(nc, g, wgt, kept, chosen)
        with s.block() as block:
            @block.sync
            def _(sp):
                sp.wait_ge(got, 64)

            @block.vector
            def _(v):
                for q in range(2):
                    v.tensor_tensor(gates[:, :, q], wgt[:], chosen[:], ALU.mult).then_inc(dv, 1)
                v.memset(zero[:], 0.0).then_inc(dv, 1)
                v.wait_ge(dv, 3)

        mlp(nc, g, s, "mlp0", w1, b1, w2, b2, (True, False), flat(gates, 2), 2, ACT.Gelu_apprx_tanh, True,
            lambda sp: zero_queries(sp, g, zero, zeroed))


MSG = 128
HEADS = 4
OUTC = MSG // HEADS
RAD = 64
GC = 4
VH = 1


def message_weights(nc, g, w, bias, wedge, wback, wout, wskip):
    with Stage(nc, "mw") as s:
        n2m = s.sb("n2m", [P, D])
        four = s.sb("four", [P, 4, P])
        fourt = s.sb("fourt", [P, 4 * P])
        we = s.sb("we", [P, RAD])
        wet = s.sb("wet", [RAD, P])
        ed = s.sb("ed", [RAD, RAD])
        m2n = s.sb("m2n", [P, 2, P])
        beta = s.sb("beta", [P, 3, P])
        pa, pb, pc, pd, pe_ = s.ps("pa"), s.ps("pb"), s.ps("pc"), s.ps("pd"), s.ps("pe")
        pf = s.ps("pf")
        got, turned, copied, made, dve = (s.sem(x) for x in ("got", "turned", "copied", "made", "dve"))
        stats = Stats(g, s)
        I = g.ins
        with s.block() as block:
            @block.scalar
            def _(act):
                stats.scalar(act)

            @block.sync
            def _(sp):
                sp.dma_start(n2m[:], I["L1_gnn_W_n2m"]).then_inc(got, 16)
                for k, n in enumerate(("Wq", "Wk", "Wv", "Wskip")):
                    sp.dma_start(four[:, k, :], I["L1_gnn_" + n]).then_inc(got, 16)
                for k, n in enumerate(("bq", "bk", "bv", "bskip")):
                    sp.dma_start(bias[:, k * P:(k + 1) * P], I["L1_gnn_" + n].partition_broadcast(P)).then_inc(got, 16)
                sp.dma_start(we[:], I["L1_gnn_We"]).then_inc(got, 16)
                sp.dma_start(ed[:], I["L1_gnn_W_edge"]).then_inc(got, 16)
                sp.dma_start(m2n[:], I["L1_gnn_W_m2n"].rearrange("(k p) m -> p k m", p=P)).then_inc(got, 16)
                sp.dma_start(flat(beta, P), I["L1_gnn_Wbeta"].rearrange("o n -> (o n)").partition_broadcast(P)).then_inc(got, 16)
                sp.wait_ge(got, 16 * 13)

            @block.tensor
            def _(pe):
                pe.wait_ge(got, 16 * 13)
                for k in range(4):
                    pe.transpose(pa[:, k * P:(k + 1) * P], four[:, k, :], g.ident[:])
                pe.transpose(pb[0:RAD, 0:P], we[:], g.ident[:])
                for k in range(2):
                    ins = pe.transpose(pc[:, k * P:(k + 1) * P], m2n[:, k, :], g.ident[:])
                ins.then_inc(turned, 1)
                pe.wait_ge(copied, 2)
                pe.matmul(pd[:, :], n2m[:, 0:P], fourt[:], start=True, stop=True)
                pe.matmul(pe_[:, :], n2m[:, P:D], fourt[:], start=True, stop=True)
                pe.matmul(pf[0:RAD, 0:P], ed[:], wet[:], start=True, stop=True).then_inc(made, 1)

            @block.vector
            def _(v):
                ln = Links(v, dve)
                stats.vector(v)
                v.wait_ge(turned, 1)
                v.tensor_copy(fourt[:], pa[:]).then_inc(copied, 1)
                v.tensor_copy(wet[:], pb[0:RAD, 0:P]).then_inc(copied, 1)
                ln.mark(v.tensor_copy(wback[:, 0, :], pc[:, 0:D]))
                ln.mark(v.tensor_tensor(wout[:], beta[:, 0, :], beta[:, 2, :], ALU.add))
                ln.mark(v.tensor_tensor(wskip[:], beta[:, 1, :], beta[:, 2, :], ALU.subtract))
                v.wait_ge(made, 1)
                ln.mark(v.tensor_copy(w[:, 0, :], pd[:]))
                ln.mark(v.tensor_copy(w[:, 1, :], pe_[:]))
                ln.mark(v.tensor_copy(wedge[:], pf[0:RAD, 0:P]))
                ln.settle()


def attend_edges(nc, g, s, wedge, keep, reset, qfirst, kvtable, sums, last):
    W = MSG + 2 * HEADS
    turns = C // BC // 2
    groups = [range(k, min(k + GC, BC)) for k in range(0, BC, GC)]
    NG = len(groups)
    ea = [s.sb(f"ea{h}", [P, BC, RAD]) for h in range(2)]
    kv = [s.sb(f"kv{h}", [P, BC, 2, MSG]) for h in range(2)]
    qd = [s.sb(f"qd{h}", [P, BC, MSG]) for h in range(2)]
    ob = [s.sb(f"ob{h}", [P, BC, W]) for h in range(2)]
    ix = [s.sb(f"ix{h}", [P, BC], U32) for h in range(2)]
    eat = [s.sb(f"eat{h}", [RAD, GC * P]) for h in range(2)]
    kc = [s.sb(f"kc{h}", [P, BC]) for h in range(2)]
    qlast = s.sb("qlast", [P, MSG])
    sc = s.sb("sc", [P, HEADS, BC])
    mb = [s.sb(f"mb{h}", [P, HEADS, BC + 1]) for h in range(2)]
    wd = [s.sb(f"wd{h}", [P, 2, HEADS, BC]) for h in range(2)]
    pt = [s.ps(f"pt{h}") for h in range(2)]
    pe_ = [s.ps(f"pe{k}") for k in range(NG)]
    scored, weighed, done, ea_used, q_used = (s.sems(x) for x in ("scored", "weighed", "done", "ea_used", "q_used"))
    ea_got, q_got, stored, scaled = (s.sems(x) for x in ("ea_got", "q_got", "stored", "scaled"))
    got = [s.gather_sem(f"got{h}") for h in range(2)]
    turned, copied, e_ready, e_read = (s.sem(x) for x in ("turned", "copied", "e_ready", "e_read"))
    dve, ixd, passed, lastd = s.sem("dve"), s.sem("ixd"), s.sem("passed"), s.sem("lastd")
    pe_passed = s.sem("pe_passed")
    rows = g.edge64.rearrange("(p c) d -> p c d", p=P)
    qrows = qfirst.rearrange("(p c) d -> p c d", p=P)
    out = sums.rearrange("(p c) w -> p c w", p=P)
    with s.block() as block:
        @block.sync
        def _(sp):
            def load(i, h):
                cols = bass.ds((i * 2 + h) * BC, BC)
                sp.wait_ge(ea_used[h], i + 1)
                sp.dma_start(ea[h][:], rows[:, cols, :]).then_inc(ea_got[h], 16)
                sp.wait_ge(q_used[h], i + 1)
                sp.dma_start(qd[h][:], qrows[:, cols, :]).then_inc(q_got[h], 16)

            def store(i, h):
                sp.wait_ge(done[h], i + 2)
                sp.dma_start(out[:, bass.ds((i * 2 + h) * BC, BC), :], ob[h][:]).then_inc(stored[h], 16)

            for h in range(2):
                sp.sem_inc(stored[h], 16)
                load(0, h)
            with sp.Fori(0, turns - 1) as i:
                for h in range(2):
                    load(i + 1, h)
                    store(i, h)
            for h in range(2):
                store(turns - 1, h)
            for h in range(2):
                sp.wait_ge(stored[h], 16 * (turns + 1))

        @block.gpsimd
        def _(pool):
            with pool.Fori(0, turns) as i:
                for h in range(2):
                    gate(pool, done[h], i + 1, passed)
                    pool.tensor_copy(ix[h][:], g.src[:, bass.ds((i * 2 + h) * BC, BC)]).then_inc(ixd, 1)
                    gate(pool, ixd, i * 2 + h + 1, passed)
                    for k in range(BC):
                        pool.indirect_dma_start(kv[h][:, k, :, :].rearrange("p a b -> p (a b)"), None, kvtable,
                                                bass.IndirectOffsetOnAxis(ap=ix[h][:, k:k + 1], axis=0)).then_inc(got[h], 16)
            for h in range(2):
                pool.wait_ge(got[h], 16 * BC * turns)

        @block.tensor
        def _(pe):
            pe.sem_inc(e_ready, 2)
            for h in range(2):
                pe.sem_inc(ea_used[h], 1)
            with pe.Fori(0, turns) as i:
                for h in range(2):
                    pe.wait_ge(ea_got[h], (i + 1) * 16)
                    for gi, cols in enumerate(groups):
                        n = h * NG + gi
                        gate(pe, copied, i * (2 * NG) + (n + 1), pe_passed)
                        for z, k in enumerate(cols):
                            ins = pe.transpose(pt[n % 2][0:RAD, z * P:(z + 1) * P], ea[h][:, k, :], g.ident[:])
                        ins.then_inc(turned, 1)
                        pe.wait_ge(copied, i * (2 * NG) + (n + 3))
                        pe.wait_ge(e_read, i * (2 * NG) + (n + 1))
                        for z, k in enumerate(cols):
                            ins = pe.matmul(pe_[gi][:, z * P:(z + 1) * P], eat[n % 2][:, z * P:(z + 1) * P], wedge[:],
                                            start=True, stop=True)
                        ins.then_inc(e_ready, 1)
                    pe.sem_inc(ea_used[h], 1)

        @block.scalar
        def _(act):
            act.sem_inc(copied, 2)
            for h in range(2):
                act.sem_inc(weighed[h], 1)

            def copy(i, h, gs):
                for gi in gs:
                    n = h * NG + gi
                    wide = len(groups[gi]) * P
                    act.wait_ge(turned, i * (2 * NG) + (n + 1))
                    act.wait_ge(e_ready, i * (2 * NG) + (n + 1))
                    act.activation(eat[n % 2][:, 0:wide], pt[n % 2][0:RAD, 0:wide], ACT.Copy).then_inc(copied, 1)

            def weigh(i, h):
                act.wait_ge(scored[h], i + 2)
                both = wd[h][:].rearrange("p a h c -> p (a h c)")
                act.activation(both, both, ACT.Exp).then_inc(weighed[h], 1)

            def scale(i, h):
                act.wait_ge(weighed[h], i + 2)
                act.wait_ge(e_read, i * (2 * NG) + (h + 2) * NG)
                for k in range(BC):
                    for a in range(VH, HEADS):
                        vv = kv[h][:, k, 1, a * OUTC:(a + 1) * OUTC]
                        ins = act.activation(vv, vv, ACT.Copy, scale=wd[h][:, 1, a, k:k + 1])
                    ins.then_inc(scaled[h], 1)

            copy(0, 0, range(NG))
            with act.Fori(0, turns - 1) as i:
                for h in range(2):
                    copy(i + h, 1 - h, range(0, 2))
                    weigh(i, h)
                    scale(i, h)
                    copy(i + h, 1 - h, range(2, NG))
            copy(turns - 1, 1, range(0, 2))
            weigh(turns - 1, 0)
            scale(turns - 1, 0)
            copy(turns - 1, 1, range(2, NG))
            weigh(turns - 1, 1)
            scale(turns - 1, 1)

        @block.vector
        def _(v):
            ln = Links(v, dve)
            v.sem_inc(e_read, NG)
            for h in range(2):
                v.sem_inc(scored[h], 1)
                v.sem_inc(done[h], 1)
                v.sem_inc(q_used[h], 1)

            def start_queries(i, h):
                v.wait_ge(q_got[h], (i + 1) * 16)
                ln.mark(v.tensor_scalar(kc[h][:], keep[:, bass.ds((i * 2 + h) * BC, BC)], 0.0, None, ALU.add))

            def carry_query(h, k):
                before = qd[h][:, k - 1, :] if k else qlast[:]
                return v.scalar_tensor_tensor(out=qd[h][:, k, :], in0=before, scalar=kc[h][:, k:k + 1],
                                              in1=qd[h][:, k, :], op0=ALU.mult, op1=ALU.add)

            def score(i, h):
                cs = bass.ds((i * 2 + h) * BC, BC)
                v.wait_ge(got[h], (i + 1) * (16 * BC))
                ln.mark(v.tensor_copy(qlast[:], qd[h][:, BC - 1, :]))
                for gi, cols in enumerate(groups):
                    n = h * NG + gi
                    nc_ = len(cols)
                    part = kv[h][:, cols[0]:cols[0] + nc_, :, :]
                    e = pe_[gi][:, 0:nc_ * P].rearrange("p (c o m) -> p c o m", o=1, m=P).to_broadcast([P, nc_, 2, P])
                    v.wait_ge(e_ready, i * (2 * NG) + (n + 3))
                    v.tensor_tensor(part, part, e, ALU.add).then_inc(e_read, 1)
                v.wait_ge(e_read, i * (2 * NG) + (h + 2) * NG)
                ln.link(v.tensor_tensor(kv[h][:, :, 0, :], qd[h][:], kv[h][:, :, 0, :], ALU.mult))
                v.sem_inc(q_used[h], 1)
                ln.mark(v.tensor_reduce(sc[:].rearrange("p h c -> p c h"),
                                        kv[h][:, :, 0, :].rearrange("p c (h d) -> p c h d", h=HEADS), AX.X, ALU.add))
                ln.link(v.tensor_copy(mb[h][:, :, 0:1], mb[1 - h][:, :, BC:BC + 1]))
                for a in range(HEADS):
                    ln.mark(v.tensor_tensor_scan(mb[h][:, a, 1:BC + 1], reset[:, cs], sc[:, a, :], mb[h][:, a, 0:1],
                                                 ALU.add, ALU.max))
                ln.settle()
                v.wait_ge(weighed[h], i + 1)
                ln.mark(v.tensor_tensor(wd[h][:, 1, :, :], sc[:], mb[h][:, :, 1:BC + 1], ALU.subtract))
                ln.link(v.tensor_tensor(wd[h][:, 0, :, :], mb[h][:, :, 0:BC], mb[h][:, :, 1:BC + 1], ALU.subtract))
                v.tensor_tensor(wd[h][:, 0, :, :], wd[h][:, 0, :, :], reset[:, cs].rearrange("p (o c) -> p o c", o=1)
                                .to_broadcast([P, HEADS, BC]), ALU.add).then_inc(scored[h], 1)

            def sum_up(i, h, more):
                v.wait_ge(stored[h], (i + 1) * 16)
                ln.mark(v.tensor_copy(ob[h][:, :, MSG + HEADS:].rearrange("p c h -> p h c"), mb[h][:, :, 1:BC + 1]))
                if more:
                    start_queries(i + h, 1 - h)
                v.wait_ge(weighed[h], i + 2)
                v.wait_ge(done[1 - h], i + 1 + h)
                ln.settle()
                before = ob[1 - h][:, BC - 1, :]
                for a in range(HEADS):
                    ln.mark(v.tensor_tensor_scan(ob[h][:, :, MSG + a], wd[h][:, 0, a, :], wd[h][:, 1, a, :],
                                                 before[:, MSG + a:MSG + a + 1], ALU.mult, ALU.add))
                for a in range(VH):
                    vv = kv[h][:, :, 1, a * OUTC:(a + 1) * OUTC]
                    ln.mark(v.tensor_tensor(vv, vv, wd[h][:, 1, a, :].rearrange("p (c o) -> p c o", o=1)
                                            .to_broadcast([P, BC, OUTC]), ALU.mult))
                ln.settle()
                for k in range(BC):
                    decay = wd[h][:, 0, :, k:k + 1].to_broadcast([P, HEADS, OUTC])
                    to = ob[h][:, k, 0:MSG]
                    ln.mark(v.tensor_tensor(to.rearrange("p (h d) -> p h d", h=HEADS),
                                            before[:, 0:MSG].rearrange("p (h d) -> p h d", h=HEADS), decay, ALU.mult))
                    decayed = ln.n
                    if more:
                        ln.mark(carry_query(1 - h, k))
                    ln.settle(decayed)
                    v.wait_ge(scaled[h], i * BC + (k + 1))
                    ins = v.tensor_tensor(to, to, kv[h][:, k, 1, :], ALU.add)
                    before = ob[h][:, k, :]
                    if k < BC - 1:
                        ln.link(ins)
                    else:
                        ins.then_inc(done[h], 1)
                ln.settle()

            ln.mark(v.memset(mb[1][:], 0.0))
            ln.mark(v.memset(qlast[:], 0.0))
            ln.mark(v.memset(ob[1][:, BC - 1, :], 0.0))
            start_queries(0, 0)
            ln.settle()
            for k in range(BC):
                ln.link(carry_query(0, k))
            with v.Fori(0, turns - 1) as i:
                ln.enter(i, 2 * (8 + 2 * HEADS + VH + 3 * BC - 1))
                for h in range(2):
                    score(i, h)
                    sum_up(i, h, True)
                ln.leave(turns - 1)
            for h in range(2):
                score(turns - 1, h)
                sum_up(turns - 1, h, h == 0)
            v.wait_ge(done[1], turns + 1)
            v.tensor_copy(last[:], ob[1][:, BC - 1, :]).then_inc(lastd, 1)
            v.wait_ge(lastd, 1)


def l1_gnn(nc, g):
    W = MSG + 2 * HEADS
    scale = float(1.0 / np.sqrt(np.float32(OUTC)))
    qtable = nc.dram_tensor("qtable", (NP, MSG), F32, kind="Internal").ap()
    kvtable = nc.dram_tensor("kvtable", (NP, 2 * MSG), F32, kind="Internal").ap()
    sums = nc.dram_tensor("msg_sums", (P * C, W), F32, kind="Internal").ap()
    with Stage(nc, "g1") as s:
        last = s.sb("last", [P, W])
        wback = s.sb("wback", [P, 1, D])
        wedge = s.sb("wedge", [RAD, P])
        wout = s.sb("wout", [P, MSG])
        wskip = s.sb("wskip", [P, MSG])
        xr = s.sb("xr", [P, NB, MSG])
        with Stage(nc, "g1p") as s1:
            w = s1.sb("w", [P, 2, 4 * MSG])
            bias = s1.sb("bias", [P, 4 * MSG])
            message_weights(nc, g, w, bias, wedge, wback, wout, wskip)

            q = s1.sb("q", [P, NB, MSG])

            def rows4(v, ln, h, b, rows, xn, po, out):
                ln.mark(v.tensor_tensor(flat(xr, MSG)[:, bass.ds(b * MSG, MSG)], po[:, 3 * MSG:], bias[:, 3 * MSG:], ALU.add))
                ln.link(v.tensor_tensor(out[:], po[:, 0:3 * MSG], bias[:, 0:3 * MSG], ALU.add))
                ln.mark(v.tensor_scalar(flat(q, MSG)[:, bass.ds(b * MSG, MSG)], out[:, 0:MSG], scale, None, ALU.mult))
                return v.tensor_scalar(out[:, 0:MSG], out[:, 0:MSG], scale, None, ALU.mult)

            spread = Spread(nc, g, "qs", MSG, g.dstf, C, g.start, g.end, g.qfirst, zeroed=True)
            with spread.s:
                project(nc, g, "qkv", w, 4 * MSG, 3 * MSG, rows4, 3, [(qtable, 0, MSG), (kvtable, MSG, 3 * MSG)],
                        beside=lambda pool, finished: spread.scatter(pool, finished, q))
                spread.lanes(qtable)
        with Stage(nc, "g1e") as s1:
            keep = s1.sb("keep", [P, C])
            reset = s1.sb("reset", [P, C])
            boundaries(nc, g, "bnd1", g.dstf, C, reset, keep)
            attend_edges(nc, g, s1, wedge, keep, reset, g.qfirst, kvtable, sums, last)
        carry_in(nc, g, "car1", g.dstf, C, last, MSG, HEADS, sums)
        rows = s.sb("rows", [P, NB, W])
        with Stage(nc, "g1f") as s1:
            ends = Ends(nc, s1, g.end, sums, rows)
            tmp = s1.sb("tmp", [P, NB, MSG])
            some, skip, beta = (s1.sb(n, [P, NB]) for n in ("some", "skip", "beta"))
            r = s1.sb("r", [P, PU, HEADS])
            logit = s1.sb("logit", [P, PU])
            one_less = s1.sb("one_less", [P, PU])
            dv, logits, exped = s1.sem("bdv"), s1.sem("logits"), s1.sem("exped")

            def part(t, i, w):
                return flat(t, w)[:, bass.ds(i * (PU * w), PU * w)].rearrange("p (b w) -> p b w", w=w)

            def wide(t, n):
                return t.rearrange("p (b o) -> p b o", o=1).to_broadcast([P, n, MSG])

            def tall(t, n):
                return t[:].rearrange("p (o m) -> p o m", o=1).to_broadcast([P, n, MSG])

            with s1.block() as block:
                @block.gpsimd
                def _(pool):
                    ends.gather(pool)

                @block.vector
                def _(v):
                    ln = Links(v, dv)
                    ln.mark(v.tensor_tensor(some[:], g.end[:], g.start[:], ALU.is_gt))
                    ln.link(v.tensor_tensor(tmp[:], xr[:], tall(wskip, NB), ALU.mult))
                    ln.link(v.tensor_reduce(skip[:], tmp[:], AX.X, ALU.add))
                    for i in range(NB // PU):
                        for u in range(PU):
                            ends.ready(v, i, u)
                        row, x_r, t = part(rows, i, W), part(xr, i, MSG), part(tmp, i, MSG)
                        o = row[:, :, 0:MSG]
                        now = bass.ds(i * PU, PU)
                        b = beta[:, now]
                        ln.link(v.tensor_scalar(r[:], row[:, :, MSG:MSG + HEADS], 1e-16, None, ALU.add))
                        ln.link(v.reciprocal(r[:], r[:]))
                        ln.link(v.tensor_tensor(r[:], r[:], some[:, now].rearrange("p (b o) -> p b o", o=1)
                                                .to_broadcast([P, PU, HEADS]), ALU.mult))
                        oh = o.rearrange("p b (h d) -> p b h d", h=HEADS)
                        ln.link(v.tensor_tensor(oh, oh, r[:].rearrange("p b (h o) -> p b h o", o=1)
                                                .to_broadcast([P, PU, HEADS, OUTC]), ALU.mult))
                        ln.link(v.tensor_tensor(t, o, tall(wout, PU), ALU.mult))
                        ln.link(v.tensor_reduce(logit[:], t, AX.X, ALU.add))
                        v.tensor_tensor(b, logit[:], skip[:, now], ALU.add).then_inc(logits, 1)
                        v.wait_ge(exped, i + 1)
                        ln.link(v.tensor_scalar(b, b, 1.0, None, ALU.add))
                        ln.link(v.reciprocal(b, b))
                        ln.link(v.tensor_scalar(one_less[:], b, -1.0, 1.0, ALU.mult, ALU.add))
                        ln.mark(v.tensor_tensor(x_r, x_r, wide(b, PU), ALU.mult))
                        ln.link(v.tensor_tensor(o, o, wide(one_less[:], PU), ALU.mult))
                        ln.link(v.tensor_tensor(x_r, x_r, o, ALU.add))

                @block.scalar
                def _(act):
                    for i in range(NB // PU):
                        act.wait_ge(logits, i + 1)
                        b = beta[:, bass.ds(i * PU, PU)]
                        act.activation(b, b, ACT.Exp, scale=-1.0).then_inc(exped, 1)

        def mixed(v, b, to):
            return v.tensor_scalar(to[:, 0:MSG], flat(xr, MSG)[:, bass.ds(b * MSG, MSG)], 0.0, None, ALU.add)

        def add(v, ln, h, b, rows_x, xn, po, out):
            return v.tensor_tensor(rows_x, rows_x, po[:, 0:D], ALU.add)

        project(nc, g, "back", wback, D, 0, add, 0, prepare=mixed, depth=1)


EXPERTS = 4
GH = 4
BC2 = 32


def finish_sort(nc, g, dstf, src):
    with Stage(nc, "so") as s:
        sort = EdgeSort(nc, g, s, resume=True)
        ends = s.sb("ends", [P, 2, C2], I32)
        dve = s.sem("dve")
        with s.block() as block:
            @block.sync
            def _(sp):
                sort.load(sp)

            @block.gpsimd
            def _(pool):
                sort.number_lanes(pool)

            @block.vector
            def _(v):
                sort.start(v)
                for _ in sort.stages(v, sort.ACROSS):
                    pass
                ln = Links(v, dve)
                keys = sort.buf[sort.at][:].bitcast(I32)
                ln.mark(v.tensor_scalar(ends[:, 0, :], keys, 2 ** ID_BITS - 1, None, ALU.bitwise_and))
                ln.mark(v.tensor_scalar(ends[:, 1, :], keys, ID_BITS, 2 ** ID_BITS - 1,
                                        ALU.logical_shift_right, ALU.bitwise_and))
                ln.settle()
                ln.mark(v.tensor_copy(src[:], ends[:, 0, :]))
                ln.mark(v.tensor_copy(dstf[:], ends[:, 1, :]))
                ln.settle()

            @block.tensor
            def _(pe):
                sort.transpose(pe)


def route_and_hide(nc, g, s, table, adst, reset, src, sums, last, w1, b1, w2, b2, loaded, outputs):
    F = GH * EXPERTS
    W, T = F + 2 * GH, F + GH
    steps = C2 // BC2
    turns = NB // SUPER
    assert steps == 2 + 3 * turns
    width = SUPER * P
    hw = width // 2
    uses = 2 * HC
    HU, YU = uses * EXPERTS, SUPER * EXPERTS
    ge = [s.sb(f"ge{k}", [P, BC2, T]) for k in range(3)]
    ob = [s.sb(f"ob{k}", [P, BC2, W]) for k in range(3)]
    ix = [s.sb(f"ix{k}", [P, BC2], U32) for k in range(3)]
    mb = [s.sb(f"mb{k}", [P, GH, BC2 + 1]) for k in range(3)]
    sc = s.sb("sc", [P, GH, BC2])
    lk = s.sb("lk", [P, GH, BC2])
    wd = s.sb("wd", [P, 2, GH, BC2])
    xn = s.sb("xn", [P, SUPER, D])
    xt = s.sb("xt", [P, 2, width])
    ht = [s.sb(f"ht{k}", [P, HC, width]) for k in range(2)]
    yb = [s.sb(f"yb{k}", [P, SUPER, D]) for k in range(2)]
    pt = [s.ps(f"pt{k}") for k in range(2)]
    ph = [s.ps(f"ph{k}") for k in range(4)]
    py = [s.ps(f"py{k}") for k in range(2)]
    scored, weighed, done, ixd, passed, lastd = (s.sem(x) for x in ("scored", "weighed", "done", "ixd", "passed", "lastd"))
    got, stored = [s.gather_sem(f"got{k}") for k in range(3)], s.sems("stored", 3)
    normed, turned, copied, hidden, acted, out_ready, out_read, dve = (s.sem(x) for x in (
        "normed", "turned", "copied", "hidden", "acted", "out_ready", "out_read", "dve"))
    y_stored = s.sems("y_stored")
    out = sums.rearrange("(p c) w -> p c w", p=P)
    with s.block() as block:
        @block.gpsimd
        def _(pool):
            def gather(i, t0):
                t, k = i * 3 + t0, t0
                gate(pool, done, t + 1, passed)
                pool.tensor_copy(ix[k][:], src[:, bass.ds(t * BC2, BC2)]).then_inc(ixd, 1)
                gate(pool, ixd, t + 1, passed)
                for c in range(BC2):
                    pool.indirect_dma_start(ge[k][:, c, :], None, table,
                                            bass.IndirectOffsetOnAxis(ap=ix[k][:, c:c + 1], axis=0)).then_inc(got[k], 16)

            with pool.Fori(0, turns) as i:
                for t0 in range(3):
                    gather(i, t0)
            gather(turns, 0)
            gather(turns, 1)
            for k in range(3):
                pool.wait_ge(got[k], 16 * BC2 * ((steps - k + 2) // 3))

        @block.sync
        def _(sp):
            def store(i, t0):
                t, k = i * 3 + t0, t0
                sp.wait_ge(done, t + 4)
                sp.dma_start(out[:, bass.ds(t * BC2, BC2), :], ob[k][:]).then_inc(stored[k], 16)

            def store_outputs(i, q):
                sp.wait_ge(out_read, i * YU + ((q + 1) * SUPER + 2))
                sp.dma_start(outputs[bass.ds((i * EXPERTS + q) * P, P), :], flat(yb[q % 2], D)).then_inc(y_stored[q % 2], 16)

            for k in range(3):
                sp.sem_inc(stored[k], 16)
            for z in range(2):
                sp.sem_inc(y_stored[z], 16)
            with sp.Fori(0, turns) as i:
                for q in range(EXPERTS):
                    store_outputs(i, q)
                    if q < 3:
                        store(i, q)
            store(turns, 0)
            store(turns, 1)
            for k in range(3):
                sp.wait_ge(stored[k], 16 * ((steps - k + 2) // 3 + 1))
            for z in range(2):
                sp.wait_ge(y_stored[z], 16 * (2 * turns + 1))

        @block.vector
        def _(v):
            ln = Links(v, dve)
            v.sem_inc(out_read, 2)
            v.sem_inc(done, 3)

            def norm(i):
                for j in range(SUPER):
                    b = i * SUPER + j
                    rows = flat(g.x, D)[:, bass.ds(b * D, D)]
                    ins = v.tensor_scalar(xn[:, j, :], rows, g.mean[:, bass.ds(b, 1)], g.rstd[:, bass.ds(b, 1)],
                                          ALU.subtract, ALU.mult)
                ins.then_inc(normed, 1)

            def add_bias(i, q):
                v.wait_ge(y_stored[q % 2], (i * 2 + (q // 2 + 1)) * 16)
                for j in range(SUPER):
                    n = q * SUPER + j
                    v.wait_ge(out_ready, i * YU + (10 + n + 1))
                    v.tensor_tensor(yb[q % 2][:, j, :], py[n % 2][:, 0:D], b2[:, q, :], ALU.add).then_inc(out_read, 1)

            def step(i, t0):
                t, k = i * 3 + t0, t0
                last_k = (t0 + 2) % 3
                cs = bass.ds(t * BC2, BC2)
                v.wait_ge(got[k], (i + 1) * (16 * BC2))
                ln.link(v.tensor_tensor(sc[:].rearrange("p h c -> p c h"), ge[k][:, :, F:T], adst[:, cs, :], ALU.add))
                ln.mark(v.tensor_copy(mb[k][:, :, 0:1], mb[last_k][:, :, BC2:BC2 + 1]))
                ln.link(v.scalar_tensor_tensor(out=lk[:], in0=sc[:], scalar=0.2, in1=sc[:], op0=ALU.mult, op1=ALU.max))
                for a in range(GH):
                    ln.mark(v.tensor_tensor_scan(mb[k][:, a, 1:BC2 + 1], reset[:, cs], lk[:, a, :], mb[k][:, a, 0:1],
                                                 ALU.add, ALU.max))
                ln.settle()
                ln.mark(v.tensor_tensor(wd[:, 1, :, :], lk[:], mb[k][:, :, 1:BC2 + 1], ALU.subtract))
                ln.link(v.tensor_tensor(wd[:, 0, :, :], mb[k][:, :, 0:BC2], mb[k][:, :, 1:BC2 + 1], ALU.subtract))
                v.tensor_tensor(wd[:, 0, :, :], wd[:, 0, :, :], reset[:, cs].rearrange("p (o c) -> p o c", o=1)
                                .to_broadcast([P, GH, BC2]), ALU.add).then_inc(scored, 1)
                v.wait_ge(stored[k], (i + 1) * 16)
                ln.mark(v.tensor_copy(ob[k][:, :, F + GH:].rearrange("p c h -> p h c"), mb[k][:, :, 1:BC2 + 1]))
                v.wait_ge(weighed, t + 1)
                v.wait_ge(done, t + 3)
                ln.settle()
                before = ob[last_k][:, BC2 - 1, :]
                for a in range(GH):
                    ln.mark(v.tensor_tensor_scan(ob[k][:, :, F + a], wd[:, 0, a, :], wd[:, 1, a, :],
                                                 before[:, F + a:F + a + 1], ALU.mult, ALU.add))
                for a in range(GH):
                    vv = ge[k][:, :, a * EXPERTS:(a + 1) * EXPERTS]
                    ln.mark(v.tensor_tensor(vv, vv, wd[:, 1, a, :].rearrange("p (c o) -> p c o", o=1)
                                            .to_broadcast([P, BC2, EXPERTS]), ALU.mult))
                ln.settle()
                for f in range(F):
                    ins = v.tensor_tensor_scan(ob[k][:, :, f], wd[:, 0, f // EXPERTS, :], ge[k][:, :, f],
                                               before[:, f:f + 1], ALU.mult, ALU.add)
                ins.then_inc(done, 1)

            def turn(i, more):
                if more:
                    v.wait_ge(turned, i * SUPER + SUPER)
                    norm(i + 1)
                for q in range(EXPERTS):
                    add_bias(i, q)
                    if q < 3:
                        step(i, q)

            ln.mark(v.memset(mb[2][:], 0.0))
            ln.link(v.memset(ob[2][:, BC2 - 1, :], 0.0))
            norm(0)
            with v.Fori(0, turns - 1) as i:
                ln.enter(i, 3 * (6 + 3 * GH))
                turn(i, True)
                ln.leave(turns - 1)
            turn(turns - 1, False)
            step(turns, 0)
            step(turns, 1)
            v.wait_ge(done, steps + 3)
            v.tensor_copy(last[:], ob[(steps - 1) % 3][:, BC2 - 1, :]).then_inc(lastd, 1)
            v.wait_ge(lastd, 1)

        @block.tensor
        def _(pe):
            pe.sem_inc(out_ready, 10)
            pe.wait_ge(loaded, 16 * (3 * EXPERTS + 1))

            def turn(i, first=False):
                pe.wait_ge(normed, i + 1)
                for j in range(SUPER):
                    if j >= 2:
                        pe.wait_ge(copied, i * SUPER + (j - 1))
                    elif not first:
                        pe.wait_ge(copied, i * SUPER)
                    pe.transpose(pt[j % 2][:, 0:P], xn[:, j, 0:P], g.ident[:])
                    pe.transpose(pt[j % 2][:, P:D], xn[:, j, P:D], g.ident[:]).then_inc(turned, 1)

            def hide(i, q):
                if q == 0:
                    pe.wait_ge(copied, i * SUPER + SUPER)
                for c in range(HC):
                    for z in range(2):
                        u = q * uses + 2 * c + z
                        ch = q * HC + c
                        pe.wait_ge(acted, i * HU + (u + 1))
                        for k in range(2):
                            ins = pe.matmul(ph[u % 4][:, 0:hw], w1[:, k, ch * P:(ch + 1) * P],
                                            xt[:, k, z * hw:(z + 1) * hw], start=(k == 0), stop=(k == 1))
                        ins.then_inc(hidden, 1)

            def down(i, q):
                pe.wait_ge(acted, i * HU + ((q + 1) * uses + 4))
                for j in range(SUPER):
                    n = q * SUPER + j
                    pe.wait_ge(out_read, i * YU + (n + 1))
                    for c in range(HC):
                        ins = pe.matmul(py[n % 2][:, 0:D], ht[q % 2][:, c, j * P:(j + 1) * P], w2[:, q * HC + c, :],
                                        start=(c == 0), stop=(c == HC - 1))
                    ins.then_inc(out_ready, 1)

            def body(i, more):
                for q in range(EXPERTS):
                    hide(i, q)
                    if q:
                        down(i, q - 1)
                if more:
                    turn(i + 1)
                down(i, EXPERTS - 1)

            turn(0, True)
            with pe.Fori(0, turns - 1) as i:
                body(i, True)
            body(turns - 1, False)

        @block.scalar
        def _(act):
            act.sem_inc(acted, 4)

            def copy(i):
                for j in range(SUPER):
                    act.wait_ge(turned, i * SUPER + (j + 1))
                    act.activation(xt[:, :, j * P:(j + 1) * P], pt[j % 2][:, 0:D].rearrange("p (k n) -> p k n", k=2),
                                   ACT.Copy).then_inc(copied, 1)

            def hide(i, q):
                act.wait_ge(out_ready, i * YU + (q * SUPER + 5))
                for c in range(HC):
                    for z in range(2):
                        u = q * uses + 2 * c + z
                        act.wait_ge(hidden, i * HU + (u + 1))
                        act.activation(ht[q % 2][:, c, z * hw:(z + 1) * hw], ph[u % 4][:, 0:hw], ACT.Gelu,
                                       bias=b1[:, q * HC + c:q * HC + c + 1]).then_inc(acted, 1)

            def weigh(i, t0):
                act.wait_ge(scored, i * 3 + (t0 + 1))
                both = wd[:].rearrange("p a h c -> p (a h c)")
                act.activation(both, both, ACT.Exp).then_inc(weighed, 1)

            def turn(i):
                for q in range(EXPERTS):
                    hide(i, q)
                    if q:
                        weigh(i, q - 1)

            copy(0)
            with act.Fori(0, turns - 1) as i:
                turn(i)
                copy(i + 1)
            turn(turns - 1)
            weigh(turns, 0)
            weigh(turns, 1)


class Combine:

    def __init__(self, nc, g, s, outputs):
        self.nc, self.g, self.s, self.outputs = nc, g, s, outputs
        self.y = [s.sb(f"y{h}", [P, EXPERTS, SUPER * D]) for h in range(2)]
        self.loaded, self.used, self.stored, self.dve = s.sems("cloaded"), s.sems("cused"), s.sem("cstored"), s.sem("cdve")

    def load(self, sp, i, h):
        sp.dma_start(self.y[h][:], self.outputs[bass.ds((i * 2 + h) * (EXPERTS * P), EXPERTS * P), :]
                     .rearrange("(q p) w -> p q w", p=P)).then_inc(self.loaded[h], 16)

    def start(self, sp):
        for h in range(2):
            self.load(sp, 0, h)

    def run(self, gates):
        g, y, loaded, used, dve = self.g, self.y, self.loaded, self.used, self.dve
        pairs = NB // SUPER // 2
        rows = SUPER * P
        with self.s.block() as block:
            @block.sync
            def _(sp):
                with sp.Fori(0, pairs - 1) as i:
                    for h in range(2):
                        sp.wait_ge(used[h], i + 1)
                        self.load(sp, i + 1, h)
                        sp.dma_start(g.out[bass.ds((i * 2 + h) * rows, rows), :].rearrange("(b p) d -> p b d", p=P),
                                     flat(g.x, D)[:, bass.ds((i * 2 + h) * (SUPER * D), SUPER * D)]
                                     .rearrange("p (b d) -> p b d", d=D)).then_inc(self.stored, 16)
                first = (pairs * 2 - 2) * SUPER
                full = N // P
                sp.wait_ge(used[0], pairs)
                sp.wait_ge(used[1], pairs)
                sp.dma_start(g.out[first * P:full * P, :].rearrange("(b p) d -> p b d", p=P),
                             g.x[:, first:full, :]).then_inc(self.stored, 16)
                sp.dma_start(g.out[full * P:N, :], g.x[0:N - full * P, full, :]).then_inc(self.stored, 16)
                sp.wait_ge(self.stored, 16 * (pairs * 2 - 2 + 2))

            @block.vector
            def _(v):
                ln = Links(v, dve)
                with v.Fori(0, pairs) as i:
                    ln.enter(i, 2 * EXPERTS * SUPER)
                    for h in range(2):
                        v.wait_ge(loaded[h], (i + 1) * 16)
                        for q in range(EXPERTS):
                            for j in range(SUPER):
                                b = (i * 2 + h) * SUPER + j
                                x = flat(g.x, D)[:, bass.ds(b * D, D)]
                                ln.mark(v.scalar_tensor_tensor(out=x, in0=y[h][:, q, j * D:(j + 1) * D],
                                                               scalar=gates[:, bass.ds(b * EXPERTS + q, 1)], in1=x,
                                                               op0=ALU.mult, op1=ALU.add))
                            ln.settle()
                        v.sem_inc(used[h], 1)
                    ln.leave(pairs)


def routing_weights(nc, g, w):
    F = GH * EXPERTS
    with Stage(nc, "rw") as s:
        att = s.sb("att", [P, 2, F])
        tmp = s.sb("tmp", [P, 2, 2, F])
        got, dve = s.sem("got"), s.sem("dve")
        with s.block() as block:
            @block.sync
            def _(sp):
                sp.dma_start(w[:, :, 0:F], g.ins["L1_ffn_W_gat"].rearrange("(k p) n -> p k n", p=P)).then_inc(got, 16)
                for z, n in enumerate(("att_src", "att_dst")):
                    sp.dma_start(att[:, z, :], g.ins["L1_ffn_" + n].rearrange("h e -> (h e)").partition_broadcast(P)).then_inc(got, 16)
                sp.wait_ge(got, 48)

            @block.vector
            def _(v):
                ln = Links(v, dve)
                v.wait_ge(got, 48)
                for k in range(2):
                    for z in range(2):
                        ln.mark(v.tensor_tensor(tmp[:, k, z, :], w[:, k, 0:F], att[:, z, :], ALU.mult))
                ln.settle()
                for k in range(2):
                    ln.mark(v.tensor_reduce(w[:, k, F:F + 2 * GH].rearrange("p (z h) -> p z h", z=2),
                                            tmp[:, k, :, :].rearrange("p z (h e) -> p z h e", h=GH), AX.X, ALU.add))
                ln.settle()


def expert_gates(nc, g, s, rows, gates):
    F = GH * EXPERTS
    W = F + 2 * GH
    par = s.sb("par", [P, 3, F])
    c = s.sb("c", [P, NB, F])
    sq = s.sb("sq", [P, NB, F])
    m = s.sb("m", [P, NB])
    r = s.sb("r", [P, NB])
    sc = s.sb("sc", [P, NB, EXPERTS])
    better = s.sb("better", [P, NB, EXPERTS])
    cmp_ = s.sb("cmp", [P, NB])
    got, rooted, exped, std, ex, dve = (s.sem(x) for x in ("egot", "rooted", "exped", "estd", "eex", "edve"))

    def wide(t, n):
        return t.rearrange("p (b o) -> p b o", o=1).to_broadcast([P, NB, n])

    def tall(t):
        return t.rearrange("p (o m) -> p o m", o=1).to_broadcast([P, NB, F])

    with s.block() as block:
        @block.sync
        def _(sp):
            for z, n in enumerate(("b_gat", "ln_gamma", "ln_beta")):
                sp.dma_start(par[:, z, :], g.ins["L1_ffn_" + n].partition_broadcast(P)).then_inc(got, 16)
            sp.wait_ge(got, 48)

        @block.vector
        def _(v):
            ln = Links(v, dve)
            v.wait_ge(got, 48)
            ln.link(v.tensor_tensor(c[:], rows[:, :, 0:F], tall(par[:, 0, :]), ALU.add))
            ln.link(v.tensor_reduce(m[:], c[:], AX.X, ALU.add))
            ln.link(v.tensor_scalar(m[:], m[:], 1.0 / F, None, ALU.mult))
            ln.link(v.tensor_tensor(c[:], c[:], wide(m[:], F), ALU.subtract))
            ln.link(v.tensor_tensor(sq[:], c[:], c[:], ALU.mult))
            ln.link(v.tensor_reduce(r[:], sq[:], AX.X, ALU.add))
            v.tensor_scalar(r[:], r[:], 1.0 / F, EPS, ALU.mult, ALU.add).then_inc(std, 1)
            v.wait_ge(rooted, 1)
            ln.link(v.reciprocal(r[:], r[:]))
            ln.link(v.tensor_tensor(c[:], c[:], wide(r[:], F), ALU.mult))
            ln.link(v.tensor_tensor(c[:], c[:], tall(par[:, 1, :]), ALU.mult))
            ln.link(v.tensor_tensor(c[:], c[:], tall(par[:, 2, :]), ALU.add))
            ln.link(v.tensor_reduce(sc[:], c[:].rearrange("p b (h e) -> p b e h", h=GH), AX.X, ALU.add))
            ln.mark(v.tensor_scalar(sc[:], sc[:], 1.0 / GH, None, ALU.mult))
            ln.mark(v.memset(better[:], 0.0))
            ln.settle()
            for e in range(EXPERTS):
                for f in range(EXPERTS):
                    if f != e:
                        ln.link(v.tensor_tensor(cmp_[:], sc[:, :, f], sc[:, :, e], ALU.is_ge if f < e else ALU.is_gt))
                        ln.link(v.tensor_tensor(better[:, :, e], better[:, :, e], cmp_[:], ALU.add))
            ln.mark(v.tensor_scalar(better[:], better[:], 1.5, None, ALU.is_lt))
            ln.link(v.tensor_reduce(m[:], sc[:], AX.X, ALU.max))
            v.tensor_tensor(sc[:], sc[:], wide(m[:], EXPERTS), ALU.subtract).then_inc(ex, 1)
            v.wait_ge(exped, 1)
            ln.link(v.tensor_tensor(sc[:], sc[:], better[:], ALU.mult))
            ln.link(v.tensor_reduce(m[:], sc[:], AX.X, ALU.add))
            ln.link(v.reciprocal(m[:], m[:]))
            ln.link(v.tensor_tensor(gates[:], sc[:], wide(m[:], EXPERTS), ALU.mult))

        @block.scalar
        def _(act):
            act.wait_ge(std, 1)
            act.activation(r[:], r[:], ACT.Sqrt).then_inc(rooted, 1)
            act.wait_ge(ex, 1)
            act.activation(sc[:], sc[:], ACT.Exp).then_inc(exped, 1)


def l1_ffn(nc, g):
    F = GH * EXPERTS
    W, T = F + 2 * GH, F + GH
    table = nc.dram_tensor("rtable", (NP, T), F32, kind="Internal").ap()
    sums = nc.dram_tensor("route_sums", (E2, W), F32, kind="Internal").ap()
    outputs = nc.dram_tensor("expert_outputs", (NB // SUPER * EXPERTS * P, SUPER * D), F32, kind="Internal").ap()
    ad = nc.dram_tensor("ad_table", (NP, GH), F32, kind="Internal").ap()
    firsts = nc.dram_tensor("ad_firsts", (E2, GH), F32, kind="Internal").ap()
    keys = nc.dram_tensor("keys2", (E2,), F32, kind="Internal").ap()
    with Stage(nc, "x1") as s:
        gates = s.sb("gates", [P, NB, EXPERTS])
        with Stage(nc, "x1r") as sr:
            start, end = sr.sb("start", [P, NB]), sr.sb("end", [P, NB])
            own = sr.sb("own", [P, NB, W])
            last = sr.sb("last", [P, W])
            H = 2 * D
            w1 = sr.sb("w1", [P, 2, EXPERTS * H])
            w2 = sr.sb("w2", [P, EXPERTS * H // P, D])
            b1 = sr.sb("b1", [P, EXPERTS * H // P])
            b2 = sr.sb("b2", [P, EXPERTS, D])
            loaded = sr.sem("loaded")
            with Stage(nc, "x1e") as s1:
                dstf = s1.sb("dstf", [P, C2])
                src = s1.sb("src", [P, C2], U32)
                keep = s1.sb("keep", [P, C2])
                reset = s1.sb("reset", [P, C2])
                adst = s1.sb("adst", [P, C2, GH])
                adn = s1.sb("adn", [P, NB, GH])
                w = s1.sb("w", [P, 2, W])
                dv = s1.sem("dv")
                finish_sort(nc, g, dstf, src)
                routing_weights(nc, g, w)

                def route_rows(v, ln, h, b, rows, xn, po, out):
                    ln.mark(v.tensor_scalar(flat(own, W)[:, bass.ds(b * W, W)], po[:, 0:W], 0.0, None, ALU.add))
                    ln.mark(v.tensor_scalar(flat(adn, GH)[:, bass.ds(b * GH, GH)], po[:, T:W], 0.0, None, ALU.add))
                    return v.tensor_copy(out[:], po[:, 0:T])

                segments(nc, g, "seg2", dstf, C2, E2, start, end, keys)
                boundaries(nc, g, "bnd2", dstf, C2, reset, keep)
                spread = Spread(nc, g, "ad", GH, dstf, C2, start, end, firsts)
                with spread.s:
                    with sr.block() as block:
                        @block.scalar
                        def _(act):
                            for e in range(EXPERTS):
                                act.dma_start(w1[:, :, e * H:(e + 1) * H], g.ins["L1_ffn_W1"][e].rearrange("(k p) n -> p k n", p=P)).then_inc(loaded, 16)
                                act.dma_start(w2[:, e * HC:(e + 1) * HC, :], g.ins["L1_ffn_W2"][e].rearrange("(k p) n -> p k n", p=P)).then_inc(loaded, 16)
                                act.dma_start(b2[:, e, :], g.ins["L1_ffn_b2"][e].partition_broadcast(P)).then_inc(loaded, 16)
                            with nc.allow_non_contiguous_dma("biases, one for a lane"):
                                act.dma_start(b1[:], g.ins["L1_ffn_b1"].rearrange("e (k p) -> p (e k)", p=P)).then_inc(loaded, 16)
                    project(nc, g, "rt1", w, W, T, route_rows, 2, [(table, 0, T)],
                            beside=lambda pool, finished: spread.scatter(pool, finished, adn))
                    spread.lanes(ad, adn[:])
                    spread.carry(keep, adst[:])
                with Stage(nc, "x1l") as s2:
                    route_and_hide(nc, g, s2, table, adst, reset, src, sums, last, w1, b1, w2, b2, loaded, outputs)
                carry_in(nc, g, "car2", dstf, C2, last, F, GH, sums)
                with s1.block() as block:
                    @block.vector
                    def _(v):
                        ln = Links(v, dv)
                        m = own[:, :, F + GH:]
                        ln.link(v.tensor_tensor(m, m, own[:, :, F:F + GH], ALU.add))
                        ln.link(v.scalar_tensor_tensor(out=m, in0=m, scalar=0.2, in1=m, op0=ALU.mult, op1=ALU.max))
                        ln.link(v.memset(own[:, :, F:F + GH], 1.0))
            rows = sr.sb("rows", [P, NB, W])
            with Stage(nc, "x1g") as s1:
                combine = Combine(nc, g, s1, outputs)
                with s1.block() as block:
                    @block.sync
                    def _(sp):
                        combine.start(sp)
                gather_ends(nc, s1, end, sums, rows)
                none = s1.sb("none", [P, NB])
                dv2 = s1.sem("dv2")
                with s1.block() as block:
                    @block.vector
                    def _(v):
                        ln = Links(v, dv2)
                        ln.link(v.tensor_tensor(none[:], end[:], start[:], ALU.is_le))
                        ln.link(v.tensor_scalar(none[:], none[:], -BIG, None, ALU.mult))
                        ln.link(v.tensor_tensor(rows[:, :, F + GH:], rows[:, :, F + GH:],
                                                none[:].rearrange("p (b o) -> p b o", o=1).to_broadcast([P, NB, GH]), ALU.add))
                merge(nc, g, s1, F, GH, rows, extra=own, eps=1e-16)
                expert_gates(nc, g, s1, rows, gates)
                combine.run(flat(gates, EXPERTS))


def program(nc, ins, out):
    Stage.used.clear()
    g = G()
    g.out = out
    g.in_x, g.in_src, g.in_dst, g.edge256, g.edge64 = (ins[n] for n in ("x", "src", "dst", "edge_attr_256", "edge_attr_64"))
    g.ins = ins
    g.W_self, g.W_func, g.W_att = (ins["L0_gnn_" + n] for n in ("W_self", "W_func", "W_att"))
    with Stage(nc, "g") as s:
        g.x = s.sb("x", [P, NB, D])
        g.mean, g.rstd, g.start, g.end, g.nodeid = (s.sb(n, [P, NB]) for n in ("mean", "rstd", "start", "end", "nodeid"))
        g.src = s.sb("src", [P, C], U32)
        g.dstf = s.sb("dstf", [P, C])
        g.ident, g.ones, g.below, g.chunkno = (s.sb(n, [P, P]) for n in ("ident", "ones", "below", "chunkno"))
        g.keys = nc.dram_tensor("keys", (P * C,), F32, kind="Internal").ap()
        g.qfirst = nc.dram_tensor("qfirst", (P * C, MSG), F32, kind="Internal").ap()
        g.sorted_keys = nc.dram_tensor("sorted_keys", (E2,), I32, kind="Internal").ap()
        load_nodes(nc, g)
        for stage in (l0_gnn, l0_ffn, l1_gnn, l1_ffn):
            stage(nc, g)
            recycle(nc)


def kernel(**inputs):
    import concourse.bacc as _bacc
    from concourse.bass_utils import run_bass_kernel_spmd as _run

    nc = _bacc.Bacc("TRN2", target_bir_lowering=False, num_devices=1)

    def lay_out(name, a):
        a = np.ascontiguousarray(a)
        if name == "x":
            a = np.concatenate([a, np.zeros((NP - N, D), a.dtype)])
        elif name in ("src", "dst"):
            a = np.concatenate([a, np.full(P * C - E, NP if name == "dst" else 0, a.dtype)]).reshape(P, C)
        elif name.startswith("edge_attr"):
            a = np.concatenate([a, np.zeros((P * C - E, a.shape[1]), a.dtype)])
        return a

    arrays, ins = {}, {}
    for name, a in inputs.items():
        a = lay_out(name, a)
        arrays[f"in_{name}"] = a
        ins[name] = nc.dram_tensor(f"in_{name}", a.shape, mybir.dt.from_np(a.dtype), kind="ExternalInput").ap()
    out = nc.dram_tensor("out_0", (N, D), F32, kind="ExternalOutput").ap()
    program(nc, ins, out)
    r = _run(nc, [arrays], core_ids=[0])
    return r.results[0]["out_0"]
```
